# Optimizing a Trainium2 kernel written in Bass

```python
import numpy as np
import jax
import jax.numpy as jnp

def _softmax(x, axis=-1):
    return jax.nn.softmax(x, axis=axis)

def _gelu(x):
    return jax.nn.gelu(x, approximate=True)

def _silu(x):
    return jax.nn.silu(x)

def _sigmoid(x):
    return jax.nn.sigmoid(x)

def _layernorm(x, axis=-1, eps=1e-05):
    m = jnp.mean(x, axis=axis, keepdims=True)
    v = jnp.var(x, axis=axis, keepdims=True)
    return (x - m) / jnp.sqrt(v + eps)

def _scatter_add(tgt, idx, src, axis=0):
    return tgt.at[idx].add(src)

def _segment_sum(src, seg, n):
    return jax.ops.segment_sum(src, seg, n)
kernel_name = 'mk_rec_standalone_d1_rec_r8_8062fc'

def setup_inputs(seed: int=0):
    np.random.seed(seed)
    _w = jnp.asarray

    def _rec_inputs():
        import jax
        import jax.numpy as jnp
        _rk = jax.random.key(seed)
        r_rowData = jnp.stack([jax.random.randint(jax.random.fold_in(jax.random.fold_in(_rk, 1), 0), (2048,), 22, 99967, jnp.int32), jax.random.randint(jax.random.fold_in(jax.random.fold_in(_rk, 1), 1), (2048,), 90, 99961, jnp.int32), jax.random.randint(jax.random.fold_in(jax.random.fold_in(_rk, 1), 2), (2048,), 40, 99975, jnp.int32), jax.random.randint(jax.random.fold_in(jax.random.fold_in(_rk, 1), 3), (2048,), 11, 99938, jnp.int32), jax.random.randint(jax.random.fold_in(jax.random.fold_in(_rk, 1), 4), (2048,), 22, 99987, jnp.int32), jax.random.randint(jax.random.fold_in(jax.random.fold_in(_rk, 1), 5), (2048,), 67, 99887, jnp.int32), jax.random.randint(jax.random.fold_in(jax.random.fold_in(_rk, 1), 6), (2048,), 20, 99966, jnp.int32), jax.random.randint(jax.random.fold_in(jax.random.fold_in(_rk, 1), 7), (2048,), 10, 99983, jnp.int32), jax.random.randint(jax.random.fold_in(jax.random.fold_in(_rk, 1), 8), (2048,), 1, 99903, jnp.int32), jax.random.randint(jax.random.fold_in(jax.random.fold_in(_rk, 1), 9), (2048,), 2, 99990, jnp.int32), jax.random.randint(jax.random.fold_in(jax.random.fold_in(_rk, 1), 10), (2048,), 8, 99951, jnp.int32), jax.random.randint(jax.random.fold_in(jax.random.fold_in(_rk, 1), 11), (2048,), 15, 99945, jnp.int32), jax.random.randint(jax.random.fold_in(jax.random.fold_in(_rk, 1), 12), (2048,), 3, 99970, jnp.int32), jax.random.randint(jax.random.fold_in(jax.random.fold_in(_rk, 1), 13), (2048,), 69, 99942, jnp.int32), jax.random.randint(jax.random.fold_in(jax.random.fold_in(_rk, 1), 14), (2048,), 7, 99966, jnp.int32), jax.random.randint(jax.random.fold_in(jax.random.fold_in(_rk, 1), 15), (2048,), 10, 99994, jnp.int32), jax.random.randint(jax.random.fold_in(jax.random.fold_in(_rk, 1), 16), (2048,), 51, 99965, jnp.int32), jax.random.randint(jax.random.fold_in(jax.random.fold_in(_rk, 1), 17), (2048,), 21, 99973, jnp.int32), jax.random.randint(jax.random.fold_in(jax.random.fold_in(_rk, 1), 18), (2048,), 41, 12500, jnp.int32), jax.random.randint(jax.random.fold_in(jax.random.fold_in(_rk, 1), 19), (2048,), 18, 99991, jnp.int32), jax.random.randint(jax.random.fold_in(jax.random.fold_in(_rk, 1), 20), (2048,), 134, 99723, jnp.int32), jax.random.randint(jax.random.fold_in(jax.random.fold_in(_rk, 1), 21), (2048,), 2, 99970, jnp.int32), jax.random.randint(jax.random.fold_in(jax.random.fold_in(_rk, 1), 22), (2048,), 40, 99941, jnp.int32), jax.random.randint(jax.random.fold_in(jax.random.fold_in(_rk, 1), 23), (2048,), 274, 99970, jnp.int32), jax.random.randint(jax.random.fold_in(jax.random.fold_in(_rk, 1), 24), (2048,), 8, 99933, jnp.int32), jax.random.randint(jax.random.fold_in(jax.random.fold_in(_rk, 1), 25), (2048,), 1, 12498, jnp.int32), jax.random.randint(jax.random.fold_in(jax.random.fold_in(_rk, 1), 26), (2048,), 12, 99955, jnp.int32), jax.random.randint(jax.random.fold_in(jax.random.fold_in(_rk, 1), 27), (2048,), 6, 99957, jnp.int32), jax.random.randint(jax.random.fold_in(jax.random.fold_in(_rk, 1), 28), (2048,), 46, 99969, jnp.int32), jax.random.randint(jax.random.fold_in(jax.random.fold_in(_rk, 1), 29), (2048,), 23, 99987, jnp.int32), jax.random.randint(jax.random.fold_in(jax.random.fold_in(_rk, 1), 30), (2048,), 80, 99988, jnp.int32), jax.random.randint(jax.random.fold_in(jax.random.fold_in(_rk, 1), 31), (2048,), 41, 99849, jnp.int32), jax.random.randint(jax.random.fold_in(jax.random.fold_in(_rk, 1), 32), (2048,), 15, 99974, jnp.int32), jax.random.randint(jax.random.fold_in(jax.random.fold_in(_rk, 1), 33), (2048,), 40, 99739, jnp.int32), jax.random.randint(jax.random.fold_in(jax.random.fold_in(_rk, 1), 34), (2048,), 242, 99995, jnp.int32), jax.random.randint(jax.random.fold_in(jax.random.fold_in(_rk, 1), 35), (2048,), 49, 99933, jnp.int32), jax.random.randint(jax.random.fold_in(jax.random.fold_in(_rk, 1), 36), (2048,), 35, 99948, jnp.int32), jax.random.randint(jax.random.fold_in(jax.random.fold_in(_rk, 1), 37), (2048,), 57, 99961, jnp.int32), jax.random.randint(jax.random.fold_in(jax.random.fold_in(_rk, 1), 38), (2048,), 148, 99971, jnp.int32), jax.random.randint(jax.random.fold_in(jax.random.fold_in(_rk, 1), 39), (2048,), 19, 99918, jnp.int32), jax.random.randint(jax.random.fold_in(jax.random.fold_in(_rk, 1), 40), (2048,), 24, 99892, jnp.int32), jax.random.randint(jax.random.fold_in(jax.random.fold_in(_rk, 1), 41), (2048,), 150, 99995, jnp.int32), jax.random.randint(jax.random.fold_in(jax.random.fold_in(_rk, 1), 42), (2048,), 17, 99979, jnp.int32), jax.random.randint(jax.random.fold_in(jax.random.fold_in(_rk, 1), 43), (2048,), 0, 99999, jnp.int32), jax.random.randint(jax.random.fold_in(jax.random.fold_in(_rk, 1), 44), (2048,), 1, 99914, jnp.int32), jax.random.randint(jax.random.fold_in(jax.random.fold_in(_rk, 1), 45), (2048,), 148, 99970, jnp.int32), jax.random.randint(jax.random.fold_in(jax.random.fold_in(_rk, 1), 46), (2048,), 49, 99975, jnp.int32), jax.random.randint(jax.random.fold_in(jax.random.fold_in(_rk, 1), 47), (2048,), 77, 99998, jnp.int32), jax.random.randint(jax.random.fold_in(jax.random.fold_in(_rk, 1), 48), (2048,), 85, 99999, jnp.int32), jax.random.randint(jax.random.fold_in(jax.random.fold_in(_rk, 1), 49), (2048,), 5, 99970, jnp.int32), jax.random.randint(jax.random.fold_in(jax.random.fold_in(_rk, 1), 50), (2048,), 75, 99959, jnp.int32), jax.random.randint(jax.random.fold_in(jax.random.fold_in(_rk, 1), 51), (2048,), 164, 12497, jnp.int32), jax.random.randint(jax.random.fold_in(jax.random.fold_in(_rk, 1), 52), (2048,), 182, 99926, jnp.int32), jax.random.randint(jax.random.fold_in(jax.random.fold_in(_rk, 1), 53), (2048,), 72, 99947, jnp.int32), jax.random.randint(jax.random.fold_in(jax.random.fold_in(_rk, 1), 54), (2048,), 21, 99955, jnp.int32), jax.random.randint(jax.random.fold_in(jax.random.fold_in(_rk, 1), 55), (2048,), 10, 99951, jnp.int32), jax.random.randint(jax.random.fold_in(jax.random.fold_in(_rk, 1), 56), (2048,), 49, 99963, jnp.int32), jax.random.randint(jax.random.fold_in(jax.random.fold_in(_rk, 1), 57), (2048,), 220, 12498, jnp.int32), jax.random.randint(jax.random.fold_in(jax.random.fold_in(_rk, 1), 58), (2048,), 72, 99907, jnp.int32), jax.random.randint(jax.random.fold_in(jax.random.fold_in(_rk, 1), 59), (2048,), 72, 99988, jnp.int32), jax.random.randint(jax.random.fold_in(jax.random.fold_in(_rk, 1), 60), (2048,), 87, 99867, jnp.int32), jax.random.randint(jax.random.fold_in(jax.random.fold_in(_rk, 1), 61), (2048,), 71, 99958, jnp.int32), jax.random.randint(jax.random.fold_in(jax.random.fold_in(_rk, 1), 62), (2048,), 36, 99911, jnp.int32), jax.random.randint(jax.random.fold_in(jax.random.fold_in(_rk, 1), 63), (2048,), 15, 99982, jnp.int32), jax.random.randint(jax.random.fold_in(jax.random.fold_in(_rk, 1), 64), (2048,), 82, 99988, jnp.int32), jax.random.randint(jax.random.fold_in(jax.random.fold_in(_rk, 1), 65), (2048,), 86, 99978, jnp.int32), jax.random.randint(jax.random.fold_in(jax.random.fold_in(_rk, 1), 66), (2048,), 29, 99986, jnp.int32), jax.random.randint(jax.random.fold_in(jax.random.fold_in(_rk, 1), 67), (2048,), 7, 12499, jnp.int32), jax.random.randint(jax.random.fold_in(jax.random.fold_in(_rk, 1), 68), (2048,), 39, 99961, jnp.int32), jax.random.randint(jax.random.fold_in(jax.random.fold_in(_rk, 1), 69), (2048,), 6, 99942, jnp.int32), jax.random.randint(jax.random.fold_in(jax.random.fold_in(_rk, 1), 70), (2048,), 7, 12493, jnp.int32), jax.random.randint(jax.random.fold_in(jax.random.fold_in(_rk, 1), 71), (2048,), 14, 99977, jnp.int32), jax.random.randint(jax.random.fold_in(jax.random.fold_in(_rk, 1), 72), (2048,), 51, 99951, jnp.int32), jax.random.randint(jax.random.fold_in(jax.random.fold_in(_rk, 1), 73), (2048,), 73, 99925, jnp.int32), jax.random.randint(jax.random.fold_in(jax.random.fold_in(_rk, 1), 74), (2048,), 36, 99794, jnp.int32), jax.random.randint(jax.random.fold_in(jax.random.fold_in(_rk, 1), 75), (2048,), 20, 99955, jnp.int32), jax.random.randint(jax.random.fold_in(jax.random.fold_in(_rk, 1), 76), (2048,), 3, 99905, jnp.int32), jax.random.randint(jax.random.fold_in(jax.random.fold_in(_rk, 1), 77), (2048,), 33, 99929, jnp.int32), jax.random.randint(jax.random.fold_in(jax.random.fold_in(_rk, 1), 78), (2048,), 83, 99921, jnp.int32), jax.random.randint(jax.random.fold_in(jax.random.fold_in(_rk, 1), 79), (2048,), 33, 99946, jnp.int32), jax.random.randint(jax.random.fold_in(jax.random.fold_in(_rk, 1), 80), (2048,), 5, 99983, jnp.int32), jax.random.randint(jax.random.fold_in(jax.random.fold_in(_rk, 1), 81), (2048,), 43, 99860, jnp.int32), jax.random.randint(jax.random.fold_in(jax.random.fold_in(_rk, 1), 82), (2048,), 15, 99997, jnp.int32), jax.random.randint(jax.random.fold_in(jax.random.fold_in(_rk, 1), 83), (2048,), 65, 99986, jnp.int32), jax.random.randint(jax.random.fold_in(jax.random.fold_in(_rk, 1), 84), (2048,), 47, 99983, jnp.int32), jax.random.randint(jax.random.fold_in(jax.random.fold_in(_rk, 1), 85), (2048,), 21, 99959, jnp.int32), jax.random.randint(jax.random.fold_in(jax.random.fold_in(_rk, 1), 86), (2048,), 28, 99950, jnp.int32), jax.random.randint(jax.random.fold_in(jax.random.fold_in(_rk, 1), 87), (2048,), 23, 99971, jnp.int32), jax.random.randint(jax.random.fold_in(jax.random.fold_in(_rk, 1), 88), (2048,), 1, 99964, jnp.int32), jax.random.randint(jax.random.fold_in(jax.random.fold_in(_rk, 1), 89), (2048,), 42, 99993, jnp.int32), jax.random.randint(jax.random.fold_in(jax.random.fold_in(_rk, 1), 90), (2048,), 20, 12497, jnp.int32), jax.random.randint(jax.random.fold_in(jax.random.fold_in(_rk, 1), 91), (2048,), 56, 99987, jnp.int32), jax.random.randint(jax.random.fold_in(jax.random.fold_in(_rk, 1), 92), (2048,), 11, 99892, jnp.int32), jax.random.randint(jax.random.fold_in(jax.random.fold_in(_rk, 1), 93), (2048,), 35, 99994, jnp.int32), jax.random.randint(jax.random.fold_in(jax.random.fold_in(_rk, 1), 94), (2048,), 100, 99965, jnp.int32), jax.random.randint(jax.random.fold_in(jax.random.fold_in(_rk, 1), 95), (2048,), 128, 99846, jnp.int32), jax.random.randint(jax.random.fold_in(jax.random.fold_in(_rk, 1), 96), (2048,), 92, 99926, jnp.int32), jax.random.randint(jax.random.fold_in(jax.random.fold_in(_rk, 1), 97), (2048,), 4, 99927, jnp.int32), jax.random.randint(jax.random.fold_in(jax.random.fold_in(_rk, 1), 98), (2048,), 4, 99975, jnp.int32), jax.random.randint(jax.random.fold_in(jax.random.fold_in(_rk, 1), 99), (2048,), 0, 99954, jnp.int32), jax.random.randint(jax.random.fold_in(jax.random.fold_in(_rk, 1), 100), (2048,), 73, 99997, jnp.int32), jax.random.randint(jax.random.fold_in(jax.random.fold_in(_rk, 1), 101), (2048,), 18, 99978, jnp.int32), jax.random.randint(jax.random.fold_in(jax.random.fold_in(_rk, 1), 102), (2048,), 8, 99996, jnp.int32), jax.random.randint(jax.random.fold_in(jax.random.fold_in(_rk, 1), 103), (2048,), 205, 99859, jnp.int32), jax.random.randint(jax.random.fold_in(jax.random.fold_in(_rk, 1), 104), (2048,), 52, 99894, jnp.int32), jax.random.randint(jax.random.fold_in(jax.random.fold_in(_rk, 1), 105), (2048,), 22, 12494, jnp.int32), jax.random.randint(jax.random.fold_in(jax.random.fold_in(_rk, 1), 106), (2048,), 52, 99998, jnp.int32), jax.random.randint(jax.random.fold_in(jax.random.fold_in(_rk, 1), 107), (2048,), 0, 99964, jnp.int32), jax.random.randint(jax.random.fold_in(jax.random.fold_in(_rk, 1), 108), (2048,), 146, 99882, jnp.int32), jax.random.randint(jax.random.fold_in(jax.random.fold_in(_rk, 1), 109), (2048,), 20, 99985, jnp.int32), jax.random.randint(jax.random.fold_in(jax.random.fold_in(_rk, 1), 110), (2048,), 103, 99902, jnp.int32), jax.random.randint(jax.random.fold_in(jax.random.fold_in(_rk, 1), 111), (2048,), 94, 99973, jnp.int32), jax.random.randint(jax.random.fold_in(jax.random.fold_in(_rk, 1), 112), (2048,), 58, 99949, jnp.int32), jax.random.randint(jax.random.fold_in(jax.random.fold_in(_rk, 1), 113), (2048,), 10, 99982, jnp.int32), jax.random.randint(jax.random.fold_in(jax.random.fold_in(_rk, 1), 114), (2048,), 17, 99986, jnp.int32), jax.random.randint(jax.random.fold_in(jax.random.fold_in(_rk, 1), 115), (2048,), 26, 99987, jnp.int32), jax.random.randint(jax.random.fold_in(jax.random.fold_in(_rk, 1), 116), (2048,), 0, 99913, jnp.int32), jax.random.randint(jax.random.fold_in(jax.random.fold_in(_rk, 1), 117), (2048,), 13, 99977, jnp.int32), jax.random.randint(jax.random.fold_in(jax.random.fold_in(_rk, 1), 118), (2048,), 5, 12498, jnp.int32), jax.random.randint(jax.random.fold_in(jax.random.fold_in(_rk, 1), 119), (2048,), 190, 99973, jnp.int32), jax.random.randint(jax.random.fold_in(jax.random.fold_in(_rk, 1), 120), (2048,), 36, 99991, jnp.int32), jax.random.randint(jax.random.fold_in(jax.random.fold_in(_rk, 1), 121), (2048,), 8, 99950, jnp.int32), jax.random.randint(jax.random.fold_in(jax.random.fold_in(_rk, 1), 122), (2048,), 137, 99970, jnp.int32), jax.random.randint(jax.random.fold_in(jax.random.fold_in(_rk, 1), 123), (2048,), 77, 99947, jnp.int32), jax.random.randint(jax.random.fold_in(jax.random.fold_in(_rk, 1), 124), (2048,), 39, 99990, jnp.int32), jax.random.randint(jax.random.fold_in(jax.random.fold_in(_rk, 1), 125), (2048,), 32, 99828, jnp.int32), jax.random.randint(jax.random.fold_in(jax.random.fold_in(_rk, 1), 126), (2048,), 2, 99985, jnp.int32), jax.random.randint(jax.random.fold_in(jax.random.fold_in(_rk, 1), 127), (2048,), 92, 99963, jnp.int32), jax.random.randint(jax.random.fold_in(jax.random.fold_in(_rk, 1), 128), (2048,), 2, 99973, jnp.int32), jax.random.randint(jax.random.fold_in(jax.random.fold_in(_rk, 1), 129), (2048,), 245, 99993, jnp.int32), jax.random.randint(jax.random.fold_in(jax.random.fold_in(_rk, 1), 130), (2048,), 30, 99967, jnp.int32), jax.random.randint(jax.random.fold_in(jax.random.fold_in(_rk, 1), 131), (2048,), 247, 99870, jnp.int32), jax.random.randint(jax.random.fold_in(jax.random.fold_in(_rk, 1), 132), (2048,), 89, 99993, jnp.int32), jax.random.randint(jax.random.fold_in(jax.random.fold_in(_rk, 1), 133), (2048,), 11, 99972, jnp.int32), jax.random.randint(jax.random.fold_in(jax.random.fold_in(_rk, 1), 134), (2048,), 58, 99934, jnp.int32), jax.random.randint(jax.random.fold_in(jax.random.fold_in(_rk, 1), 135), (2048,), 120, 99978, jnp.int32), jax.random.randint(jax.random.fold_in(jax.random.fold_in(_rk, 1), 136), (2048,), 67, 99919, jnp.int32), jax.random.randint(jax.random.fold_in(jax.random.fold_in(_rk, 1), 137), (2048,), 84, 99940, jnp.int32), jax.random.randint(jax.random.fold_in(jax.random.fold_in(_rk, 1), 138), (2048,), 10, 99927, jnp.int32), jax.random.randint(jax.random.fold_in(jax.random.fold_in(_rk, 1), 139), (2048,), 22, 99977, jnp.int32), jax.random.randint(jax.random.fold_in(jax.random.fold_in(_rk, 1), 140), (2048,), 28, 99921, jnp.int32), jax.random.randint(jax.random.fold_in(jax.random.fold_in(_rk, 1), 141), (2048,), 84, 99961, jnp.int32), jax.random.randint(jax.random.fold_in(jax.random.fold_in(_rk, 1), 142), (2048,), 41, 99883, jnp.int32), jax.random.randint(jax.random.fold_in(jax.random.fold_in(_rk, 1), 143), (2048,), 123, 99942, jnp.int32), jax.random.randint(jax.random.fold_in(jax.random.fold_in(_rk, 1), 144), (2048,), 36, 99930, jnp.int32), jax.random.randint(jax.random.fold_in(jax.random.fold_in(_rk, 1), 145), (2048,), 118, 99965, jnp.int32), jax.random.randint(jax.random.fold_in(jax.random.fold_in(_rk, 1), 146), (2048,), 78, 99900, jnp.int32), jax.random.randint(jax.random.fold_in(jax.random.fold_in(_rk, 1), 147), (2048,), 24, 99982, jnp.int32), jax.random.randint(jax.random.fold_in(jax.random.fold_in(_rk, 1), 148), (2048,), 101, 99973, jnp.int32), jax.random.randint(jax.random.fold_in(jax.random.fold_in(_rk, 1), 149), (2048,), 48, 99997, jnp.int32), jax.random.randint(jax.random.fold_in(jax.random.fold_in(_rk, 1), 150), (2048,), 129, 99954, jnp.int32), jax.random.randint(jax.random.fold_in(jax.random.fold_in(_rk, 1), 151), (2048,), 152, 99966, jnp.int32), jax.random.randint(jax.random.fold_in(jax.random.fold_in(_rk, 1), 152), (2048,), 62, 99747, jnp.int32), jax.random.randint(jax.random.fold_in(jax.random.fold_in(_rk, 1), 153), (2048,), 63, 99997, jnp.int32), jax.random.randint(jax.random.fold_in(jax.random.fold_in(_rk, 1), 154), (2048,), 148, 99993, jnp.int32), jax.random.randint(jax.random.fold_in(jax.random.fold_in(_rk, 1), 155), (2048,), 108, 12494, jnp.int32), jax.random.randint(jax.random.fold_in(jax.random.fold_in(_rk, 1), 156), (2048,), 11, 99988, jnp.int32), jax.random.randint(jax.random.fold_in(jax.random.fold_in(_rk, 1), 157), (2048,), 2, 12494, jnp.int32), jax.random.randint(jax.random.fold_in(jax.random.fold_in(_rk, 1), 158), (2048,), 18, 99998, jnp.int32), jax.random.randint(jax.random.fold_in(jax.random.fold_in(_rk, 1), 159), (2048,), 64, 99988, jnp.int32), jax.random.randint(jax.random.fold_in(jax.random.fold_in(_rk, 1), 160), (2048,), 13, 99935, jnp.int32), jax.random.randint(jax.random.fold_in(jax.random.fold_in(_rk, 1), 161), (2048,), 103, 99963, jnp.int32), jax.random.randint(jax.random.fold_in(jax.random.fold_in(_rk, 1), 162), (2048,), 11, 99986, jnp.int32), jax.random.randint(jax.random.fold_in(jax.random.fold_in(_rk, 1), 163), (2048,), 14, 99978, jnp.int32), jax.random.randint(jax.random.fold_in(jax.random.fold_in(_rk, 1), 164), (2048,), 31, 99973, jnp.int32), jax.random.randint(jax.random.fold_in(jax.random.fold_in(_rk, 1), 165), (2048,), 18, 99979, jnp.int32), jax.random.randint(jax.random.fold_in(jax.random.fold_in(_rk, 1), 166), (2048,), 31, 99963, jnp.int32), jax.random.randint(jax.random.fold_in(jax.random.fold_in(_rk, 1), 167), (2048,), 125, 12483, jnp.int32), jax.random.randint(jax.random.fold_in(jax.random.fold_in(_rk, 1), 168), (2048,), 20, 99995, jnp.int32), jax.random.randint(jax.random.fold_in(jax.random.fold_in(_rk, 1), 169), (2048,), 39, 99980, jnp.int32), jax.random.randint(jax.random.fold_in(jax.random.fold_in(_rk, 1), 170), (2048,), 32, 99975, jnp.int32), jax.random.randint(jax.random.fold_in(jax.random.fold_in(_rk, 1), 171), (2048,), 80, 99883, jnp.int32), jax.random.randint(jax.random.fold_in(jax.random.fold_in(_rk, 1), 172), (2048,), 24, 99986, jnp.int32), jax.random.randint(jax.random.fold_in(jax.random.fold_in(_rk, 1), 173), (2048,), 12, 99942, jnp.int32), jax.random.randint(jax.random.fold_in(jax.random.fold_in(_rk, 1), 174), (2048,), 144, 99982, jnp.int32), jax.random.randint(jax.random.fold_in(jax.random.fold_in(_rk, 1), 175), (2048,), 19, 99924, jnp.int32), jax.random.randint(jax.random.fold_in(jax.random.fold_in(_rk, 1), 176), (2048,), 7, 99990, jnp.int32), jax.random.randint(jax.random.fold_in(jax.random.fold_in(_rk, 1), 177), (2048,), 68, 99991, jnp.int32), jax.random.randint(jax.random.fold_in(jax.random.fold_in(_rk, 1), 178), (2048,), 26, 99993, jnp.int32), jax.random.randint(jax.random.fold_in(jax.random.fold_in(_rk, 1), 179), (2048,), 81, 99987, jnp.int32), jax.random.randint(jax.random.fold_in(jax.random.fold_in(_rk, 1), 180), (2048,), 87, 99982, jnp.int32), jax.random.randint(jax.random.fold_in(jax.random.fold_in(_rk, 1), 181), (2048,), 13, 99908, jnp.int32), jax.random.randint(jax.random.fold_in(jax.random.fold_in(_rk, 1), 182), (2048,), 58, 99993, jnp.int32), jax.random.randint(jax.random.fold_in(jax.random.fold_in(_rk, 1), 183), (2048,), 42, 99994, jnp.int32), jax.random.randint(jax.random.fold_in(jax.random.fold_in(_rk, 1), 184), (2048,), 0, 12491, jnp.int32), jax.random.randint(jax.random.fold_in(jax.random.fold_in(_rk, 1), 185), (2048,), 2, 99977, jnp.int32), jax.random.randint(jax.random.fold_in(jax.random.fold_in(_rk, 1), 186), (2048,), 12, 99980, jnp.int32), jax.random.randint(jax.random.fold_in(jax.random.fold_in(_rk, 1), 187), (2048,), 29, 99998, jnp.int32), jax.random.randint(jax.random.fold_in(jax.random.fold_in(_rk, 1), 188), (2048,), 155, 99899, jnp.int32), jax.random.randint(jax.random.fold_in(jax.random.fold_in(_rk, 1), 189), (2048,), 34, 12500, jnp.int32), jax.random.randint(jax.random.fold_in(jax.random.fold_in(_rk, 1), 190), (2048,), 29, 12481, jnp.int32), jax.random.randint(jax.random.fold_in(jax.random.fold_in(_rk, 1), 191), (2048,), 0, 99996, jnp.int32), jax.random.randint(jax.random.fold_in(jax.random.fold_in(_rk, 1), 192), (2048,), 24, 99949, jnp.int32), jax.random.randint(jax.random.fold_in(jax.random.fold_in(_rk, 1), 193), (2048,), 16, 99925, jnp.int32), jax.random.randint(jax.random.fold_in(jax.random.fold_in(_rk, 1), 194), (2048,), 9, 99919, jnp.int32), jax.random.randint(jax.random.fold_in(jax.random.fold_in(_rk, 1), 195), (2048,), 59, 99979, jnp.int32), jax.random.randint(jax.random.fold_in(jax.random.fold_in(_rk, 1), 196), (2048,), 89, 99990, jnp.int32), jax.random.randint(jax.random.fold_in(jax.random.fold_in(_rk, 1), 197), (2048,), 8, 99906, jnp.int32), jax.random.randint(jax.random.fold_in(jax.random.fold_in(_rk, 1), 198), (2048,), 153, 99926, jnp.int32), jax.random.randint(jax.random.fold_in(jax.random.fold_in(_rk, 1), 199), (2048,), 4, 99981, jnp.int32), jax.random.randint(jax.random.fold_in(jax.random.fold_in(_rk, 1), 200), (2048,), 6, 99963, jnp.int32), jax.random.randint(jax.random.fold_in(jax.random.fold_in(_rk, 1), 201), (2048,), 0, 99967, jnp.int32)], axis=1)
        return r_rowData
    r_rowData = _rec_inputs()

    def _L0_rec_setup():
        import jax, jax.numpy as jnp
        import numpy as np
        B, T, G = (256, 200, 6)
        N_MOVIES, GENRE_VOCAB, E = (12500, 20, 64)
        EPS_POOL = 1e-08
        BN_EPS = 1e-05

        def prelu(x, a):
            return jnp.where(x >= 0, x, a * x)

        def bn_train(x, g, b):
            m = jnp.mean(x, axis=0)
            v = jnp.var(x, axis=0)
            return (x - m) / jnp.sqrt(v + BN_EPS) * g + b

        def masked_mean(emb, ids):
            mask = (ids > 0).astype(jnp.float32)
            length = jnp.sum(mask, axis=-1, keepdims=True)
            return jnp.sum(emb, axis=-2) / (length + EPS_POOL)
        key = jax.random.key(seed)
        ks = jax.random.split(key, 24)
        rowData = jax.random.randint(ks[0], (B, T + 2), 0, N_MOVIES)
        userFeature = jax.random.randint(ks[1], (B, 1), 0, 755)
        movie_ids = jax.random.randint(ks[2], (N_MOVIES, 1), 0, N_MOVIES)
        genres = jax.random.randint(ks[3], (N_MOVIES, G), 0, GENRE_VOCAB)
        movieFeature = jnp.concatenate([movie_ids, genres], axis=1)

        def w(k, shape):
            fan_in = shape[0]
            return jax.random.normal(k, shape, dtype=jnp.float32) / np.sqrt(fan_in)
        emb_movie = (jax.random.normal(ks[4], (N_MOVIES, E)) * 0.01).at[0].set(0.0)
        emb_genre = (jax.random.normal(ks[5], (GENRE_VOCAB, E)) * 0.01).at[0].set(0.0)
        return {'rowData': rowData, 'userFeature': userFeature, 'movieFeature': movieFeature, 'emb_movie': emb_movie, 'emb_genre': emb_genre, 'att_w1': w(ks[6], (6 * E, 80)), 'att_b1': jnp.zeros((80,)), 'att_a1': jnp.float32(0.25), 'att_w2': w(ks[7], (80, 40)), 'att_b2': jnp.zeros((40,)), 'att_a2': jnp.float32(0.25), 'att_wo': w(ks[8], (40, 1)), 'att_bo': jnp.zeros((1,)), 'mlp_w1': w(ks[9], (4 * E, 200)), 'mlp_b1': jnp.zeros((200,)), 'bn1_g': jnp.ones((200,)), 'bn1_b': jnp.zeros((200,)), 'mlp_a1': jnp.float32(0.25), 'mlp_w2': w(ks[10], (200, 80)), 'mlp_b2': jnp.zeros((80,)), 'bn2_g': jnp.ones((80,)), 'bn2_b': jnp.zeros((80,)), 'mlp_a2': jnp.float32(0.25), 'out_w': w(ks[11], (80, 2)), 'out_b': jnp.zeros((2,))}
    _L0_rec_all = _L0_rec_setup()
    _L0_rec_in = {k: v for k, v in _L0_rec_all.items() if k in ('userFeature', 'movieFeature', 'emb_movie', 'emb_genre', 'att_w1', 'att_b1', 'att_a1', 'att_w2', 'att_b2', 'att_a2', 'att_wo', 'att_bo', 'mlp_w1', 'mlp_b1', 'bn1_g', 'bn1_b', 'mlp_a1', 'mlp_w2', 'mlp_b2', 'bn2_g', 'bn2_b', 'mlp_a2', 'out_w', 'out_b')}
    del _L0_rec_all
    return {'r_rowData': r_rowData, 'L0_rec_userFeature': _L0_rec_in['userFeature'], 'L0_rec_movieFeature': _L0_rec_in['movieFeature'], 'L0_rec_emb_movie': _L0_rec_in['emb_movie'], 'L0_rec_emb_genre': _L0_rec_in['emb_genre'], 'L0_rec_att_w1': _L0_rec_in['att_w1'], 'L0_rec_att_b1': _L0_rec_in['att_b1'], 'L0_rec_att_a1': _L0_rec_in['att_a1'], 'L0_rec_att_w2': _L0_rec_in['att_w2'], 'L0_rec_att_b2': _L0_rec_in['att_b2'], 'L0_rec_att_a2': _L0_rec_in['att_a2'], 'L0_rec_att_wo': _L0_rec_in['att_wo'], 'L0_rec_att_bo': _L0_rec_in['att_bo'], 'L0_rec_mlp_w1': _L0_rec_in['mlp_w1'], 'L0_rec_mlp_b1': _L0_rec_in['mlp_b1'], 'L0_rec_bn1_g': _L0_rec_in['bn1_g'], 'L0_rec_bn1_b': _L0_rec_in['bn1_b'], 'L0_rec_mlp_a1': _L0_rec_in['mlp_a1'], 'L0_rec_mlp_w2': _L0_rec_in['mlp_w2'], 'L0_rec_mlp_b2': _L0_rec_in['mlp_b2'], 'L0_rec_bn2_g': _L0_rec_in['bn2_g'], 'L0_rec_bn2_b': _L0_rec_in['bn2_b'], 'L0_rec_mlp_a2': _L0_rec_in['mlp_a2'], 'L0_rec_out_w': _L0_rec_in['out_w'], 'L0_rec_out_b': _L0_rec_in['out_b']}

def reference(r_rowData, L0_rec_userFeature, L0_rec_movieFeature, L0_rec_emb_movie, L0_rec_emb_genre, L0_rec_att_w1, L0_rec_att_b1, L0_rec_att_a1, L0_rec_att_w2, L0_rec_att_b2, L0_rec_att_a2, L0_rec_att_wo, L0_rec_att_bo, L0_rec_mlp_w1, L0_rec_mlp_b1, L0_rec_bn1_g, L0_rec_bn1_b, L0_rec_mlp_a1, L0_rec_mlp_w2, L0_rec_mlp_b2, L0_rec_bn2_g, L0_rec_bn2_b, L0_rec_mlp_a2, L0_rec_out_w, L0_rec_out_b):
    import jax
    import jax.numpy as jnp

    def _L0_rec_ref(rowData, userFeature, movieFeature, emb_movie, emb_genre, att_w1, att_b1, att_a1, att_w2, att_b2, att_a2, att_wo, att_bo, mlp_w1, mlp_b1, bn1_g, bn1_b, mlp_a1, mlp_w2, mlp_b2, bn2_g, bn2_b, mlp_a2, out_w, out_b):
        import jax, jax.numpy as jnp
        import numpy as np
        B, T, G = (256, 200, 6)
        N_MOVIES, GENRE_VOCAB, E = (12500, 20, 64)
        EPS_POOL = 1e-08
        BN_EPS = 1e-05

        def prelu(x, a):
            return jnp.where(x >= 0, x, a * x)

        def bn_train(x, g, b):
            m = jnp.mean(x, axis=0)
            v = jnp.var(x, axis=0)
            return (x - m) / jnp.sqrt(v + BN_EPS) * g + b

        def masked_mean(emb, ids):
            mask = (ids > 0).astype(jnp.float32)
            length = jnp.sum(mask, axis=-1, keepdims=True)
            return jnp.sum(emb, axis=-2) / (length + EPS_POOL)
        seq = rowData[:, 1:-1]
        ads = rowData[:, -1]
        mfs = movieFeature[seq]
        adsF = movieFeature[ads]
        movieIdFeat = emb_movie[mfs[:, :, 0]]
        movieGenreFeat = masked_mean(emb_genre[mfs[:, :, 1:]], mfs[:, :, 1:])
        adsIdFeat = emb_movie[adsF[:, 0]]
        adsGenreFeat = masked_mean(emb_genre[adsF[:, 1:]], adsF[:, 1:])
        movieEmb = jnp.concatenate([movieIdFeat, movieGenreFeat], axis=-1)
        adsEmb = jnp.concatenate([adsIdFeat, adsGenreFeat], axis=-1)
        target = jnp.broadcast_to(adsEmb[:, None, :], movieEmb.shape)
        x = jnp.concatenate([movieEmb, target, movieEmb * target], axis=-1)
        h = prelu(x @ att_w1 + att_b1, att_a1)
        h = prelu(h @ att_w2 + att_b2, att_a2)
        attW = h @ att_wo + att_bo
        pooled = jnp.sum(movieEmb * attW, axis=-2)
        z = jnp.concatenate([pooled, adsEmb], axis=-1)
        z = prelu(bn_train(z @ mlp_w1 + mlp_b1, bn1_g, bn1_b), mlp_a1)
        z = prelu(bn_train(z @ mlp_w2 + mlp_b2, bn2_g, bn2_b), mlp_a2)
        return jax.nn.softmax(z @ out_w + out_b, axis=1)
    y = _L0_rec_ref(r_rowData, L0_rec_userFeature, L0_rec_movieFeature, L0_rec_emb_movie, L0_rec_emb_genre, L0_rec_att_w1, L0_rec_att_b1, L0_rec_att_a1, L0_rec_att_w2, L0_rec_att_b2, L0_rec_att_a2, L0_rec_att_wo, L0_rec_att_bo, L0_rec_mlp_w1, L0_rec_mlp_b1, L0_rec_bn1_g, L0_rec_bn1_b, L0_rec_mlp_a1, L0_rec_mlp_w2, L0_rec_mlp_b2, L0_rec_bn2_g, L0_rec_bn2_b, L0_rec_mlp_a2, L0_rec_out_w, L0_rec_out_b)
    return y

_drawn_inputs = setup_inputs


def setup_inputs(seed=0):
    import zlib

    import numpy as np

    out = dict(_drawn_inputs(seed))
    spreads = {'L0_rec_att_b1': (0.0, 0.1),
     'L0_rec_att_b2': (0.0, 0.1),
     'L0_rec_mlp_b1': (0.0, 0.8),
     'L0_rec_bn1_g': (1.0, 0.2),
     'L0_rec_bn1_b': (0.0, 0.374),
     'L0_rec_mlp_b2': (0.0, 0.8),
     'L0_rec_bn2_g': (1.0, 0.2),
     'L0_rec_bn2_b': (0.0, 0.1),
     'L0_rec_out_b': (0.0, 0.1)}
    factors = {}
    for name, (base, spread) in spreads.items():
        noise = np.random.default_rng([zlib.crc32(name.encode()), seed]).standard_normal(out[name].shape)
        drawn = base * np.exp(spread * noise) if base else spread * noise
        out[name] = jnp.asarray(drawn.astype(out[name].dtype))
    for name, factor in factors.items():
        out[name] = (out[name] * factor).astype(out[name].dtype)
    return out
```

```python
from contextlib import ExitStack

import concourse.bass as bass
from concourse import mybir
from concourse.alu_op_type import AluOpType as ALU

ACT = mybir.ActivationFunctionType
F32 = mybir.dt.float32
BF16 = mybir.dt.bfloat16
I32 = mybir.dt.int32
U32 = mybir.dt.uint32
AX_X = mybir.AxisListType.X

USERS = 8
PARTS = 3
UNIT_TILES = 3
UNIT = 128 * UNIT_TILES
RUN = 64
RING = 8
BN_EPS = 1e-5
POOL_EPS = 1e-8


class Step:

    def __init__(self, block, slot, first_block, last):
        self.block, self.slot, self.first_block, self.last = block, slot, first_block, last

    def has(self, lag):
        if not isinstance(self.block, int):
            return True
        return 0 <= RING * self.block + self.slot - lag < self.last

    def unit(self, lag):
        return Unit(self.block - (self.slot < lag), (self.slot - lag) % RING, self.first_block)


class Unit:

    def __init__(self, block, slot, first_block):
        self.slot = slot
        self.group = RING * block + slot
        self.turn = block + first_block
        self.n = RING * self.turn + slot

    def after(self, depth):
        return not isinstance(self.n, int) or self.n >= depth


def columns(first, n):
    return slice(first, first + n) if isinstance(first, int) else bass.ds(first, n)


def run_pass(eng, step, groups, first_block, lag):
    for s in range(RING):
        step(Step(0, s, first_block, groups))
    with eng.Fori(1, groups // RING) as block:
        for s in range(RING):
            step(Step(block, s, first_block, groups))
    for s in range(lag):
        step(Step(groups // RING, s, first_block, groups))


def build(nc, rows, movie_feature, emb_movie, emb_genre, att_w1, att_b1, att_a1, att_w2, att_b2,
          att_a2, att_wo, att_bo, mlp_w1, mlp_b1, bn1_g, bn1_b, mlp_a1, mlp_w2, mlp_b2, bn2_g,
          bn2_b, mlp_a2, out_w, out_b, out):
    B, NCOL = rows.shape
    T = NCOL - 2
    N_ROWS, FEATS = movie_feature.shape
    GENRES = FEATS - 1
    VOCAB, E = emb_genre.shape
    D = 2 * E
    H1, H2 = att_w2.shape
    M1, M2 = mlp_w2.shape
    GROUPS = B // USERS
    TILES = GROUPS // 128
    LAST_ROW = N_ROWS - 1
    PASSES = -(-USERS * T // UNIT)
    REGION = PASSES * UNIT
    UPPER = 64
    H2X = UPPER + H2
    SEG = 3 * USERS
    TP = 125
    TK = N_ROWS // TP
    KB = 5
    PIECES = 4
    MH = M1 // 2
    NCH = 4
    CH = B // NCH
    TC = D + H1
    assert B % (USERS * 128) == 0 and N_ROWS == TP * TK and D == 128 and TK % (KB * PIECES) == 0

    list_dram = nc.dram_tensor("list_dram", [GROUPS * REGION, 1], U32, kind="Internal").ap()
    table_dram = nc.dram_tensor("table_dram", [N_ROWS, D], F32, kind="Internal").ap()
    seg_dram = nc.dram_tensor("seg_dram", [GROUPS, SEG], F32, kind="Internal").ap()
    tc_dram = nc.dram_tensor("tc_dram", [GROUPS, USERS * PARTS, TC], BF16, kind="Internal").ap()
    list_by_group = list_dram.rearrange("(g e) o -> g (e o)", e=REGION)
    unit_lists = list_dram.rearrange("(g c p k) o -> g c p (k o)", c=PASSES, p=128, k=UNIT_TILES)

    with ExitStack() as ctx:
        def sb(name, shape, dt=F32):
            return ctx.enter_context(nc.sbuf_tensor(name, shape, dt))

        def bank(name, shape=(128, 512), dt=F32):
            return ctx.enter_context(nc.psum_tensor(name, list(shape), dt))

        def sem(name):
            return ctx.enter_context(nc.semaphore(name))

        rows_sb = sb("rows_sb", [128, TILES, USERS, NCOL], I32)
        idx_sb = sb("idx_sb", [128, TILES, USERS, NCOL], U32)
        key_sb = sb("key_sb", [128, TILES, USERS, NCOL])
        work = sb("work", [128, TILES, T])
        best = sb("best", [128, TILES, RUN])
        run_idx = sb("run_idx", [128, TILES, USERS, RUN], U32)
        count = sb("count", [128, TILES, USERS])
        start9 = sb("start9", [128, TILES, USERS + 1])
        seg_sb = sb("seg_sb", [128, TILES, 3, USERS])
        rep_sb = sb("rep_sb", [128, TILES, 2, USERS, PARTS])
        seg_rows = sb("seg_rows", [USERS * PARTS, 2, GROUPS])
        seg_all = sb("seg_all", [128, GROUPS, 3, USERS])
        scatter_to = sb("scatter_to", [128, TILES, USERS], U32)
        small = sb("small", [128, 4, TILES, USERS])
        flag_col = sb("flag_col", [128, 1])
        flag_i = sb("flag_i", [1, 1], I32)
        group_base = sb("group_base", [128, TILES, 1], I32)
        plain_start = sb("plain_start", [128, USERS], I32)
        ident = sb("ident", [128, 128])
        ones_col = sb("ones_col", [128, 1])
        ones_row = sb("ones_row", [1, 128])

        feat_sb = sb("feat_sb", [TP, TK, FEATS], I32)
        feat_f = sb("feat_f", [TP, 2, TK, FEATS])
        movie_idx = sb("movie_idx", [TP, TK], U32)
        genre_bf = sb("genre_bf", [TP, GENRES, TK], BF16)
        genre_is = sb("genre_is", [TP, VOCAB // 2, GENRES, TK], BF16)
        genre_cnt = sb("genre_cnt", [TP, TK, VOCAB])
        genre_cntT = sb("genre_cntT", [KB * VOCAB, 2, TP])
        genre_blocks = sb("genre_blocks", [KB * VOCAB, KB * E])
        genre_len = sb("genre_len", [TP, 2, TK])
        table_whole = sb("table_sb", [128, TK, D])
        table_sb = table_whole[0:TP]

        w1_sb = sb("w1_sb", [D, 3, H1])
        b1_row = sb("b1_row", [1, H1])
        w2_sb = sb("w2_sb", [H1, H2X])
        b2_col = sb("b2_col", [H2X, 1])
        wo_col = sb("wo_col", [H2X, 1])
        scal = sb("scal", [128, 8])
        A1, A2, BO, AM1, AM2, C1, CM1, CM2 = range(8)

        adsT = sb("adsT", [D, USERS, GROUPS])

        idx_ring = sb("idx_ring", [128, RING, UNIT_TILES], U32)
        tc_ring = sb("tc_ring", [USERS * PARTS, RING, TC], BF16)
        entries = rows_sb[:, :, :, :].rearrange("p t u c -> p (t u c)").bitcast(F32)[
            :, 0:RING * UNIT_TILES * D].rearrange("p (r k d) -> p r k d", r=RING, k=UNIT_TILES)
        pos_row = sb("pos_row", [USERS * PARTS, UNIT_TILES, 128])
        pos_init = sb("pos_init", [128, UNIT_TILES])
        pos_col = sb("pos_col", [128, 2, UNIT_TILES])
        past_end = sb("past_end", [USERS * PARTS, 2, UNIT])
        user_of = sb("user_of", [USERS * PARTS, 2, UNIT], BF16)
        wts = sb("wts", [128, 2, 4, UNIT_TILES, USERS])
        wt_tmp = sb("wt_tmp", [128, 3, 4, UNIT_TILES, USERS])
        entT = sb("entT", [D, 2, UNIT])
        prodT = sb("prodT", [D, 2, UNIT])
        neg1 = sb("neg1", [H1, 2, UNIT])
        act1 = sb("act1", [H1, 2, UNIT])
        act2 = sb("act2", [H2X, 2, UNIT])
        att_w = sb("att_w", [128, 2, UNIT_TILES, USERS])
        pooledT = sb("pooledT", [D, USERS, GROUPS])

        m1_sb = sb("m1_sb", [D, 2, M1])
        m2_sb = sb("m2_sb", [MH, 2, M2])
        bnp1 = sb("bnp1", [MH, 3, 2])
        bnp2 = sb("bnp2", [M2, 3])
        ow_sb = sb("ow_sb", [M2, 2])
        ob_sb = sb("ob_sb", [128, 2])
        stats = sb("stats", [128, 3, NCH, 6])
        aggr = sb("aggr", [128, 3, 2])
        bnv = sb("bnv", [128, 3, 8])
        probs = sb("probs", [128, TILES * USERS, 2])
        lmax = sb("lmax", [128, 2, TILES * USERS])
        arena = table_whole[:, :, :].rearrange("p k d -> p (k d)")
        sizes = [TILES * USERS * D, 8 * TC, 8 * TC, 8 * PARTS * TC // 2]
        at = [sum(sizes[:i]) for i in range(5)]
        ads_rows = arena[:, at[0]:at[1]].rearrange("p (t u d) -> p t u d", t=TILES, u=USERS)
        tc_val = arena[:, at[1]:at[2]].rearrange("p (i u c) -> p i u c", i=2, u=4)
        tc_res = arena[:, at[2]:at[3]].rearrange("p (i u c) -> p i u c", i=2, u=4)
        tc_parts = arena[:, at[3]:at[4]].bitcast(BF16).rearrange(
            "p (i u s c) -> p i u s c", i=2, u=4, s=PARTS)
        z1 = arena[0:MH, 0:2 * B].rearrange("p (h b) -> p h b", h=2)
        z1n = arena[0:MH, 2 * B:4 * B].rearrange("p (h b) -> p h b", h=2)
        z2 = arena[0:M2, 4 * B:5 * B]
        z2n = arena[0:M2, 5 * B:6 * B]

        ps_ent = [bank("ps_ent0"), bank("ps_ent1")]
        ps_tgt = bank("ps_tgt")
        ps_h1 = [bank("ps_h1a"), bank("ps_h1b")]
        ps_h2 = bank("ps_h2")
        ps_att = bank("ps_att")
        ps_pool = bank("ps_pool")

        s_rows = sem("rows_in")
        s_feat = sem("feat_in")
        s_w = sem("weights_in")
        s_wz = sem("weights_zeroed")
        s_wsc = sem("weights_scaled")
        s_mlpw = sem("mlp_weights_in")
        s_const = sem("constants_made")
        s_ident = sem("identity_zeroed")
        s_d = sem("vector_steps")
        s_idx = sem("row_numbers_made")
        s_seg = sem("segments_made")
        s_movie = sem("movie_numbers_made")
        s_cnt = sem("genre_counts_made")
        s_blocks = sem("genre_blocks_in")
        s_blkz = sem("genre_blocks_zeroed")
        s_listp = sem("plain_lists_out")
        s_segout = sem("segments_out")
        s_segin = sem("segments_in")
        s_flag_ps = sem("flag_summed")
        s_flag = sem("flag_ready")
        s_segT = sem("segments_turned")
        s_segrow = sem("segment_rows_ready")
        s_runs = sem("runs_sorted")
        s_scat = [sem(f"runs_out{t}") for t in range(TILES)]
        s_lists = sem("lists_ready")
        s_tabrow = [sem(f"table_movies{q}") for q in range(PIECES)]
        s_cT = sem("counts_turned")
        s_cTc = sem("counts_copied")
        s_gps = sem("genre_products")
        s_gev = sem("genre_halves_written")
        s_table = sem("table_out")
        s_ads = sem("ads_gathered")
        s_adsps = sem("ads_turned")
        s_adsT = sem("ads_copied")
        s_cps = sem("target_share_products")
        s_tcv = sem("target_values_ready")
        s_tchi = sem("target_parts_hi")
        s_tcr = sem("target_rests")
        s_tcp = sem("target_parts_ready")
        s_tcout = [sem(f"target_parts_out{i}") for i in range(2)]

        s_ix = [sem(f"unit_index{k}") for k in range(RING)]
        s_tc = [sem(f"unit_target{k}") for k in range(RING)]
        s_g = [sem(f"unit_entries{k}") for k in range(RING)]
        s_begun = sem("unit_gathers_begun")
        s_oh_t = sem("past_end_made")
        s_oh = sem("user_matrix_made")
        s_wt = sem("weight_steps")
        s_T = sem("entries_turned")
        s_tg = sem("targets_spread")
        s_cp = sem("entries_copied")
        s_pr = sem("products_made")
        s_1 = sem("layer1_summed")
        s_n = sem("layer1_negated")
        s_a1 = sem("layer1_done")
        s_2 = sem("layer2_summed")
        s_a2 = sem("layer2_done")
        s_at = sem("attention_summed")
        s_aw = sem("attention_weighted")
        s_pl = sem("pool_summed")
        s_pa = sem("pool_added")
        s_pos = sem("positions_moved")
        s_main_dve = sem("vector_main_done")

        s_m1 = sem("mlp1_summed")
        s_m1c = sem("mlp1_copied")
        s_v1 = sem("norm1_variance")
        s_sq1 = sem("norm1_root")
        s_bn1 = sem("norm1_ready")
        s_n1 = sem("mlp1_negated")
        s_z1 = sem("mlp1_done")
        s_m2 = sem("mlp2_summed")
        s_m2c = sem("mlp2_copied")
        s_v2 = sem("norm2_variance")
        s_sq2 = sem("norm2_root")
        s_bn2 = sem("norm2_ready")
        s_n2 = sem("mlp2_negated")
        s_z2 = sem("mlp2_done")
        s_lg = sem("logits_summed")
        s_sh = sem("logits_shifted")
        s_ex = sem("exponentials")
        s_pb = sem("probabilities")
        s_out = sem("output_out")

        N_CONST = 8 + TILES
        N_W = 13
        block = ctx.enter_context(nc.Block())

        @block.sync
        def _(sp):
            rows_v = rows.rearrange("(t p u) c -> t p (u c)", t=TILES, u=USERS)
            sp.dma_start(feat_sb[:, :, :].rearrange("p k c -> p (k c)"),
                         movie_feature.rearrange("(p k) c -> p (k c)", p=TP)).then_inc(s_feat, 16)
            for t in range(TILES):
                sp.dma_start(rows_sb[:, t, :, :].rearrange("p u c -> p (u c)"),
                             rows_v[t]).then_inc(s_rows, 16)
            sp.wait_ge(s_blkz, 1)
            for i in range(KB):
                sp.dma_start(genre_blocks[i * VOCAB:(i + 1) * VOCAB, i * E:(i + 1) * E],
                             emb_genre).then_inc(s_blocks, 16)

            sp.wait_ge(s_idx, TILES)
            for t in range(TILES):
                groups = list_by_group[t * 128:(t + 1) * 128, :]
                sp.dma_start(groups[:, 0:USERS * T].rearrange("g (u e) -> g u e", u=USERS),
                             idx_sb[:, t, :, 1:1 + T]).then_inc(s_listp, 16)
                sp.dma_start(groups[:, USERS * T:REGION],
                             idx_sb[:, t, :, :].rearrange("p u c -> p (u c)")
                             [:, 0:REGION - USERS * T]).then_inc(s_listp, 16)

            sp.wait_ge(s_seg, 1)
            sp.dma_start(seg_dram.rearrange("(t p) s -> p t s", t=TILES),
                         seg_sb[:, :, :, :].rearrange("p t s u -> p t (s u)")).then_inc(s_segout, 16)
            sp.wait_ge(s_segout, 16)
            sp.dma_start(seg_all[:, :, :, :].rearrange("p g s u -> p (g s u)"),
                         seg_dram.rearrange("(o g) s -> o (g s)", o=1)
                         .broadcast_to([128, GROUPS * SEG])).then_inc(s_segin, 16)

            table_v = table_dram.rearrange("(p k) d -> p (k d)", p=TP)
            step = TK // PIECES
            for q in range(PIECES):
                sp.wait_ge(s_tabrow[q], 16 * step)
                sp.wait_ge(s_gev, (q + 1) * step // KB)
                sp.dma_start(table_v[:, q * step * D:(q + 1) * step * D],
                             table_sb[:, q * step:(q + 1) * step, :].rearrange("p k d -> p (k d)")
                             ).then_inc(s_table, 16)

            tc_v = tc_dram.rearrange("(t p) (u s) c -> t p u s c", t=TILES, u=USERS)
            for b in range(TILES * USERS // 4):
                t, u = divmod(4 * b, USERS)
                sp.wait_ge(s_tcp, b + 1)
                sp.dma_start(tc_v[t, :, u:u + 4].rearrange("p u s c -> p (u s c)"),
                             tc_parts[:, b % 2].rearrange("p u s c -> p (u s c)")
                             ).then_inc(s_tcout[b % 2], 16)

            for i in range(2):
                sp.wait_ge(s_tcout[i], 16 * (TILES * USERS // 8))
            sp.wait_ge(s_lists, 1)
            sp.wait_ge(s_flag, 1)
            general = sp.value_load(flag_i[0:1, 0:1], min_val=0, max_val=GROUPS)

            def step_sp(s, chunk):
                if s.has(0):
                    u = s.unit(0)
                    if u.after(RING):
                        sp.wait_ge(s_g[u.slot], 16 * UNIT_TILES * u.turn)
                    sp.dma_start(idx_ring[:, u.slot, :],
                                 unit_lists[u.group, chunk]).then_inc(s_ix[u.slot], 16)
                    if u.after(RING):
                        sp.wait_ge(s_1, u.n - RING + 1)
                    sp.dma_start(tc_ring[:, u.slot, :], tc_dram[u.group]).then_inc(s_tc[u.slot], 16)

            run_pass(sp, lambda s: step_sp(s, 0), GROUPS, 0, 0)
            with sp.If(general > 0):
                with sp.Fori(1, PASSES) as p:
                    run_pass(sp, lambda s: step_sp(s, p), GROUPS, p * (GROUPS // RING), 0)
            with sp.Else():
                sp.nop()

            sp.wait_ge(s_pb, 1)
            sp.dma_start(out.rearrange("(t p u) c -> p t (u c)", t=TILES, u=USERS),
                         probs[:, :, :].rearrange("p (t u) c -> p t (u c)", t=TILES)
                         ).then_inc(s_out, 16)
            sp.wait_ge(s_out, 16)

        @block.gpsimd
        def _(pool):
            pool.memset(genre_blocks[:, :], 0.0).then_inc(s_blkz, 1)
            pool.memset(ident[:, :], 0.0).then_inc(s_ident, 1)
            pool.memset(w2_sb[:, :], 0.0).then_inc(s_wz, 1)
            pool.memset(b2_col[:, :], 0.0).then_inc(s_wz, 1)
            pool.memset(wo_col[:, :], 0.0).then_inc(s_wz, 1)
            pool.wait_ge(s_ident, 1)
            pool.affine_select(out=ident[:, :], in_=ident[:, :], compare_op=ALU.not_equal, fill=1.0,
                               base=0, pattern=[[-1, 128]], channel_multiplier=1).then_inc(s_const, 1)
            pool.memset(ones_col[:, :], 1.0).then_inc(s_const, 1)
            pool.memset(ones_row[:, :], 1.0).then_inc(s_const, 1)
            pool.memset(pooledT[:, :, :], 0.0).then_inc(s_const, 1)
            for t in range(TILES):
                pool.iota(group_base[:, t, :], pattern=[[0, 1]], base=t * 128 * REGION,
                          channel_multiplier=REGION).then_inc(s_const, 1)
            pool.iota(plain_start[:, :], pattern=[[T, USERS]], channel_multiplier=0).then_inc(s_const, 1)
            pool.iota(pos_init[:, :], pattern=[[1, UNIT_TILES]], channel_multiplier=UNIT_TILES,
                      allow_small_or_imprecise_dtypes=True).then_inc(s_const, 1)
            pool.iota(pos_row[:, :, :], pattern=[[1, UNIT_TILES], [UNIT_TILES, 128]],
                      channel_multiplier=0, allow_small_or_imprecise_dtypes=True).then_inc(s_const, 1)
            pool.memset(act2[:, :, :], 0.0).then_inc(s_const, 1)

            def gather_movies(k):
                pool.indirect_dma_start(
                    out=table_sb[:, k, 0:E], out_offset=None, in_=emb_movie,
                    in_offset=bass.IndirectOffsetOnAxis(ap=movie_idx[:, k:k + 1], axis=0),
                ).then_inc(s_tabrow[k // (TK // PIECES)], 16)

            def scatter_run(t, u):
                pool.wait_ge(s_runs, TILES * u + t + 1)
                if u:
                    pool.wait_ge(s_scat[t], 16 * u)
                pool.indirect_dma_start(
                    out=list_dram,
                    out_offset=bass.IndirectOffsetOnAxis(ap=scatter_to[:, t, u:u + 1], axis=0),
                    in_=run_idx[:, t, u, :], in_offset=None).then_inc(s_scat[t], 16)

            pool.wait_ge(s_movie, 1)
            early = TK - 4 * (USERS - 1)
            for k in range(early):
                gather_movies(k)
            pool.wait_ge(s_flag, 1)
            general = pool.value_load(flag_i[0:1, 0:1], min_val=0, max_val=GROUPS)
            pool.wait_ge(s_listp, 16 * 2 * TILES)
            with pool.If(general > 0):
                for k in range(early, TK):
                    gather_movies(k)
                pool.sem_inc(s_lists, 1)
            with pool.Else():
                for u in range(USERS):
                    for t in range(TILES):
                        scatter_run(t, u)
                    if u < USERS - 1:
                        for k in range(early + 4 * u, early + 4 * u + 4):
                            gather_movies(k)
                for t in range(TILES):
                    pool.wait_ge(s_scat[t], 16 * USERS)
                pool.sem_inc(s_lists, 1)

            pool.wait_ge(s_table, 16 * PIECES)
            for t in range(TILES):
                for u in range(USERS):
                    pool.indirect_dma_start(
                        out=ads_rows[:, t, u, :], out_offset=None, in_=table_dram,
                        in_offset=bass.IndirectOffsetOnAxis(ap=idx_sb[:, t, u, NCOL - 1:NCOL], axis=0),
                    ).then_inc(s_ads, 16)

            def step_pool(s):
                if s.has(0):
                    u = s.unit(0)
                    pool.wait_ge(s_ix[u.slot], 16 * (u.turn + 1))
                    if u.after(RING):
                        pool.wait_ge(s_pl, u.n - RING + 1)
                    pool.sem_inc(s_begun, 1)
                    for k in range(UNIT_TILES):
                        pool.indirect_dma_start(
                            out=entries[:, u.slot, k, :], out_offset=None, in_=table_dram,
                            in_offset=bass.IndirectOffsetOnAxis(ap=idx_ring[:, u.slot, k:k + 1], axis=0),
                        ).then_inc(s_g[u.slot], 16)

            run_pass(pool, step_pool, GROUPS, 0, 0)
            with pool.If(general > 0):
                with pool.Fori(1, PASSES) as p:
                    run_pass(pool, step_pool, GROUPS, p * (GROUPS // RING), 0)
            with pool.Else():
                pool.nop()

        @block.scalar
        def _(act):
            def load(dst, src, s):
                act.dma_start(dst, src).then_inc(s, 16)

            def col(v):
                return v.rearrange("(p o) -> p o", o=1)

            load(w1_sb[:, :, :], att_w1.rearrange("(s p) h -> p s h", p=D), s_w)
            load(b1_row[:, :], att_b1.rearrange("(o h) -> o h", o=1), s_w)
            for c, v in ((A1, att_a1), (A2, att_a2), (BO, att_bo), (AM1, mlp_a1), (AM2, mlp_a2)):
                load(scal[:, c:c + 1], v.rearrange("(o h) -> o h", o=1).broadcast_to([128, 1]), s_w)
            act.wait_ge(s_wz, 3)
            for p in (0, UPPER):
                load(w2_sb[:, p:p + H2], att_w2, s_w)
                load(b2_col[p:p + H2, :], col(att_b2), s_w)
                load(wo_col[p:p + H2, :], att_wo, s_w)

            for i in range(TK // KB):
                act.wait_ge(s_cT, i + 1)
                if i >= 2:
                    act.wait_ge(s_gps, i - 1)
                act.activation(genre_cntT[:, i % 2, :], ps_ent[i % 2][0:KB * VOCAB, 0:TP],
                               ACT.Copy).then_inc(s_cTc, 1)

            for h in range(2):
                load(m1_sb[:, h, :], mlp_w1[h * D:(h + 1) * D, :], s_mlpw)
                load(m2_sb[:, h, :], mlp_w2[h * MH:(h + 1) * MH, :], s_mlpw)
                for c, v in enumerate((mlp_b1, bn1_g, bn1_b)):
                    load(bnp1[:, c, h:h + 1], col(v[h * MH:(h + 1) * MH]), s_mlpw)
            for c, v in enumerate((mlp_b2, bn2_g, bn2_b)):
                load(bnp2[:, c:c + 1], col(v), s_mlpw)
            load(ow_sb[:, :], out_w, s_mlpw)
            load(ob_sb[:, :], out_b.rearrange("(o h) -> o h", o=1).broadcast_to([128, 2]), s_mlpw)

            for b in range(TILES * USERS // 4):
                t, u = divmod(4 * b, USERS)
                act.wait_ge(s_adsps, b + 1)
                act.activation(adsT[:, u:u + 4, t * 128:(t + 1) * 128],
                               ps_ent[b % 2][:, :].rearrange("p (u g) -> p u g", u=4), ACT.Copy).then_inc(s_adsT, 1)
                act.wait_ge(s_tcv, 2 * b + 2)
                if b >= 2:
                    act.wait_ge(s_tcout[b % 2], 16 * (b // 2))
                act.activation(tc_parts[:, b % 2, :, 0, :], tc_val[:, b % 2, :, :],
                               ACT.Copy).then_inc(s_tchi, 1)
                act.wait_ge(s_tcr, 2 * b + 1)
                act.activation(tc_parts[:, b % 2, :, 1, :], tc_res[:, b % 2, :, :],
                               ACT.Copy).then_inc(s_tchi, 1)
                act.wait_ge(s_tcr, 2 * b + 2)
                act.activation(tc_parts[:, b % 2, :, 2, :], tc_val[:, b % 2, :, :],
                               ACT.Copy).then_inc(s_tcp, 1)

            act.wait_ge(s_flag, 1)
            general = act.value_load(flag_i[0:1, 0:1], min_val=0, max_val=GROUPS)

            def step_act(s):
                if s.has(0):
                    u = s.unit(0)
                    q = u.slot % 2
                    act.wait_ge(s_T, u.n + 1)
                    if u.after(2):
                        act.wait_ge(s_1, u.n - 1)
                    act.activation(entT[:, q, :], ps_ent[q][:, 0:UNIT], ACT.Copy).then_inc(s_cp, 1)
                if s.has(1):
                    u = s.unit(1)
                    q = u.slot % 2
                    act.wait_ge(s_1, u.n + 1)
                    if u.after(2):
                        act.wait_ge(s_a1, u.n - 1)
                    act.activation(neg1[:, q, :], ps_h1[q][0:H1, 0:UNIT], ACT.Relu,
                                   scale=-1.0).then_inc(s_n, 1)
                if s.has(2):
                    u = s.unit(2)
                    q = u.slot % 2
                    act.wait_ge(s_2, u.n + 1)
                    if u.after(2):
                        act.wait_ge(s_at, u.n - 1)
                    act.activation(act2[:, q, :], ps_h2[0:H2X, 0:UNIT], ACT.Relu,
                                   bias=b2_col[:, 0:1]).then_inc(s_a2, 1)

            act.wait_ge(s_w, 16 * N_W)
            act.wait_ge(s_wsc, 5)
            run_pass(act, step_act, GROUPS, 0, 2)
            with act.If(general > 0):
                with act.Fori(1, PASSES) as p:
                    run_pass(act, step_act, GROUPS, p * (GROUPS // RING), 2)
            with act.Else():
                act.nop()

            act.wait_ge(s_mlpw, 16 * 15)
            banks = [ps_ent[0], ps_ent[1], ps_h1[0], ps_h1[1]]
            for i in range(2 * NCH):
                h, c = divmod(i, NCH)
                act.wait_ge(s_m1, i + 1)
                act.activation(z1[:, h, c * CH:(c + 1) * CH], banks[i % 4][0:MH, :], ACT.Identity,
                               bias=bnp1[:, 0, h:h + 1]).then_inc(s_m1c, 1)
            act.wait_ge(s_v1, 1)
            act.activation(bnv[0:MH, 0:2, 1], bnv[0:MH, 0:2, 0], ACT.Sqrt).then_inc(s_sq1, 1)
            act.wait_ge(s_bn1, 1)
            for c in range(NCH):
                for h in range(2):
                    act.activation(z1n[:, h, c * CH:(c + 1) * CH], z1[:, h, c * CH:(c + 1) * CH],
                                   ACT.Relu, bias=bnv[0:MH, h, 7:8], scale=bnv[0:MH, h, 6:7]
                                   ).then_inc(s_n1, 1)
            for c in range(NCH):
                act.wait_ge(s_m2, c + 1)
                act.activation(z2[:, c * CH:(c + 1) * CH], banks[c][0:M2, :], ACT.Identity,
                               bias=bnp2[:, 0:1]).then_inc(s_m2c, 1)
            act.wait_ge(s_v2, 1)
            act.activation(bnv[0:M2, 2:3, 1], bnv[0:M2, 2:3, 0], ACT.Sqrt).then_inc(s_sq2, 1)
            act.wait_ge(s_bn2, 1)
            for c in range(NCH):
                act.activation(z2n[:, c * CH:(c + 1) * CH], z2[:, c * CH:(c + 1) * CH],
                               ACT.Relu, bias=bnv[0:M2, 2, 7:8], scale=bnv[0:M2, 2, 6:7]
                               ).then_inc(s_n2, 1)
            act.wait_ge(s_sh, 3)
            act.activation(probs[:, :, :], probs[:, :, :], ACT.Exp).then_inc(s_ex, 1)

        @block.tensor
        def _(pe):
            pe.wait_ge(s_const, N_CONST)

            pe.wait_ge(s_flag_ps, 1)
            nc.tensor.matmul(ps_att[0:1, 0:1], flag_col[:, :], ones_col[:, :],
                             start=True, stop=True).then_inc(s_segT, 1)
            pe.wait_ge(s_seg, 1)
            for t in range(TILES):
                for w in range(2):
                    c = w * GROUPS + t * 128
                    mm = nc.tensor.transpose(ps_tgt[0:USERS * PARTS, c:c + 128],
                                             rep_sb[:, t, w, :, :].rearrange("p u s -> p (u s)"),
                                             ident[:, :])
            mm.then_inc(s_segT, 1)

            pe.wait_ge(s_cnt, 1)
            pe.wait_ge(s_blocks, 16 * KB)

            def turn_counts(i):
                if i >= 2:
                    pe.wait_ge(s_cTc, i - 1)
                nc.tensor.transpose(ps_ent[i % 2][0:KB * VOCAB, 0:TP],
                                    genre_cnt[:, i * KB:(i + 1) * KB, :].rearrange("p k v -> p (k v)"),
                                    ident[0:TP, 0:TP]).then_inc(s_cT, 1)

            turn_counts(0)
            for i in range(TK // KB):
                if i + 1 < TK // KB:
                    turn_counts(i + 1)
                pe.wait_ge(s_cTc, i + 1)
                if i >= 2:
                    pe.wait_ge(s_gev, i - 1)
                nc.tensor.matmul(ps_h1[i % 2][0:TP, 0:KB * E], genre_cntT[:, i % 2, :],
                                 genre_blocks[:, :], start=True, stop=True).then_inc(s_gps, 1)

            pe.wait_ge(s_w, 16 * N_W)
            pe.wait_ge(s_gev, TK // KB)
            for b in range(TILES * USERS // 4):
                t, u = divmod(4 * b, USERS)
                pe.wait_ge(s_ads, 16 * TILES * USERS)
                for i in range(4):
                    mm = nc.tensor.transpose(ps_ent[b % 2][:, i * 128:(i + 1) * 128],
                                             ads_rows[:, t, u + i, :], ident[:, :])
                mm.then_inc(s_adsps, 1)
                pe.wait_ge(s_adsT, b + 1)
                if b >= 2:
                    pe.wait_ge(s_tcv, 2 * (b - 1))
                for i in range(4):
                    dst = ps_h1[b % 2][:, i * H1:(i + 1) * H1]
                    nc.tensor.matmul(dst, adsT[:, u + i, t * 128:(t + 1) * 128], w1_sb[:, 1, :], start=True, stop=False)
                    mm = nc.tensor.matmul(dst, ones_row[:, :], b1_row[:, :], start=False, stop=True)
                mm.then_inc(s_cps, 1)

            pe.wait_ge(s_tcv, 2 * (TILES * USERS // 4))
            pe.wait_ge(s_segrow, 1)
            pe.wait_ge(s_wsc, 5)
            pe.wait_ge(s_flag, 1)
            general = pe.value_load(flag_i[0:1, 0:1], min_val=0, max_val=GROUPS)

            def step_pe(s):
                if s.has(0):
                    u = s.unit(0)
                    q = u.slot % 2
                    pe.wait_ge(s_g[u.slot], 16 * UNIT_TILES * (u.turn + 1))
                    if u.after(2):
                        pe.wait_ge(s_cp, u.n - 1)
                    for k in range(UNIT_TILES):
                        mm = nc.tensor.transpose(ps_ent[q][:, k * 128:(k + 1) * 128],
                                                 entries[:, u.slot, k, :], ident[:, :])
                    mm.then_inc(s_T, 1)
                    pe.wait_ge(s_tc[u.slot], 16 * (u.turn + 1))
                    pe.wait_ge(s_oh, u.n + 1)
                    if u.after(1):
                        pe.wait_ge(s_pr, u.n)
                    nc.tensor.matmul(ps_tgt[:, 0:UNIT], tc_ring[:, u.slot, 0:D], user_of[:, q, :],
                                     start=True, stop=True).then_inc(s_tg, 1)
                if s.has(1):
                    u = s.unit(1)
                    q = u.slot % 2
                    dst = ps_h1[q][0:H1, 0:UNIT]
                    pe.wait_ge(s_cp, u.n + 1)
                    if u.after(2):
                        pe.wait_ge(s_a1, u.n - 1)
                    nc.tensor.matmul(dst, w1_sb[:, 0, :], entT[:, q, :], start=True, stop=False)
                    nc.tensor.matmul(dst, tc_ring[:, u.slot, D:TC], user_of[:, q, :],
                                     start=False, stop=False)
                    pe.wait_ge(s_pr, u.n + 1)
                    nc.tensor.matmul(dst, w1_sb[:, 2, :], prodT[:, q, :],
                                     start=False, stop=True).then_inc(s_1, 1)
                if s.has(2):
                    u = s.unit(2)
                    q = u.slot % 2
                    pe.wait_ge(s_a1, u.n + 1)
                    if u.after(1):
                        pe.wait_ge(s_a2, u.n)
                    nc.tensor.matmul(ps_h2[0:H2X, 0:UNIT], w2_sb[:, :], act1[:, q, :],
                                     start=True, stop=True).then_inc(s_2, 1)
                if s.has(3):
                    u = s.unit(3)
                    q = u.slot % 2
                    pe.wait_ge(s_a2, u.n + 1)
                    if u.after(1):
                        pe.wait_ge(s_aw, u.n)
                    for k in range(UNIT_TILES):
                        mm = nc.tensor.matmul(ps_att[:, k:k + 1], act2[:, q, k * 128:(k + 1) * 128],
                                              wo_col[:, :], start=True, stop=True)
                    mm.then_inc(s_at, 1)
                if s.has(4):
                    u = s.unit(4)
                    q = u.slot % 2
                    pe.wait_ge(s_aw, u.n + 1)
                    if u.after(1):
                        pe.wait_ge(s_pa, u.n)
                    for k in range(UNIT_TILES):
                        mm = nc.tensor.matmul(ps_pool[:, 0:USERS], entries[:, u.slot, k, :],
                                              att_w[:, q, k, :], start=(k == 0),
                                              stop=(k == UNIT_TILES - 1))
                    mm.then_inc(s_pl, 1)

            run_pass(pe, step_pe, GROUPS, 0, 4)
            with pe.If(general > 0):
                with pe.Fori(1, PASSES) as p:
                    run_pass(pe, step_pe, GROUPS, p * (GROUPS // RING), 4)
            with pe.Else():
                pe.nop()

            pe.wait_ge(s_mlpw, 16 * 15)
            pe.wait_ge(s_main_dve, 1)
            pooled_v = pooledT[:, :, :].rearrange("p u g -> p (u g)")
            ads_v = adsT[:, :, :].rearrange("p u g -> p (u g)")
            banks = [ps_ent[0], ps_ent[1], ps_h1[0], ps_h1[1]]
            for i in range(2 * NCH):
                h, c = divmod(i, NCH)
                if i >= 4:
                    pe.wait_ge(s_m1c, i - 3)
                dst = banks[i % 4][0:MH, :]
                nc.tensor.matmul(dst, m1_sb[:, 1, h * MH:(h + 1) * MH], ads_v[:, c * CH:(c + 1) * CH],
                                 start=True, stop=False)
                nc.tensor.matmul(dst, m1_sb[:, 0, h * MH:(h + 1) * MH], pooled_v[:, c * CH:(c + 1) * CH],
                                 start=False, stop=True).then_inc(s_m1, 1)
            for c in range(NCH):
                pe.wait_ge(s_m1c, 2 * NCH)
                pe.wait_ge(s_z1, 2 * (c + 1))
                for h in range(2):
                    mm = nc.tensor.matmul(banks[c][0:M2, :], m2_sb[:, h, :], z1[:, h, c * CH:(c + 1) * CH],
                                          start=(h == 0), stop=(h == 1))
                mm.then_inc(s_m2, 1)
            for c in range(NCH):
                pe.wait_ge(s_z2, c + 1)
                for i in range(4):
                    j = 4 * c + i
                    u, t = divmod(j, TILES)
                    at = 2 * (t * USERS + u)
                    mm = nc.tensor.matmul(ps_att[:, at:at + 2], z2[:, j * 128:(j + 1) * 128],
                                          ow_sb[:, :], start=True, stop=True)
            mm.then_inc(s_lg, 1)

        @block.vector
        def _(dve):
            V = nc.vector
            steps = [0]

            def link(ins):
                steps[0] += 1
                ins.then_inc(s_d, 1)
                dve.wait_ge(s_d, steps[0])

            def row_numbers(dst, raw, tmp, n):
                link(V.tensor_scalar(tmp, raw, 0.0, float(n), ALU.is_lt, ALU.mult))
                link(V.tensor_tensor(tmp, tmp, raw, ALU.add))
                link(V.tensor_scalar(dst, tmp, 0.0, float(n - 1), ALU.max, ALU.min))

            dve.wait_ge(s_feat, 16)
            movies = feat_sb[:, :, 0]
            row_numbers(movie_idx[:, :], movies, feat_f[:, 0, :, 0], N_ROWS)
            dve.sem_inc(s_movie, 1)

            dve.wait_ge(s_rows, 16 * TILES)
            flat = "p u c -> p (u c)"
            for t in range(TILES):
                key = key_sb[:, t].rearrange(flat)
                row_numbers(idx_sb[:, t].rearrange(flat), rows_sb[:, t].rearrange(flat), key, N_ROWS)
                dve.sem_inc(s_idx, 1)
                link(V.tensor_scalar(key, idx_sb[:, t].rearrange(flat), -1.0, float(LAST_ROW),
                                     ALU.mult, ALU.add))
                ones = rows_sb[:, t].rearrange(flat).bitcast(F32)
                link(V.tensor_scalar(ones, key, 1.0, None, ALU.min))
                link(V.tensor_reduce(count[:, t, :],
                                     rows_sb[:, t, :, 1:1 + T].bitcast(F32), AX_X, ALU.add))

            link(V.memset(start9[:, :, 0:1], 0.0))
            length = small[:, 0]
            link(V.tensor_scalar(length, count[:, :, :], 1.0, None, ALU.add))
            for u in range(USERS):
                link(V.tensor_tensor(start9[:, :, u + 1], start9[:, :, u], length[:, :, u], ALU.add))
            starts, ends, extra = (seg_sb[:, :, i, :] for i in range(3))
            link(V.tensor_copy(starts, start9[:, :, 0:USERS]))
            link(V.tensor_copy(ends, start9[:, :, 1:USERS + 1]))
            link(V.tensor_scalar(extra, count[:, :, :], -1.0, float(T - 1), ALU.mult, ALU.add))
            over = small[:, 1]
            link(V.tensor_scalar(over, ends, float(UNIT), None, ALU.is_gt))
            link(V.tensor_scalar(small[:, 2], length, float(RUN), None, ALU.is_gt))
            link(V.tensor_tensor(over, over, small[:, 2], ALU.max))
            link(V.tensor_reduce(flag_col[:, :], over.rearrange("p t u -> p (t u)"), AX_X, ALU.max))
            dve.sem_inc(s_flag_ps, 1)
            dve.wait_ge(s_const, N_CONST)
            link(V.tensor_scalar(small[:, 3], starts, float(UNIT), None, ALU.min))
            link(V.tensor_tensor(scatter_to[:, :, :], small[:, 3],
                                 group_base[:, :, :].broadcast_to([128, TILES, USERS]), ALU.add))
            dve.wait_ge(s_segT, 1)
            link(V.tensor_copy(flag_i[:, :], ps_att[0:1, 0:1]))
            dve.sem_inc(s_flag, 1)
            general = dve.value_load(flag_i[0:1, 0:1], min_val=0, max_val=GROUPS)
            base = steps[0]
            with dve.If(general > 0):
                for t in range(TILES):
                    V.tensor_copy(seg_sb[:, t, 0, :], plain_start[:, :]).then_inc(s_d, 1)
                    V.tensor_scalar(seg_sb[:, t, 1, :], plain_start[:, :], float(T), None,
                                    ALU.add).then_inc(s_d, 1)
                    V.memset(seg_sb[:, t, 2, :], 0.0).then_inc(s_d, 1)
            with dve.Else():
                dve.sem_inc(s_d, 3 * TILES)
            steps[0] = base + 3 * TILES
            dve.wait_ge(s_d, steps[0])
            for t in range(TILES):
                for w in range(2):
                    link(V.tensor_copy(rep_sb[:, t, w, :, :],
                                       seg_sb[:, t, w, :].rearrange("p (u o) -> p u o", o=1)
                                       .broadcast_to([128, USERS, PARTS])))
            dve.sem_inc(s_seg, 1)

            row_numbers(genre_bf[:, :, :].rearrange("p j k -> p k j"), feat_sb[:, :, 1:FEATS],
                        feat_f[:, 0, :, 1:FEATS], VOCAB)
            for half in range(2):
                for v in range(VOCAB // 2):
                    ins = V.tensor_scalar(genre_is[:, v, :, :], genre_bf[:, :, :],
                                          float(half * VOCAB // 2 + v), None, ALU.is_equal)
                    ins.then_inc(s_d, 1)
                steps[0] += VOCAB // 2
                dve.wait_ge(s_d, steps[0])
                for j in range(1, GENRES - 1):
                    link(V.tensor_tensor(genre_is[:, :, 0, :], genre_is[:, :, 0, :],
                                         genre_is[:, :, j, :], ALU.add))
                link(V.tensor_tensor(
                    genre_cnt[:, :, half * (VOCAB // 2):(half + 1) * (VOCAB // 2)]
                    .rearrange("p k v -> p v k"),
                    genre_is[:, :, 0, :], genre_is[:, :, GENRES - 1, :], ALU.add))
            dve.sem_inc(s_cnt, 1)
            link(V.tensor_scalar(feat_f[:, 1, :, 1:FEATS], feat_sb[:, :, 1:FEATS], 0.0, None, ALU.is_gt))
            link(V.tensor_reduce(genre_len[:, 0, :], feat_f[:, 1, :, 1:FEATS], AX_X, ALU.add))
            link(V.tensor_scalar(genre_len[:, 0, :], genre_len[:, 0, :], POOL_EPS, None, ALU.add))
            link(V.reciprocal(genre_len[:, 1, :], genre_len[:, 0, :]))
            dve.wait_ge(s_segT, 2)
            link(V.tensor_copy(seg_rows[:, :, :].rearrange("p w g -> p (w g)"),
                               ps_tgt[0:USERS * PARTS, 0:2 * TILES * 128]))
            dve.sem_inc(s_segrow, 1)

            dve.wait_ge(s_w, 16 * N_W)
            V.tensor_scalar(w2_sb[:, UPPER:H2X], w2_sb[:, UPPER:H2X], -1.0, None, ALU.mult).then_inc(s_wsc, 1)
            V.tensor_scalar(b2_col[UPPER:H2X, :], b2_col[UPPER:H2X, :], -1.0, None, ALU.mult).then_inc(s_wsc, 1)
            V.tensor_scalar(wo_col[UPPER:H2X, :], wo_col[UPPER:H2X, :], scal[UPPER:H2X, A2:A2 + 1], -1.0,
                            ALU.mult, ALU.mult).then_inc(s_wsc, 1)
            V.tensor_scalar(scal[:, C1:C1 + 1], scal[:, A1:A1 + 1], -1.0, 1.0, ALU.mult, ALU.add).then_inc(s_wsc, 1)
            V.tensor_scalar(scal[:, CM1:CM2 + 1], scal[:, AM1:AM2 + 1], -1.0, 1.0,
                            ALU.mult, ALU.add).then_inc(s_wsc, 1)
            dve.wait_ge(s_wsc, 5)

            def write_genres(i):
                dve.wait_ge(s_gps, i + 1)
                V.tensor_tensor(table_sb[:, i * KB:(i + 1) * KB, E:D],
                                ps_h1[i % 2][0:TP, 0:KB * E].rearrange("p (k e) -> p k e", k=KB),
                                genre_len[:, 1, i * KB:(i + 1) * KB].rearrange("p (k o) -> p k o", o=1)
                                .broadcast_to([TP, KB, E]), ALU.mult).then_inc(s_gev, 1)

            for i in range(TK // KB):
                write_genres(i)

            for u in range(USERS):
                for r in range(RUN // 8):
                    for t in range(TILES):
                        src = work[:, t, :] if r else key_sb[:, t, u, 1:1 + T]
                        if r:
                            dve.wait_ge(s_d, steps[0] - TILES + 1)
                        V.max(best[:, t, 8 * r:8 * r + 8], src).then_inc(s_d, 1)
                        steps[0] += 1
                    if r < RUN // 8 - 1:
                        for t in range(TILES):
                            src = work[:, t, :] if r else key_sb[:, t, u, 1:1 + T]
                            dve.wait_ge(s_d, steps[0] - TILES + 1)
                            V.match_replace(work[:, t, :], best[:, t, 8 * r:8 * r + 8], src,
                                            -1.0).then_inc(s_d, 1)
                            steps[0] += 1
                dve.wait_ge(s_d, steps[0])
                for t in range(TILES):
                    V.tensor_scalar(run_idx[:, t, u, :], best[:, t, :], -1.0, float(LAST_ROW),
                                    ALU.mult, ALU.add).then_inc(s_runs, 1)
                dve.wait_ge(s_runs, TILES * (u + 1))

            dve.wait_ge(s_ads, 16 * TILES * USERS)
            for b in range(TILES * USERS // 4):
                t, u = divmod(4 * b, USERS)
                if b >= 2:
                    dve.wait_ge(s_tcp, b - 1)
                V.tensor_copy(tc_val[:, b % 2, :, 0:D], ads_rows[:, t, u:u + 4, :]).then_inc(s_tcv, 1)
                dve.wait_ge(s_cps, b + 1)
                V.tensor_copy(tc_val[:, b % 2, :, D:TC],
                              ps_h1[b % 2][:, 0:4 * H1].rearrange("p (u h) -> p u h", u=4)).then_inc(s_tcv, 1)
                dve.wait_ge(s_tcv, 2 * b + 2)
                dve.wait_ge(s_tchi, 2 * b + 1)
                V.tensor_tensor(tc_res[:, b % 2], tc_val[:, b % 2], tc_parts[:, b % 2, :, 0, :],
                                ALU.subtract).then_inc(s_tcr, 1)
                dve.wait_ge(s_tchi, 2 * b + 2)
                V.tensor_tensor(tc_val[:, b % 2], tc_res[:, b % 2], tc_parts[:, b % 2, :, 1, :],
                                ALU.subtract).then_inc(s_tcr, 1)

            WT_STEPS = 6

            def entry_weights(u):
                half = u.slot // 4
                g = seg_all[:, columns(u.group, 4), :, :]
                done = WT_STEPS * (2 * u.turn + half)
                shape = [128, 4, UNIT_TILES, USERS]
                start, end, extra = (g[:, :, i:i + 1, :].broadcast_to(shape) for i in range(3))
                pos, next_pos = (pos_col[:, i, :].rearrange("p (a k b) -> p a k b", a=1, b=1)
                                 .broadcast_to(shape) for i in range(2))
                if u.after(4):
                    dve.wait_ge(s_wt, done)
                V.tensor_tensor(wt_tmp[:, 0], pos, start, ALU.is_ge).then_inc(s_wt, 1)
                V.tensor_tensor(wt_tmp[:, 1], pos, end, ALU.is_ge).then_inc(s_wt, 1)
                V.tensor_tensor(wt_tmp[:, 2], next_pos, end, ALU.is_equal).then_inc(s_wt, 1)
                dve.wait_ge(s_wt, done + 3)
                V.tensor_tensor(wt_tmp[:, 0], wt_tmp[:, 0], wt_tmp[:, 1], ALU.subtract).then_inc(s_wt, 1)
                V.tensor_tensor(wt_tmp[:, 2], wt_tmp[:, 2], extra, ALU.mult).then_inc(s_wt, 1)
                dve.wait_ge(s_wt, done + 5)
                if u.after(8):
                    dve.wait_ge(s_aw, u.n - 4)
                V.tensor_tensor(wts[:, half], wt_tmp[:, 0], wt_tmp[:, 2], ALU.add).then_inc(s_wt, 1)

            pos_flat = pos_row[:, :, :].rearrange("p k e -> p (k e)")

            def step_dve(s):
                if s.has(0):
                    u = s.unit(0)
                    q = u.slot % 2
                    if u.slot % 4 == 0:
                        entry_weights(u)
                    if u.after(2):
                        dve.wait_ge(s_oh, u.n - 1)
                    V.tensor_scalar(past_end[:, q, :], pos_flat, seg_rows[:, 1, columns(u.group, 1)],
                                    None, ALU.is_ge).then_inc(s_oh_t, 1)
                    dve.wait_ge(s_oh_t, u.n + 1)
                    if u.after(2):
                        dve.wait_ge(s_1, u.n - 1)
                    V.scalar_tensor_tensor(user_of[:, q, :], pos_flat,
                                           seg_rows[:, 0, columns(u.group, 1)], past_end[:, q, :],
                                           ALU.is_ge, ALU.subtract).then_inc(s_oh, 1)
                if s.has(1):
                    u = s.unit(1)
                    q = u.slot % 2
                    dve.wait_ge(s_cp, u.n + 1)
                    dve.wait_ge(s_tg, u.n + 1)
                    if u.after(2):
                        dve.wait_ge(s_1, u.n - 1)
                    V.tensor_tensor(prodT[:, q, :], entT[:, q, :], ps_tgt[:, 0:UNIT],
                                    ALU.mult).then_inc(s_pr, 1)
                if s.has(2):
                    u = s.unit(2)
                    q = u.slot % 2
                    dve.wait_ge(s_n, u.n + 1)
                    if u.after(2):
                        dve.wait_ge(s_2, u.n - 1)
                    V.scalar_tensor_tensor(act1[:, q, :], neg1[:, q, :], scal[0:H1, C1:C1 + 1],
                                           ps_h1[q][0:H1, 0:UNIT], ALU.mult, ALU.add).then_inc(s_a1, 1)
                if s.has(4):
                    u = s.unit(4)
                    q = u.slot % 2
                    dve.wait_ge(s_at, u.n + 1)
                    dve.wait_ge(s_wt, WT_STEPS * (2 * u.turn + u.slot // 4 + 1))
                    if u.after(2):
                        dve.wait_ge(s_pl, u.n - 1)
                    V.scalar_tensor_tensor(
                        att_w[:, q], ps_att[:, 0:UNIT_TILES].rearrange("p (k o) -> p k o", o=1)
                        .broadcast_to([128, UNIT_TILES, USERS]), scal[:, BO:BO + 1],
                        wts[:, u.slot // 4, u.slot % 4], ALU.add, ALU.mult).then_inc(s_aw, 1)
                if s.has(5):
                    u = s.unit(5)
                    dve.wait_ge(s_pl, u.n + 1)
                    dst = pooledT[:, :, columns(u.group, 1)]
                    V.tensor_tensor(dst, dst, ps_pool[:, 0:USERS].rearrange("p (u o) -> p u o", o=1),
                                    ALU.add).then_inc(s_pa, 1)

            dve.wait_ge(s_segin, 16)
            link(V.tensor_copy(pos_col[:, 0, :], pos_init[:, :]))
            link(V.tensor_scalar(pos_col[:, 1, :], pos_col[:, 0, :], 1.0, None, ALU.add))
            run_pass(dve, step_dve, GROUPS, 0, 5)
            with dve.If(general > 0):
                with dve.Fori(1, PASSES) as p:
                    dve.wait_ge(s_pa, GROUPS * p)
                    V.tensor_scalar(pos_col[:, :, :], pos_col[:, :, :], float(UNIT), None,
                                    ALU.add).then_inc(s_pos, 1)
                    V.tensor_scalar(pos_row[:, :, :], pos_row[:, :, :], float(UNIT), None,
                                    ALU.add).then_inc(s_pos, 1)
                    dve.wait_ge(s_pos, 2 * p)
                    run_pass(dve, step_dve, GROUPS, p * (GROUPS // RING), 5)
                dve.wait_ge(s_pa, GROUPS * PASSES)
            with dve.Else():
                dve.wait_ge(s_pa, GROUPS)
            dve.sem_inc(s_main_dve, 1)

            def norm(P, cols, bnp, var_ready, root_ready, bn_ready):
                v = bnv[0:P, cols, :]
                link(V.tensor_scalar(v[:, :, 0], aggr[0:P, cols, 1], BN_EPS, None, ALU.add))
                dve.sem_inc(var_ready, 1)
                dve.wait_ge(root_ready, 1)
                link(V.reciprocal(v[:, :, 2], v[:, :, 1]))
                link(V.tensor_tensor(v[:, :, 3], v[:, :, 2], v[:, :, 2], ALU.mult))
                link(V.tensor_tensor(v[:, :, 3], v[:, :, 3], v[:, :, 0], ALU.mult))
                link(V.tensor_scalar(v[:, :, 3], v[:, :, 3], -0.5, 1.5, ALU.mult, ALU.add))
                link(V.tensor_tensor(v[:, :, 3], v[:, :, 3], v[:, :, 2], ALU.mult))
                link(V.tensor_tensor(v[:, :, 4], v[:, :, 3], bnp[:, 1], ALU.mult))
                link(V.tensor_tensor(v[:, :, 3], v[:, :, 4], aggr[0:P, cols, 0], ALU.mult))
                link(V.tensor_tensor(v[:, :, 5], bnp[:, 2], v[:, :, 3], ALU.subtract))
                link(V.tensor_scalar(v[:, :, 6:8], v[:, :, 4:6], -1.0, None, ALU.mult))
                dve.sem_inc(bn_ready, 1)

            dve.wait_ge(s_mlpw, 16 * 15)
            for i in range(2 * NCH):
                h, c = divmod(i, NCH)
                dve.wait_ge(s_m1c, i + 1)
                V.bn_stats(stats[0:MH, h, c, :], z1[:, h, c * CH:(c + 1) * CH]).then_inc(s_d, 1)
            steps[0] += 2 * NCH
            dve.wait_ge(s_d, steps[0])
            for h in range(2):
                link(V.bn_aggr(aggr[0:MH, h, :], stats[0:MH, h, :, :].rearrange("p c s -> p (c s)")))
            norm(MH, slice(0, 2), bnp1[:, :, :], s_v1, s_sq1, s_bn1)
            for c in range(NCH):
                for h in range(2):
                    z = z1[:, h, c * CH:(c + 1) * CH]
                    dve.wait_ge(s_n1, 2 * c + h + 1)
                    link(V.tensor_scalar(z, z, bnv[0:MH, h, 4:5], bnv[0:MH, h, 5:6], ALU.mult, ALU.add))
                    V.scalar_tensor_tensor(z, z1n[:, h, c * CH:(c + 1) * CH], scal[0:MH, CM1:CM1 + 1],
                                           z, ALU.mult, ALU.add).then_inc(s_z1, 1)
            for c in range(NCH):
                dve.wait_ge(s_m2c, c + 1)
                V.bn_stats(stats[0:M2, 2, c, :], z2[:, c * CH:(c + 1) * CH]).then_inc(s_d, 1)
            steps[0] += NCH
            dve.wait_ge(s_d, steps[0])
            link(V.bn_aggr(aggr[0:M2, 2, :], stats[0:M2, 2, :, :].rearrange("p c s -> p (c s)")))
            norm(M2, slice(2, 3), bnp2[:, :].rearrange("p (c o) -> p c o", o=1), s_v2, s_sq2, s_bn2)
            for c in range(NCH):
                z = z2[:, c * CH:(c + 1) * CH]
                dve.wait_ge(s_n2, c + 1)
                link(V.tensor_scalar(z, z, bnv[0:M2, 2, 4:5], bnv[0:M2, 2, 5:6], ALU.mult, ALU.add))
                V.scalar_tensor_tensor(z, z2n[:, c * CH:(c + 1) * CH], scal[0:M2, CM2:CM2 + 1],
                                       z, ALU.mult, ALU.add).then_inc(s_z2, 1)
            dve.wait_ge(s_lg, 1)
            K = TILES * USERS
            V.tensor_tensor(probs[:, :, :], ps_att[:, 0:2 * K].rearrange("p (k c) -> p k c", c=2),
                            ob_sb[:, :].rearrange("p (o c) -> p o c", o=1).broadcast_to([128, K, 2]),
                            ALU.add).then_inc(s_sh, 1)
            dve.wait_ge(s_sh, 1)
            V.tensor_tensor(lmax[:, 0, :], probs[:, :, 0], probs[:, :, 1], ALU.max).then_inc(s_sh, 1)
            dve.wait_ge(s_sh, 2)
            V.tensor_tensor(probs[:, :, :], probs[:, :, :],
                            lmax[:, 0, :].rearrange("p (k o) -> p k o", o=1).broadcast_to([128, K, 2]),
                            ALU.subtract).then_inc(s_sh, 1)
            dve.wait_ge(s_ex, 1)
            link(V.tensor_tensor(lmax[:, 0, :], probs[:, :, 0], probs[:, :, 1], ALU.add))
            link(V.reciprocal(lmax[:, 1, :], lmax[:, 0, :]))
            V.tensor_tensor(probs[:, :, :], probs[:, :, :],
                            lmax[:, 1, :].rearrange("p (k o) -> p k o", o=1).broadcast_to([128, K, 2]),
                            ALU.mult).then_inc(s_pb, 1)


_INS = ['r_rowData', 'L0_rec_movieFeature', 'L0_rec_emb_movie', 'L0_rec_emb_genre',
        'L0_rec_att_w1', 'L0_rec_att_b1', 'L0_rec_att_a1', 'L0_rec_att_w2', 'L0_rec_att_b2',
        'L0_rec_att_a2', 'L0_rec_att_wo', 'L0_rec_att_bo', 'L0_rec_mlp_w1', 'L0_rec_mlp_b1',
        'L0_rec_bn1_g', 'L0_rec_bn1_b', 'L0_rec_mlp_a1', 'L0_rec_mlp_w2', 'L0_rec_mlp_b2',
        'L0_rec_bn2_g', 'L0_rec_bn2_b', 'L0_rec_mlp_a2', 'L0_rec_out_w', 'L0_rec_out_b']


def kernel(**inputs):
    import numpy as np
    import concourse.bacc as bacc
    from concourse.bass_utils import run_bass_kernel_spmd

    nc = bacc.Bacc("TRN2", target_bir_lowering=False, num_devices=1)
    arrays, args = {}, []
    for name in _INS:
        a = np.ascontiguousarray(inputs[name])
        if a.ndim == 0:
            a = a.reshape(1)
        arrays[f"in_{name}"] = a
        args.append(nc.dram_tensor(f"in_{name}", a.shape, mybir.dt.from_np(a.dtype),
                                   kind="ExternalInput").ap())
    out = nc.dram_tensor("out_0", (inputs['r_rowData'].shape[0], 2), F32, kind="ExternalOutput").ap()
    build(nc, *args, out)
    r = run_bass_kernel_spmd(nc, [arrays], core_ids=[0])
    return r.results[0]["out_0"]
```

```python
from contextlib import ExitStack

import concourse.bass as bass
from concourse import mybir
from concourse.alu_op_type import AluOpType as ALU

ACT = mybir.ActivationFunctionType
F32 = mybir.dt.float32
BF16 = mybir.dt.bfloat16
F16 = mybir.dt.float16
I32 = mybir.dt.int32
U32 = mybir.dt.uint32
AX_X = mybir.AxisListType.X

USERS = 8
PARTS = 3
UNIT_TILES = 3
TILE = 124
UNIT = TILE * UNIT_TILES
FETCH = 128 * UNIT_TILES
RUN = 64
DEEP = 4
RING = 8
BN_EPS = 1e-5
POOL_EPS = 1e-8


class Step:

    def __init__(self, block, slot, first_block, last):
        self.block, self.slot, self.first_block, self.last = block, slot, first_block, last

    def has(self, lag):
        if not isinstance(self.block, int):
            return True
        return 0 <= RING * self.block + self.slot - lag < self.last

    def unit(self, lag):
        return Unit(self.block - (self.slot < lag), (self.slot - lag) % RING, self.first_block)


class Unit:

    def __init__(self, block, slot, first_block):
        self.slot = slot
        self.group = RING * block + slot
        self.turn = block + first_block
        self.n = RING * self.turn + slot

    def after(self, depth):
        return not isinstance(self.n, int) or self.n >= depth


def columns(first, n):
    return slice(first, first + n) if isinstance(first, int) else bass.ds(first, n)


def run_pass(eng, step, groups, first_block, lag):
    run_steps(eng, step, groups, first_block)
    for s in range(lag):
        step(Step(groups // RING, s, first_block, groups))


def run_steps(eng, step, groups, first_block):
    for s in range(RING):
        step(Step(0, s, first_block, groups))
    with eng.Fori(1, groups // RING) as block:
        for s in range(RING):
            step(Step(block, s, first_block, groups))


def build(nc, rows, movie_feature, emb_movie, emb_genre, att_w1, att_b1, att_a1, att_w2, att_b2,
          att_a2, att_wo, att_bo, mlp_w1, mlp_b1, bn1_g, bn1_b, mlp_a1, mlp_w2, mlp_b2, bn2_g,
          bn2_b, mlp_a2, out_w, out_b, out):
    B, NCOL = rows.shape
    T = NCOL - 2
    N_ROWS, FEATS = movie_feature.shape
    GENRES = FEATS - 1
    VOCAB, E = emb_genre.shape
    D = 2 * E
    H1, H2 = att_w2.shape
    M1, M2 = mlp_w2.shape
    GROUPS = B // USERS
    TILES = GROUPS // 128
    LAST_ROW = N_ROWS - 1
    PASSES = -(-USERS * T // UNIT)
    REGION = (PASSES - 1) * UNIT + FETCH
    ONE = H1
    LAYER2 = UNIT_TILES * H2
    BATCHES = TILES * 2
    SEG = 3 * USERS
    TP = 125
    TK = N_ROWS // TP
    KB = 5
    PIECE_ENDS = tuple(range(2 * KB, TK + 1, 2 * KB))
    MH = M1 // 2
    NCH = 4
    CH = B // NCH
    TC = D + H1
    assert B % (USERS * 128) == 0 and N_ROWS == TP * TK and D == 128 and PIECE_ENDS[-1] == TK

    list_dram = nc.dram_tensor("list_dram", [GROUPS * REGION, 1], U32, kind="Internal").ap()
    table_dram = nc.dram_tensor("table_dram", [N_ROWS, D], F32, kind="Internal").ap()
    seg_dram = nc.dram_tensor("seg_dram", [GROUPS, SEG], F32, kind="Internal").ap()
    tc_dram = nc.dram_tensor("tc_dram", [GROUPS, USERS * PARTS, TC], BF16, kind="Internal").ap()
    list_by_group = list_dram.rearrange("(g e) o -> g (e o)", e=REGION)

    def unit_list(group, chunk):
        return (list_by_group[columns(group, 1), columns(chunk * UNIT, FETCH)]
                .rearrange("g (p k) -> (g p) k", p=128))

    with ExitStack() as ctx:
        def sb(name, shape, dt=F32):
            return ctx.enter_context(nc.sbuf_tensor(name, shape, dt))

        def bank(name, shape=(128, 512), dt=F32):
            return ctx.enter_context(nc.psum_tensor(name, list(shape), dt))

        def sem(name):
            return ctx.enter_context(nc.semaphore(name))

        rows_sb = sb("rows_sb", [128, TILES, USERS, NCOL], I32)
        idx_sb = sb("idx_sb", [128, TILES, USERS, NCOL], U32)
        key_sb = sb("key_sb", [128, TILES, USERS, NCOL])
        work = sb("work", [128, TILES, T])
        best = sb("best", [128, TILES, RUN])
        run_idx = sb("run_idx", [128, TILES, USERS, RUN], U32)
        count = sb("count", [128, TILES, USERS])
        start9 = sb("start9", [128, TILES, USERS + 1])
        seg_sb = sb("seg_sb", [128, TILES, 3, USERS])
        rep_sb = sb("rep_sb", [128, TILES, 2, USERS, PARTS])
        seg_rows = sb("seg_rows", [USERS * PARTS, 2, GROUPS])
        seg_all = sb("seg_all", [128, GROUPS, 3, USERS])
        scatter_to = sb("scatter_to", [128, TILES, USERS], U32)
        small = sb("small", [128, 4, TILES, USERS])
        flag_col = sb("flag_col", [128, 1])
        flag_i = sb("flag_i", [1, 1], I32)
        group_base = sb("group_base", [128, TILES, 1], I32)
        plain_start = sb("plain_start", [128, USERS], I32)
        ident = sb("ident", [128, 128])
        ones_col = sb("ones_col", [128, 1])

        feat_sb = sb("feat_sb", [TP, TK, FEATS], I32)
        feat_f = sb("feat_f", [TP, 2, TK, FEATS])
        movie_idx = sb("movie_idx", [TP, TK], U32)
        genre_bf = sb("genre_bf", [TP, GENRES, TK], BF16)
        genre_whole = sb("genre_is", [128, VOCAB // 2, GENRES, TK], BF16)
        genre_is = genre_whole[0:TP]
        genre_cnt = sb("genre_cnt", [TP, TK, VOCAB])
        genre_cntT = sb("genre_cntT", [KB * VOCAB, 2, TP])
        genre_blocks = sb("genre_blocks", [KB * VOCAB, KB * E])
        genre_len = sb("genre_len", [TP, 2, TK])
        table_whole = sb("table_sb", [128, TK, D])
        table_sb = table_whole[0:TP]

        w1_sb = sb("w1_sb", [D, 3, H1])
        b1_bc = sb("b1_bc", [128, H1])
        w2_sb = sb("w2_sb", [H1 + 1, H2])
        wo_bc = sb("wo_bc", [128, H2])
        scal = sb("scal", [128, 9])
        A1, A2, AM1, AM2, BO, C1, C2, CM1, CM2 = range(9)

        adsT = sb("adsT", [D, USERS, GROUPS])

        idx_ring = sb("idx_ring", [128, RING, UNIT_TILES], U32)
        tc_ring = sb("tc_ring", [USERS * PARTS, RING, TC], BF16)
        entries = rows_sb[:, :, :, :].rearrange("p t u c -> p (t u c)").bitcast(F32)[
            :, 0:RING * UNIT_TILES * D].rearrange("p (r k d) -> p r k d", r=RING, k=UNIT_TILES)
        pos_row = sb("pos_row", [USERS * PARTS, UNIT_TILES, TILE], F16)
        pos_init = sb("pos_init", [128, UNIT_TILES])
        pos_col = sb("pos_col", [128, 2, UNIT_TILES])
        reached = sb("reached", [USERS * PARTS, 2, 2, UNIT], BF16)
        user_of = sb("user_of", [USERS * PARTS, DEEP, UNIT], BF16)
        wts = sb("wts", [128, 2, 4, UNIT_TILES, USERS])
        wt_tmp = sb("wt_tmp", [128, 3, 4, UNIT_TILES, USERS])
        two = [whole.bitcast(F32)[:, i * DEEP * UNIT:(i + 1) * DEEP * UNIT]
               .rearrange("p (r e) -> p r e", r=DEEP)
               for whole in (key_sb[:, :, :, :].rearrange("p t u c -> p (t u c)"),
                             genre_whole[:, :, :, :].rearrange("p v j k -> p (v j k)"))
               for i in range(2)]
        entT, prodT, neg1, act1 = two[0], two[1], two[2][0:H1], two[3][0:H1 + 1]
        neg2 = sb("neg2", [TILE, DEEP, LAYER2])
        act2 = sb("act2", [TILE, LAYER2])
        scaled2 = sb("scaled2", [TILE, LAYER2])
        att_sum = sb("att_sum", [TILE, UNIT_TILES])
        att_w = sb("att_w", [TILE, DEEP, UNIT_TILES, USERS])
        pooledT = sb("pooledT", [D, USERS, GROUPS])

        m1_sb = sb("m1_sb", [D, 2, M1])
        m2_sb = sb("m2_sb", [MH, 2, M2])
        bnp1 = sb("bnp1", [MH, 3, 2])
        bnp2 = sb("bnp2", [M2, 3])
        ow_sb = sb("ow_sb", [M2, 2])
        ob_sb = sb("ob_sb", [128, 2])
        stats = sb("stats", [128, 3, NCH, 6])
        aggr = sb("aggr", [128, 3, 2])
        bnv = sb("bnv", [128, 3, 8])
        probs = sb("probs", [128, TILES * USERS, 2])
        lmax = sb("lmax", [128, 2, TILES * USERS])
        arena = table_whole[:, :, :].rearrange("p k d -> p (k d)")
        sizes = [4 * BATCHES * TC, 4 * BATCHES * TC, 4 * BATCHES * PARTS * TC // 2]
        at = [sum(sizes[:i]) for i in range(4)]
        tc_val = arena[:, at[0]:at[1]].rearrange("p (b u c) -> p b u c", b=BATCHES, u=4)
        tc_res = arena[:, at[1]:at[2]].rearrange("p (b u c) -> p b u c", b=BATCHES, u=4)
        tc_parts = arena[:, at[2]:at[3]].bitcast(BF16).rearrange(
            "p (b u s c) -> p b u s c", b=BATCHES, u=4, s=PARTS)
        z1 = arena[0:MH, 0:2 * B].rearrange("p (h b) -> p h b", h=2)
        z1n = arena[0:MH, 2 * B:4 * B].rearrange("p (h b) -> p h b", h=2)
        z2 = arena[0:M2, 4 * B:5 * B]
        z2n = arena[0:M2, 5 * B:6 * B]

        ps_ent = [bank("ps_ent0"), bank("ps_ent1")]
        ps_tgt = [bank("ps_tgt0"), bank("ps_tgt1")]
        ps_h1 = [bank("ps_h1a"), bank("ps_h1b")]
        ps_h2 = bank("ps_h2")
        ps_pool = bank("ps_pool")

        mlp_banks = ps_ent + ps_tgt + ps_h1 + [ps_h2, ps_pool]

        s_rows = sem("rows_in")
        s_feat = sem("feat_in")
        s_w = sem("weights_in")
        s_wsc = sem("weights_scaled")
        s_mlpw = sem("mlp_weights_in")
        s_const = sem("constants_made")
        s_ident = sem("identity_zeroed")
        s_d = sem("vector_steps")
        s_idx = sem("row_numbers_made")
        s_seg = sem("segments_made")
        s_movie = sem("movie_numbers_made")
        s_cnt = sem("genre_counts_made")
        s_blocks = sem("genre_blocks_in")
        s_blkz = sem("genre_blocks_zeroed")
        s_listp = sem("plain_lists_out")
        s_segout = sem("segments_out")
        s_segin = sem("segments_in")
        s_flag_ps = sem("flag_summed")
        s_flag = sem("flag_ready")
        s_segT = sem("segments_turned")
        s_segrow = sem("segment_rows_ready")
        s_runs = sem("runs_sorted")
        s_scat = [sem(f"runs_out{t}") for t in range(TILES)]
        s_tabrow = [sem(f"table_movies{q}") for q in range(len(PIECE_ENDS))]
        s_cT = sem("counts_turned")
        s_cTc = sem("counts_copied")
        s_gps = sem("genre_products")
        s_gev = sem("genre_halves_written")
        s_table = sem("table_out")
        s_ads = [sem(f"ads_gathered{t}") for t in range(TILES)]
        s_adsps = sem("ads_turned")
        s_adsT = sem("ads_copied")
        s_cps = sem("target_share_products")
        s_tcv = sem("target_values_ready")
        s_tchi = sem("target_parts_hi")
        s_tcr = sem("target_rests")
        s_tcp = sem("target_parts_ready")
        s_tcout = sem("target_parts_out")

        s_ix = [sem(f"unit_index{k}") for k in range(RING)]
        s_tc = [sem(f"unit_target{k}") for k in range(RING)]
        s_g = [sem(f"unit_entries{k}") for k in range(RING)]
        s_begun = sem("unit_gathers_begun")
        s_oh_t = sem("reached_made")
        s_oh = sem("user_matrix_made")
        s_wt = sem("weight_steps")
        s_T = sem("entries_turned")
        s_tg = sem("targets_spread")
        s_cp = sem("entries_copied")
        s_pr = sem("products_made")
        s_1 = sem("layer1_summed")
        s_n = sem("layer1_negated")
        s_a1 = sem("layer1_done")
        s_2 = sem("layer2_summed")
        s_n2 = sem("layer2_negated")
        s_a2 = sem("layer2_done")
        s_m2w = sem("layer2_scaled")
        s_at = sem("attention_summed")
        s_aw = sem("attention_weighted")
        s_pl = sem("pool_summed")
        s_pa = sem("pool_added")
        s_pos = sem("positions_moved")
        s_main_dve = sem("vector_main_done")

        s_m1 = sem("mlp1_summed")
        s_v1n = sem("mlp1_normed")
        s_v1 = sem("norm1_variance")
        s_sq1 = sem("norm1_root")
        s_bn1 = sem("norm1_ready")
        s_n1 = sem("mlp1_negated")
        s_z1 = sem("mlp1_done")
        s_m2 = sem("mlp2_summed")
        s_v2n = sem("mlp2_normed")
        s_v2 = sem("norm2_variance")
        s_sq2 = sem("norm2_root")
        s_bn2 = sem("norm2_ready")
        s_nz2 = sem("mlp2_negated")
        s_z2 = sem("mlp2_done")
        s_lg = sem("logits_summed")
        s_sh = sem("logits_shifted")
        s_ex = sem("exponentials")
        s_pb = sem("probabilities")
        s_out = sem("output_out")

        N_CONST = 6 + TILES
        N_W = 10
        block = ctx.enter_context(nc.Block())

        @block.sync
        def _(sp):
            rows_v = rows.rearrange("(t p u) c -> t p (u c)", t=TILES, u=USERS)
            sp.dma_start(feat_sb[:, :, :].rearrange("p k c -> p (k c)"),
                         movie_feature.rearrange("(p k) c -> p (k c)", p=TP)).then_inc(s_feat, 16)
            for t in range(TILES):
                sp.dma_start(rows_sb[:, t, :, :].rearrange("p u c -> p (u c)"),
                             rows_v[t]).then_inc(s_rows, 16)
            sp.wait_ge(s_blkz, 1)
            for i in range(KB):
                sp.dma_start(genre_blocks[i * VOCAB:(i + 1) * VOCAB, i * E:(i + 1) * E],
                             emb_genre).then_inc(s_blocks, 16)

            sp.wait_ge(s_idx, TILES)
            for t in range(TILES):
                groups = list_by_group[t * 128:(t + 1) * 128, :]
                sp.dma_start(groups[:, 0:USERS * T].rearrange("g (u e) -> g u e", u=USERS),
                             idx_sb[:, t, :, 1:1 + T]).then_inc(s_listp, 16)
                sp.dma_start(groups[:, USERS * T:REGION],
                             idx_sb[:, t, :, :].rearrange("p u c -> p (u c)")
                             [:, 0:REGION - USERS * T]).then_inc(s_listp, 16)

            sp.wait_ge(s_seg, 1)
            sp.dma_start(seg_dram.rearrange("(t p) s -> p t s", t=TILES),
                         seg_sb[:, :, :, :].rearrange("p t s u -> p t (s u)")).then_inc(s_segout, 16)
            sp.wait_ge(s_segout, 16)
            sp.dma_start(seg_all[:, :, :, :].rearrange("p g s u -> p (g s u)"),
                         seg_dram.rearrange("(o g) s -> o (g s)", o=1)
                         .broadcast_to([128, GROUPS * SEG])).then_inc(s_segin, 16)

            table_v = table_dram.rearrange("(p k) d -> p (k d)", p=TP)
            for q, end in enumerate(PIECE_ENDS):
                first = PIECE_ENDS[q - 1] if q else 0
                sp.wait_ge(s_tabrow[q], 16 * (end - first))
                sp.wait_ge(s_gev, end // KB)
                sp.dma_start(table_v[:, first * D:end * D],
                             table_sb[:, first:end, :].rearrange("p k d -> p (k d)")
                             ).then_inc(s_table, 16)

            for t in range(TILES):
                sp.wait_ge(s_scat[t], 16 * USERS)
            for k in range(RING):
                sp.dma_start(idx_ring[:, k, :], unit_list(k, 0)).then_inc(s_ix[k], 16)

            tc_v = tc_dram.rearrange("(t p) (u s) c -> t p u s c", t=TILES, u=USERS)
            for b in range(BATCHES):
                t, u = divmod(4 * b, USERS)
                sp.wait_ge(s_tcp, b + 1)
                sp.dma_start(tc_v[t, :, u:u + 4].rearrange("p u s c -> p (u s c)"),
                             tc_parts[:, b].rearrange("p u s c -> p (u s c)")).then_inc(s_tcout, 16)
                if b == 1:
                    sp.wait_ge(s_tcout, 16 * 2)
                    for k in range(RING):
                        sp.dma_start(tc_ring[:, k, :], tc_dram[k]).then_inc(s_tc[k], 16)
            sp.wait_ge(s_tcout, 16 * BATCHES)
            sp.wait_ge(s_flag, 1)
            general = sp.value_load(flag_i[0:1, 0:1], min_val=0, max_val=GROUPS)

            def step_sp(s, chunk):
                if s.has(0):
                    u = s.unit(0)
                    if u.after(RING):
                        sp.wait_ge(s_g[u.slot], 16 * UNIT_TILES * u.turn)
                        sp.dma_start(idx_ring[:, u.slot, :],
                                     unit_list(u.group, chunk)).then_inc(s_ix[u.slot], 16)
                        sp.wait_ge(s_1, u.n - RING + 1)
                        sp.dma_start(tc_ring[:, u.slot, :], tc_dram[u.group]).then_inc(s_tc[u.slot], 16)

            run_pass(sp, lambda s: step_sp(s, 0), GROUPS, 0, 0)
            with sp.If(general > 0):
                with sp.Fori(1, PASSES) as p:
                    run_pass(sp, lambda s: step_sp(s, p), GROUPS, p * (GROUPS // RING), 0)
            with sp.Else():
                sp.nop()

            sp.wait_ge(s_pb, 1)
            sp.dma_start(out.rearrange("(t p u) c -> p t (u c)", t=TILES, u=USERS),
                         probs[:, :, :].rearrange("p (t u) c -> p t (u c)", t=TILES)
                         ).then_inc(s_out, 16)
            sp.wait_ge(s_out, 16)

        @block.gpsimd
        def _(pool):
            pool.memset(genre_blocks[:, :], 0.0).then_inc(s_blkz, 1)
            pool.memset(ident[:, :], 0.0).then_inc(s_ident, 1)
            pool.wait_ge(s_ident, 1)
            pool.affine_select(out=ident[:, :], in_=ident[:, :], compare_op=ALU.not_equal, fill=1.0,
                               base=0, pattern=[[-1, 128]], channel_multiplier=1).then_inc(s_const, 1)
            pool.memset(ones_col[:, :], 1.0).then_inc(s_const, 1)
            pool.memset(pooledT[:, :, :], 0.0).then_inc(s_const, 1)
            for t in range(TILES):
                pool.iota(group_base[:, t, :], pattern=[[0, 1]], base=t * 128 * REGION,
                          channel_multiplier=REGION).then_inc(s_const, 1)
            pool.iota(plain_start[:, :], pattern=[[T, USERS]], channel_multiplier=0).then_inc(s_const, 1)
            pool.iota(pos_init[:, :], pattern=[[1, UNIT_TILES]], channel_multiplier=UNIT_TILES,
                      allow_small_or_imprecise_dtypes=True).then_inc(s_const, 1)
            pool.iota(pos_row[:, :, :], pattern=[[1, UNIT_TILES], [UNIT_TILES, TILE]],
                      channel_multiplier=0, allow_small_or_imprecise_dtypes=True).then_inc(s_const, 1)

            def gather_movies(k):
                pool.indirect_dma_start(
                    out=table_sb[:, k, 0:E], out_offset=None, in_=emb_movie,
                    in_offset=bass.IndirectOffsetOnAxis(ap=movie_idx[:, k:k + 1], axis=0),
                ).then_inc(s_tabrow[sum(k >= end for end in PIECE_ENDS)], 16)

            def scatter_run(t, u):
                pool.wait_ge(s_runs, USERS * t + u + 1)
                if u:
                    pool.wait_ge(s_scat[t], 16 * u)
                pool.indirect_dma_start(
                    out=list_dram,
                    out_offset=bass.IndirectOffsetOnAxis(ap=scatter_to[:, t, u:u + 1], axis=0),
                    in_=run_idx[:, t, u, :], in_offset=None).then_inc(s_scat[t], 16)

            def gather_target(t, u):
                pool.indirect_dma_start(
                    out=tc_val[:, 2 * t + u // 4, u % 4, 0:D], out_offset=None, in_=table_dram,
                    in_offset=bass.IndirectOffsetOnAxis(ap=idx_sb[:, t, u, NCOL - 1:NCOL], axis=0),
                ).then_inc(s_ads[t], 16)

            between = [3, 4] * 6 + [3, 5] * 2
            assert len(between) == TILES * USERS
            movies_between = sum(between[:12])
            assert sum(between[12:]) == TILES * USERS
            early = TK - movies_between
            pool.wait_ge(s_movie, 1)
            for k in range(early):
                gather_movies(k)
            pool.wait_ge(s_flag, 1)
            general = pool.value_load(flag_i[0:1, 0:1], min_val=0, max_val=GROUPS)
            pool.wait_ge(s_listp, 16 * 2 * TILES)
            with pool.If(general > 0):
                for k in range(early, TK):
                    gather_movies(k)
                pool.wait_ge(s_table, 16 * len(PIECE_ENDS))
                for i in range(TILES * USERS):
                    gather_target(*divmod(i, USERS))
                for t in range(TILES):
                    pool.sem_inc(s_scat[t], 16 * USERS)
            with pool.Else():
                k = early
                target = 0
                for i in range(TILES * USERS):
                    scatter_run(*divmod(i, USERS))
                    if i == 12:
                        pool.wait_ge(s_table, 16 * len(PIECE_ENDS))
                    for _ in range(between[i]):
                        if i < 12:
                            gather_movies(k)
                            k += 1
                        else:
                            gather_target(*divmod(target, USERS))
                            target += 1

            def step_pool(s):
                if s.has(0):
                    u = s.unit(0)
                    pool.wait_ge(s_ix[u.slot], 16 * (u.turn + 1))
                    if u.after(RING):
                        pool.wait_ge(s_pl, u.n - RING + 1)
                    pool.sem_inc(s_begun, 1)
                    for k in range(UNIT_TILES):
                        pool.indirect_dma_start(
                            out=entries[:, u.slot, k, :], out_offset=None, in_=table_dram,
                            in_offset=bass.IndirectOffsetOnAxis(ap=idx_ring[:, u.slot, k:k + 1], axis=0),
                        ).then_inc(s_g[u.slot], 16)

            run_pass(pool, step_pool, GROUPS, 0, 0)
            with pool.If(general > 0):
                with pool.Fori(1, PASSES) as p:
                    run_pass(pool, step_pool, GROUPS, p * (GROUPS // RING), 0)
            with pool.Else():
                pool.nop()

        @block.scalar
        def _(act):
            def load(dst, src, s):
                act.dma_start(dst, src).then_inc(s, 16)

            def col(v):
                return v.rearrange("(p o) -> p o", o=1)

            load(w1_sb[:, :, :], att_w1.rearrange("(s p) h -> p s h", p=D), s_w)
            load(b1_bc[:, :], att_b1.rearrange("(o h) -> o h", o=1).broadcast_to([128, H1]), s_w)
            for c, v in ((A1, att_a1), (A2, att_a2), (AM1, mlp_a1), (AM2, mlp_a2), (BO, att_bo)):
                load(scal[:, c:c + 1], v.rearrange("(o h) -> o h", o=1).broadcast_to([128, 1]), s_w)
            load(w2_sb[0:H1, :], att_w2, s_w)
            load(w2_sb[ONE:ONE + 1, :], att_b2.rearrange("(o h) -> o h", o=1), s_w)
            load(wo_bc[:, :], att_wo.rearrange("h o -> o h").broadcast_to([128, H2]), s_w)

            for i in range(TK // KB):
                act.wait_ge(s_cT, i + 1)
                if i >= 2:
                    act.wait_ge(s_gps, i - 1)
                act.activation(genre_cntT[:, i % 2, :], ps_ent[i % 2][0:KB * VOCAB, 0:TP],
                               ACT.Copy).then_inc(s_cTc, 1)

            for h in range(2):
                load(m1_sb[:, h, :], mlp_w1[h * D:(h + 1) * D, :], s_mlpw)
                load(m2_sb[:, h, :], mlp_w2[h * MH:(h + 1) * MH, :], s_mlpw)
                for c, v in enumerate((mlp_b1, bn1_g, bn1_b)):
                    load(bnp1[:, c, h:h + 1], col(v[h * MH:(h + 1) * MH]), s_mlpw)
            for c, v in enumerate((mlp_b2, bn2_g, bn2_b)):
                load(bnp2[:, c:c + 1], col(v), s_mlpw)
            load(ow_sb[:, :], out_w, s_mlpw)
            load(ob_sb[:, :], out_b.rearrange("(o h) -> o h", o=1).broadcast_to([128, 2]), s_mlpw)

            for t in range(TILES):
                pair = (2 * t, 2 * t + 1)
                for b in pair:
                    u = 4 * (b % 2)
                    act.wait_ge(s_adsps, b + 1)
                    act.activation(adsT[:, u:u + 4, t * 128:(t + 1) * 128],
                                   ps_ent[b % 2][:, :].rearrange("p (u g) -> p u g", u=4),
                                   ACT.Copy).then_inc(s_adsT, 1)
                for b in pair:
                    act.wait_ge(s_tcv, b + 1)
                    act.activation(tc_parts[:, b, :, 0, :], tc_val[:, b, :, :],
                                   ACT.Copy).then_inc(s_tchi, 1)
                for b in pair:
                    act.wait_ge(s_tcr, b + 1)
                    act.activation(tc_parts[:, b, :, 1, :], tc_res[:, b, :, :],
                                   ACT.Copy).then_inc(s_tchi, 1)

            act.wait_ge(s_flag, 1)
            general = act.value_load(flag_i[0:1, 0:1], min_val=0, max_val=GROUPS)

            def step_act(s):
                if s.has(0):
                    u = s.unit(0)
                    act.wait_ge(s_T, u.n + 1)
                    if u.after(DEEP):
                        act.wait_ge(s_1, u.n - DEEP + 1)
                    act.activation(entT[:, u.slot % DEEP, :], ps_ent[u.slot % 2][:, 0:UNIT],
                                   ACT.Copy).then_inc(s_cp, 1)
                if s.has(1):
                    u = s.unit(1)
                    act.wait_ge(s_1, u.n + 1)
                    if u.after(DEEP):
                        act.wait_ge(s_a1, u.n - DEEP + 1)
                    act.activation(neg1[:, u.slot % DEEP, :], ps_h1[u.slot % 2][0:H1, 0:UNIT],
                                   ACT.Relu, scale=-1.0).then_inc(s_n, 1)
                if s.has(2):
                    u = s.unit(2)
                    act.wait_ge(s_2, u.n + 1)
                    if u.after(DEEP):
                        act.wait_ge(s_a2, u.n - DEEP + 1)
                    act.activation(neg2[:, u.slot % DEEP, :], ps_h2[0:TILE, 0:LAYER2], ACT.Relu,
                                   scale=-1.0).then_inc(s_n2, 1)

            run_pass(act, step_act, GROUPS, 0, 2)
            with act.If(general > 0):
                with act.Fori(1, PASSES) as p:
                    run_pass(act, step_act, GROUPS, p * (GROUPS // RING), 2)
            with act.Else():
                act.nop()

            act.wait_ge(s_v1, 1)
            act.activation(bnv[0:MH, 0:2, 1], bnv[0:MH, 0:2, 0], ACT.Sqrt).then_inc(s_sq1, 1)
            act.wait_ge(s_bn1, 1)
            for c in range(NCH):
                for h in range(2):
                    act.activation(z1n[:, h, c * CH:(c + 1) * CH], mlp_banks[2 * c + h][0:MH, :],
                                   ACT.Relu, bias=bnv[0:MH, h, 7:8], scale=bnv[0:MH, h, 6:7]
                                   ).then_inc(s_n1, 1)
                act.activation(z1[:, 0, c * CH:(c + 1) * CH], mlp_banks[2 * c][0:MH, :],
                               ACT.Identity, bias=bnv[0:MH, 0, 5:6], scale=bnv[0:MH, 0, 4:5]
                               ).then_inc(s_v1n, 1)
            act.wait_ge(s_v2, 1)
            act.activation(bnv[0:M2, 2:3, 1], bnv[0:M2, 2:3, 0], ACT.Sqrt).then_inc(s_sq2, 1)
            act.wait_ge(s_bn2, 1)
            for c in range(NCH):
                act.activation(z2n[:, c * CH:(c + 1) * CH], mlp_banks[2 * c][0:M2, :],
                               ACT.Relu, bias=bnv[0:M2, 2, 7:8], scale=bnv[0:M2, 2, 6:7]
                               ).then_inc(s_nz2, 1)
                if c % 2:
                    act.activation(z2[:, c * CH:(c + 1) * CH], mlp_banks[2 * c][0:M2, :],
                                   ACT.Identity, bias=bnv[0:M2, 2, 5:6], scale=bnv[0:M2, 2, 4:5]
                                   ).then_inc(s_v2n, 1)
            act.wait_ge(s_sh, 3)
            act.activation(probs[:, :, :], probs[:, :, :], ACT.Exp).then_inc(s_ex, 1)

        @block.tensor
        def _(pe):
            pe.wait_ge(s_const, N_CONST)

            pe.wait_ge(s_flag_ps, 1)
            nc.tensor.matmul(ps_pool[0:1, 0:1], flag_col[:, :], ones_col[:, :],
                             start=True, stop=True).then_inc(s_segT, 1)
            pe.wait_ge(s_seg, 1)
            for t in range(TILES):
                for w in range(2):
                    c = w * GROUPS + t * 128
                    mm = nc.tensor.transpose(ps_tgt[0][0:USERS * PARTS, c:c + 128],
                                             rep_sb[:, t, w, :, :].rearrange("p u s -> p (u s)"),
                                             ident[:, :])
            mm.then_inc(s_segT, 1)

            pe.wait_ge(s_cnt, 1)
            pe.wait_ge(s_blocks, 16 * KB)

            def turn_counts(i):
                if i >= 2:
                    pe.wait_ge(s_cTc, i - 1)
                nc.tensor.transpose(ps_ent[i % 2][0:KB * VOCAB, 0:TP],
                                    genre_cnt[:, i * KB:(i + 1) * KB, :].rearrange("p k v -> p (k v)"),
                                    ident[0:TP, 0:TP]).then_inc(s_cT, 1)

            turn_counts(0)
            for i in range(TK // KB):
                if i + 1 < TK // KB:
                    turn_counts(i + 1)
                pe.wait_ge(s_cTc, i + 1)
                if i >= 2:
                    pe.wait_ge(s_gev, i - 1)
                nc.tensor.matmul(ps_h1[i % 2][0:TP, 0:KB * E], genre_cntT[:, i % 2, :],
                                 genre_blocks[:, :], start=True, stop=True).then_inc(s_gps, 1)

            pe.wait_ge(s_w, 16 * N_W)
            pe.wait_ge(s_gev, TK // KB)
            for t in range(TILES):
                pe.wait_ge(s_ads[t], 16 * USERS)
                if t:
                    pe.wait_ge(s_adsT, 2 * t)
                for b in (2 * t, 2 * t + 1):
                    for i in range(4):
                        mm = nc.tensor.transpose(ps_ent[b % 2][:, i * 128:(i + 1) * 128],
                                                 tc_val[:, b, i, 0:D], ident[:, :])
                    mm.then_inc(s_adsps, 1)
                for b in (2 * t, 2 * t + 1):
                    pe.wait_ge(s_adsT, b + 1)
                    if t:
                        pe.wait_ge(s_tcv, b - 1)
                    for i in range(4):
                        dst = ps_h1[b % 2][:, i * H1:(i + 1) * H1]
                        mm = nc.tensor.matmul(dst, adsT[:, 4 * (b % 2) + i, t * 128:(t + 1) * 128],
                                              w1_sb[:, 1, :], start=True, stop=True)
                    mm.then_inc(s_cps, 1)

            pe.wait_ge(s_tcv, BATCHES)
            pe.wait_ge(s_segrow, 1)
            pe.wait_ge(s_flag, 1)
            general = pe.value_load(flag_i[0:1, 0:1], min_val=0, max_val=GROUPS)

            def step_pe(s):
                if s.has(0):
                    u = s.unit(0)
                    q, d = u.slot % 2, u.slot % DEEP
                    pe.wait_ge(s_g[u.slot], 16 * UNIT_TILES * (u.turn + 1))
                    if u.after(2):
                        pe.wait_ge(s_cp, u.n - 1)
                    for k in range(UNIT_TILES):
                        mm = nc.tensor.transpose(ps_ent[q][:, k * TILE:(k + 1) * TILE],
                                                 entries[0:TILE, u.slot, k, :], ident[0:TILE, 0:TILE])
                    mm.then_inc(s_T, 1)
                    pe.wait_ge(s_tc[u.slot], 16 * (u.turn + 1))
                    pe.wait_ge(s_oh, u.n + 1)
                    if u.after(2):
                        pe.wait_ge(s_pr, u.n - 1)
                    nc.tensor.matmul(ps_tgt[q][:, 0:UNIT], tc_ring[:, u.slot, 0:D],
                                     user_of[:, d, :], start=True, stop=True).then_inc(s_tg, 1)
                if s.has(1):
                    u = s.unit(1)
                    q, d = u.slot % 2, u.slot % DEEP
                    dst = ps_h1[q][0:H1, 0:UNIT]
                    pe.wait_ge(s_cp, u.n + 1)
                    if u.after(2):
                        pe.wait_ge(s_a1, u.n - 1)
                    nc.tensor.matmul(dst, w1_sb[:, 0, :], entT[:, d, :], start=True, stop=False)
                    nc.tensor.matmul(dst, tc_ring[:, u.slot, D:TC], user_of[:, d, :],
                                     start=False, stop=False)
                    pe.wait_ge(s_pr, u.n + 1)
                    nc.tensor.matmul(dst, w1_sb[:, 2, :], prodT[:, d, :],
                                     start=False, stop=True).then_inc(s_1, 1)
                if s.has(2):
                    u = s.unit(2)
                    q, d = u.slot % 2, u.slot % DEEP
                    pe.wait_ge(s_a1, u.n + 1)
                    if u.after(1):
                        pe.wait_ge(s_a2, u.n)
                    for k in range(UNIT_TILES):
                        mm = nc.tensor.matmul(ps_h2[0:TILE, k * H2:(k + 1) * H2],
                                              act1[:, d, k * TILE:(k + 1) * TILE], w2_sb[:, :],
                                              start=True, stop=True)
                    mm.then_inc(s_2, 1)
                if s.has(3):
                    u = s.unit(3)
                    q, d = u.slot % 2, u.slot % DEEP
                    pe.wait_ge(s_aw, u.n + 1)
                    if u.after(1):
                        pe.wait_ge(s_pa, u.n)
                    for k in range(UNIT_TILES):
                        mm = nc.tensor.matmul(ps_pool[:, 0:USERS], entries[0:TILE, u.slot, k, :],
                                              att_w[:, d, k, :], start=(k == 0),
                                              stop=(k == UNIT_TILES - 1))
                    mm.then_inc(s_pl, 1)

            pooled_v = pooledT[:, :, :].rearrange("p u g -> p (u g)")
            ads_v = adsT[:, :, :].rearrange("p u g -> p (u g)")

            def mlp1(i, part):
                c, h = divmod(i, 2)
                data = (pooled_v, ads_v)[part][:, c * CH:(c + 1) * CH]
                return nc.tensor.matmul(mlp_banks[i][0:MH, :], m1_sb[:, part, h * MH:(h + 1) * MH],
                                        data, start=(part == 1), stop=(part == 0))

            last_steps = 3
            run_steps(pe, step_pe, GROUPS, 0)
            pe.wait_ge(s_mlpw, 16 * 15)
            with pe.If(general > 0):
                for k in range(last_steps):
                    step_pe(Step(GROUPS // RING, k, 0, GROUPS))
                with pe.Fori(1, PASSES) as p:
                    run_pass(pe, step_pe, GROUPS, p * (GROUPS // RING), last_steps)
                pe.wait_ge(s_cp, GROUPS * PASSES)
                pe.wait_ge(s_pr, GROUPS * PASSES)
                for i in range(4):
                    mlp1(i, 1)
            with pe.Else():
                step_pe(Step(GROUPS // RING, 0, 0, GROUPS))
                pe.wait_ge(s_cp, GROUPS)
                for i in range(2):
                    mlp1(i, 1)
                step_pe(Step(GROUPS // RING, 1, 0, GROUPS))
                pe.wait_ge(s_pr, GROUPS)
                for i in range(2, 4):
                    mlp1(i, 1)
                step_pe(Step(GROUPS // RING, 2, 0, GROUPS))

            pe.wait_ge(s_main_dve, 1)
            for i in range(2 * NCH):
                if i >= 4:
                    mlp1(i, 1)
                mlp1(i, 0).then_inc(s_m1, 1)
            for c in range(NCH):
                pe.wait_ge(s_z1, 2 * (c + 1))
                for h in range(2):
                    mm = nc.tensor.matmul(mlp_banks[2 * c][0:M2, :], m2_sb[:, h, :],
                                          z1[:, h, c * CH:(c + 1) * CH], start=(h == 0), stop=(h == 1))
                mm.then_inc(s_m2, 1)
            for c in range(NCH):
                pe.wait_ge(s_z2, c + 1)
                for i in range(4):
                    j = 4 * c + i
                    u, t = divmod(j, TILES)
                    at = 2 * (t * USERS + u)
                    mm = nc.tensor.matmul(ps_pool[:, at:at + 2], z2[:, j * 128:(j + 1) * 128],
                                          ow_sb[:, :], start=True, stop=True)
            mm.then_inc(s_lg, 1)

        @block.vector
        def _(dve):
            V = nc.vector
            steps = [0]

            def link(ins):
                steps[0] += 1
                ins.then_inc(s_d, 1)
                dve.wait_ge(s_d, steps[0])

            def row_numbers(dst, raw, tmp, n):
                link(V.tensor_scalar(tmp, raw, 0.0, float(n), ALU.is_lt, ALU.mult))
                link(V.tensor_tensor(tmp, tmp, raw, ALU.add))
                link(V.tensor_scalar(dst, tmp, 0.0, float(n - 1), ALU.max, ALU.min))

            dve.wait_ge(s_feat, 16)
            movies = feat_sb[:, :, 0]
            row_numbers(movie_idx[:, :], movies, feat_f[:, 0, :, 0], N_ROWS)
            dve.sem_inc(s_movie, 1)

            dve.wait_ge(s_rows, 16 * TILES)
            flat = "p u c -> p (u c)"
            for t in range(TILES):
                key = key_sb[:, t].rearrange(flat)
                row_numbers(idx_sb[:, t].rearrange(flat), rows_sb[:, t].rearrange(flat), key, N_ROWS)
                dve.sem_inc(s_idx, 1)
                link(V.tensor_scalar(key, idx_sb[:, t].rearrange(flat), -1.0, float(LAST_ROW),
                                     ALU.mult, ALU.add))
                ones = rows_sb[:, t].rearrange(flat).bitcast(F32)
                link(V.tensor_scalar(ones, key, 1.0, None, ALU.min))
                link(V.tensor_reduce(count[:, t, :],
                                     rows_sb[:, t, :, 1:1 + T].bitcast(F32), AX_X, ALU.add))

            link(V.memset(start9[:, :, 0:1], 0.0))
            length = small[:, 0]
            link(V.tensor_scalar(length, count[:, :, :], 1.0, None, ALU.add))
            for u in range(USERS):
                link(V.tensor_tensor(start9[:, :, u + 1], start9[:, :, u], length[:, :, u], ALU.add))
            starts, ends, extra = (seg_sb[:, :, i, :] for i in range(3))
            link(V.tensor_copy(starts, start9[:, :, 0:USERS]))
            link(V.tensor_copy(ends, start9[:, :, 1:USERS + 1]))
            link(V.tensor_scalar(extra, count[:, :, :], -1.0, float(T - 1), ALU.mult, ALU.add))
            over = small[:, 1]
            link(V.tensor_scalar(over, ends, float(UNIT), None, ALU.is_gt))
            link(V.tensor_scalar(small[:, 2], length, float(RUN), None, ALU.is_gt))
            link(V.tensor_tensor(over, over, small[:, 2], ALU.max))
            link(V.tensor_reduce(flag_col[:, :], over.rearrange("p t u -> p (t u)"), AX_X, ALU.max))
            dve.sem_inc(s_flag_ps, 1)
            dve.wait_ge(s_const, N_CONST)
            link(V.tensor_scalar(small[:, 3], starts, float(UNIT), None, ALU.min))
            link(V.tensor_tensor(scatter_to[:, :, :], small[:, 3],
                                 group_base[:, :, :].broadcast_to([128, TILES, USERS]), ALU.add))
            dve.wait_ge(s_segT, 1)
            link(V.tensor_copy(flag_i[:, :], ps_pool[0:1, 0:1]))
            dve.sem_inc(s_flag, 1)
            general = dve.value_load(flag_i[0:1, 0:1], min_val=0, max_val=GROUPS)
            base = steps[0]
            with dve.If(general > 0):
                for t in range(TILES):
                    V.tensor_copy(seg_sb[:, t, 0, :], plain_start[:, :]).then_inc(s_d, 1)
                    V.tensor_scalar(seg_sb[:, t, 1, :], plain_start[:, :], float(T), None,
                                    ALU.add).then_inc(s_d, 1)
                    V.memset(seg_sb[:, t, 2, :], 0.0).then_inc(s_d, 1)
            with dve.Else():
                dve.sem_inc(s_d, 3 * TILES)
            steps[0] = base + 3 * TILES
            dve.wait_ge(s_d, steps[0])
            for t in range(TILES):
                for w in range(2):
                    link(V.tensor_copy(rep_sb[:, t, w, :, :],
                                       seg_sb[:, t, w, :].rearrange("p (u o) -> p u o", o=1)
                                       .broadcast_to([128, USERS, PARTS])))
            dve.sem_inc(s_seg, 1)

            row_numbers(genre_bf[:, :, :].rearrange("p j k -> p k j"), feat_sb[:, :, 1:FEATS],
                        feat_f[:, 0, :, 1:FEATS], VOCAB)
            for half in range(2):
                for v in range(VOCAB // 2):
                    ins = V.tensor_scalar(genre_is[:, v, :, :], genre_bf[:, :, :],
                                          float(half * VOCAB // 2 + v), None, ALU.is_equal)
                    ins.then_inc(s_d, 1)
                steps[0] += VOCAB // 2
                dve.wait_ge(s_d, steps[0])
                for j in range(1, GENRES - 1):
                    link(V.tensor_tensor(genre_is[:, :, 0, :], genre_is[:, :, 0, :],
                                         genre_is[:, :, j, :], ALU.add))
                link(V.tensor_tensor(
                    genre_cnt[:, :, half * (VOCAB // 2):(half + 1) * (VOCAB // 2)]
                    .rearrange("p k v -> p v k"),
                    genre_is[:, :, 0, :], genre_is[:, :, GENRES - 1, :], ALU.add))
            dve.sem_inc(s_cnt, 1)
            link(V.memset(act1[64:ONE + 1, :, :], 1.0))
            link(V.tensor_scalar(feat_f[:, 1, :, 1:FEATS], feat_sb[:, :, 1:FEATS], 0.0, None, ALU.is_gt))
            link(V.tensor_reduce(genre_len[:, 0, :], feat_f[:, 1, :, 1:FEATS], AX_X, ALU.add))
            link(V.tensor_scalar(genre_len[:, 0, :], genre_len[:, 0, :], POOL_EPS, None, ALU.add))
            link(V.reciprocal(genre_len[:, 1, :], genre_len[:, 0, :]))
            dve.wait_ge(s_segT, 2)
            link(V.tensor_copy(seg_rows[:, :, :].rearrange("p w g -> p (w g)"),
                               ps_tgt[0][0:USERS * PARTS, 0:2 * TILES * 128]))
            dve.sem_inc(s_segrow, 1)

            dve.wait_ge(s_w, 16 * N_W)
            V.tensor_scalar(scal[:, C1:CM2 + 1], scal[:, A1:AM2 + 1], -1.0, 1.0,
                            ALU.mult, ALU.add).then_inc(s_wsc, 1)
            dve.wait_ge(s_wsc, 1)

            def write_genres(i):
                dve.wait_ge(s_gps, i + 1)
                V.tensor_tensor(table_sb[:, i * KB:(i + 1) * KB, E:D],
                                ps_h1[i % 2][0:TP, 0:KB * E].rearrange("p (k e) -> p k e", k=KB),
                                genre_len[:, 1, i * KB:(i + 1) * KB].rearrange("p (k o) -> p k o", o=1)
                                .broadcast_to([TP, KB, E]), ALU.mult).then_inc(s_gev, 1)

            blocks_left = iter(range(TK // KB))
            for pair in range(TILES * USERS // 2):
                t, first = divmod(2 * pair, USERS)
                for r in range(RUN // 8):
                    for i in range(2):
                        src = work[:, i, :] if r else key_sb[:, t, first + i, 1:1 + T]
                        if r:
                            dve.wait_ge(s_d, steps[0] - 1)
                        V.max(best[:, i, 8 * r:8 * r + 8], src).then_inc(s_d, 1)
                        steps[0] += 1
                    if r < RUN // 8 - 1:
                        for i in range(2):
                            src = work[:, i, :] if r else key_sb[:, t, first + i, 1:1 + T]
                            dve.wait_ge(s_d, steps[0] - 1)
                            V.match_replace(work[:, i, :], best[:, i, 8 * r:8 * r + 8], src,
                                            -1.0).then_inc(s_d, 1)
                            steps[0] += 1
                    for i in blocks_left:
                        write_genres(i)
                        break
                dve.wait_ge(s_d, steps[0])
                for i in range(2):
                    V.tensor_scalar(run_idx[:, t, first + i, :], best[:, i, :], -1.0, float(LAST_ROW),
                                    ALU.mult, ALU.add).then_inc(s_runs, 1)
                dve.wait_ge(s_runs, 2 * (pair + 1))

            for t in range(TILES):
                pair = (2 * t, 2 * t + 1)
                for b in pair:
                    dve.wait_ge(s_cps, b + 1)
                    V.tensor_tensor(tc_val[:, b, :, D:TC], ps_h1[b % 2][:, 0:4 * H1]
                                    .rearrange("p (u h) -> p u h", u=4),
                                    b1_bc[:, :].rearrange("p (o h) -> p o h", o=1)
                                    .broadcast_to([128, 4, H1]), ALU.add).then_inc(s_tcv, 1)
                for b in pair:
                    dve.wait_ge(s_tcv, b + 1)
                    dve.wait_ge(s_tchi, 2 * t + b + 1)
                    V.tensor_tensor(tc_res[:, b], tc_val[:, b], tc_parts[:, b, :, 0, :],
                                    ALU.subtract).then_inc(s_tcr, 1)
                for b in pair:
                    dve.wait_ge(s_tcr, b + 1)
                    dve.wait_ge(s_tchi, 2 * t + b + 3)
                    V.tensor_tensor(tc_parts[:, b, :, 2, :], tc_res[:, b], tc_parts[:, b, :, 1, :],
                                    ALU.subtract).then_inc(s_tcp, 1)

            WT_STEPS = 6

            def entry_weights(u, part):
                half = u.slot // 4
                g = seg_all[:, columns(u.group, 4), :, :]
                done = WT_STEPS * (2 * u.turn + half)
                shape = [128, 4, UNIT_TILES, USERS]
                start, end, extra = (g[:, :, i:i + 1, :].broadcast_to(shape) for i in range(3))
                pos, next_pos = (pos_col[:, i, :].rearrange("p (a k b) -> p a k b", a=1, b=1)
                                 .broadcast_to(shape) for i in range(2))
                if part == 0:
                    if u.after(4):
                        dve.wait_ge(s_wt, done)
                    V.tensor_tensor(wt_tmp[:, 0], pos, start, ALU.is_ge).then_inc(s_wt, 1)
                    V.tensor_tensor(wt_tmp[:, 1], pos, end, ALU.is_ge).then_inc(s_wt, 1)
                    V.tensor_tensor(wt_tmp[:, 2], next_pos, end, ALU.is_equal).then_inc(s_wt, 1)
                elif part == 1:
                    dve.wait_ge(s_wt, done + 3)
                    V.tensor_tensor(wt_tmp[:, 0], wt_tmp[:, 0], wt_tmp[:, 1], ALU.subtract).then_inc(s_wt, 1)
                    V.tensor_tensor(wt_tmp[:, 2], wt_tmp[:, 2], extra, ALU.mult).then_inc(s_wt, 1)
                else:
                    dve.wait_ge(s_wt, done + 5)
                    if u.after(8):
                        dve.wait_ge(s_aw, u.n - 4)
                    V.tensor_tensor(wts[:, half], wt_tmp[:, 0], wt_tmp[:, 2], ALU.add).then_inc(s_wt, 1)

            pos_flat = pos_row[:, :, :].rearrange("p k e -> p (k e)")

            def step_dve(s):
                att, ahead = s.has(4), s.has(0)
                if att:
                    u = s.unit(4)
                    d = u.slot % DEEP
                    dve.wait_ge(s_n2, u.n + 1)
                    if u.after(1):
                        dve.wait_ge(s_aw, u.n)
                    V.scalar_tensor_tensor(act2[:, :], neg2[:, d, :], scal[0:TILE, C2:C2 + 1],
                                           ps_h2[0:TILE, 0:LAYER2], ALU.mult, ALU.add).then_inc(s_a2, 1)
                if ahead:
                    v = s.unit(0)
                    e = v.slot % 2
                    if v.after(2):
                        dve.wait_ge(s_oh, v.n - 1)
                    V.tensor_scalar(reached[:, e, 1, :], pos_flat,
                                    seg_rows[:, 1, columns(v.group, 1)],
                                    None, ALU.is_ge).then_inc(s_oh_t, 1)
                if att:
                    dve.wait_ge(s_a2, u.n + 1)
                    V.tensor_tensor(scaled2[:, :].rearrange("p (k h) -> p k h", k=UNIT_TILES),
                                    act2[:, :].rearrange("p (k h) -> p k h", k=UNIT_TILES),
                                    wo_bc[0:TILE, :].rearrange("p (o h) -> p o h", o=1)
                                    .broadcast_to([TILE, UNIT_TILES, H2]), ALU.mult).then_inc(s_m2w, 1)
                if ahead:
                    V.tensor_scalar(reached[:, e, 0, :], pos_flat,
                                    seg_rows[:, 0, columns(v.group, 1)],
                                    None, ALU.is_ge).then_inc(s_oh_t, 1)
                if att:
                    dve.wait_ge(s_m2w, u.n + 1)
                    V.tensor_reduce(att_sum[:, :], scaled2[:, :].rearrange("p (k h) -> p k h", k=UNIT_TILES),
                                    AX_X, ALU.add).then_inc(s_at, 1)
                if ahead:
                    dve.wait_ge(s_oh_t, 2 * v.n + 2)
                    if v.after(DEEP):
                        dve.wait_ge(s_1, v.n - DEEP + 1)
                    V.tensor_tensor(user_of[:, v.slot % DEEP, :], reached[:, e, 0, :],
                                    reached[:, e, 1, :], ALU.subtract).then_inc(s_oh, 1)
                if att:
                    dve.wait_ge(s_at, u.n + 1)
                    dve.wait_ge(s_wt, WT_STEPS * (2 * u.turn + u.slot // 4 + 1))
                    if u.after(DEEP):
                        dve.wait_ge(s_pl, u.n - DEEP + 1)
                    V.scalar_tensor_tensor(
                        att_w[:, d], att_sum[:, :].rearrange("p (k o) -> p k o", o=1)
                        .broadcast_to([TILE, UNIT_TILES, USERS]), scal[0:TILE, BO:BO + 1],
                        wts[0:TILE, u.slot // 4, u.slot % 4], ALU.add, ALU.mult).then_inc(s_aw, 1)
                if s.has(5):
                    u = s.unit(5)
                    dve.wait_ge(s_pl, u.n + 1)
                    dst = pooledT[:, :, columns(u.group, 1)]
                    V.tensor_tensor(dst, dst, ps_pool[:, 0:USERS].rearrange("p (u o) -> p u o", o=1),
                                    ALU.add).then_inc(s_pa, 1)
                if s.has(1):
                    u = s.unit(1)
                    dve.wait_ge(s_cp, u.n + 1)
                    dve.wait_ge(s_tg, u.n + 1)
                    if u.after(DEEP):
                        dve.wait_ge(s_1, u.n - DEEP + 1)
                    V.tensor_tensor(prodT[:, u.slot % DEEP, :], entT[:, u.slot % DEEP, :],
                                    ps_tgt[u.slot % 2][:, 0:UNIT], ALU.mult).then_inc(s_pr, 1)
                if ahead and s.slot % 4 < 3:
                    entry_weights(Step(s.block, s.slot // 4 * 4, s.first_block, s.last).unit(0),
                                  s.slot % 4)
                if s.has(2):
                    u = s.unit(2)
                    d = u.slot % DEEP
                    dve.wait_ge(s_n, u.n + 1)
                    if u.after(DEEP):
                        dve.wait_ge(s_2, u.n - DEEP + 1)
                    V.scalar_tensor_tensor(act1[0:H1, d, :], neg1[:, d, :], scal[0:H1, C1:C1 + 1],
                                           ps_h1[u.slot % 2][0:H1, 0:UNIT], ALU.mult, ALU.add
                                           ).then_inc(s_a1, 1)

            dve.wait_ge(s_segin, 16)
            link(V.tensor_copy(pos_col[:, 0, :], pos_init[:, :]))
            link(V.tensor_scalar(pos_col[:, 1, :], pos_col[:, 0, :], 1.0, None, ALU.add))
            run_pass(dve, step_dve, GROUPS, 0, 5)
            with dve.If(general > 0):
                with dve.Fori(1, PASSES) as p:
                    dve.wait_ge(s_pa, GROUPS * p)
                    V.tensor_scalar(pos_col[:, :, :], pos_col[:, :, :], float(UNIT), None,
                                    ALU.add).then_inc(s_pos, 1)
                    V.tensor_scalar(seg_rows[:, :, :], seg_rows[:, :, :], -float(UNIT), None,
                                    ALU.add).then_inc(s_pos, 1)
                    dve.wait_ge(s_pos, 2 * p)
                    run_pass(dve, step_dve, GROUPS, p * (GROUPS // RING), 5)
                dve.wait_ge(s_pa, GROUPS * PASSES)
            with dve.Else():
                dve.wait_ge(s_pa, GROUPS)
            dve.sem_inc(s_main_dve, 1)

            def norm(P, cols, bnp, var_ready, root_ready, bn_ready):
                v = bnv[0:P, cols, :]
                link(V.tensor_scalar(v[:, :, 0], aggr[0:P, cols, 1], BN_EPS, None, ALU.add))
                dve.sem_inc(var_ready, 1)
                link(V.tensor_tensor(v[:, :, 5], aggr[0:P, cols, 0], bnp[:, 0], ALU.add))
                link(V.tensor_tensor(v[:, :, 5], v[:, :, 5], bnp[:, 0], ALU.subtract))
                dve.wait_ge(root_ready, 1)
                link(V.reciprocal(v[:, :, 2], v[:, :, 1]))
                link(V.tensor_tensor(v[:, :, 3], v[:, :, 2], v[:, :, 2], ALU.mult))
                link(V.tensor_tensor(v[:, :, 3], v[:, :, 3], v[:, :, 0], ALU.mult))
                link(V.tensor_scalar(v[:, :, 3], v[:, :, 3], -0.5, 1.5, ALU.mult, ALU.add))
                link(V.tensor_tensor(v[:, :, 3], v[:, :, 3], v[:, :, 2], ALU.mult))
                link(V.tensor_tensor(v[:, :, 4], v[:, :, 3], bnp[:, 1], ALU.mult))
                link(V.tensor_tensor(v[:, :, 3], v[:, :, 4], v[:, :, 5], ALU.mult))
                link(V.tensor_tensor(v[:, :, 5], bnp[:, 2], v[:, :, 3], ALU.subtract))
                link(V.tensor_scalar(v[:, :, 6:8], v[:, :, 4:6], -1.0, None, ALU.mult))
                dve.sem_inc(bn_ready, 1)

            def prelu(z, neg, bank, col, P, c1, done):
                link(V.tensor_scalar(z, neg, c1, bnv[0:P, col, 5:6], ALU.mult, ALU.add))
                V.scalar_tensor_tensor(z, bank[0:P, :], bnv[0:P, col, 4:5], z,
                                       ALU.mult, ALU.add).then_inc(done, 1)

            dve.wait_ge(s_mlpw, 16 * 15)
            for i in range(2 * NCH):
                c, h = divmod(i, 2)
                dve.wait_ge(s_m1, i + 1)
                V.bn_stats(stats[0:MH, h, c, :], mlp_banks[i][0:MH, :]).then_inc(s_d, 1)
            steps[0] += 2 * NCH
            dve.wait_ge(s_d, steps[0])
            for h in range(2):
                link(V.bn_aggr(aggr[0:MH, h, :], stats[0:MH, h, :, :].rearrange("p c s -> p (c s)")))
            norm(MH, slice(0, 2), bnp1[:, :, :], s_v1, s_sq1, s_bn1)
            slope = scal[0:MH, CM1:CM1 + 1]
            for c in range(NCH):
                z, neg = (buf[:, :, c * CH:(c + 1) * CH] for buf in (z1, z1n))
                dve.wait_ge(s_n1, 2 * c + 2)
                prelu(z[:, 1], neg[:, 1], mlp_banks[2 * c + 1], 1, MH, slope, s_z1)
                dve.wait_ge(s_v1n, c + 1)
                V.scalar_tensor_tensor(z[:, 0], neg[:, 0], slope, z[:, 0],
                                       ALU.mult, ALU.add).then_inc(s_z1, 1)
            for c in range(NCH):
                dve.wait_ge(s_m2, c + 1)
                V.bn_stats(stats[0:M2, 2, c, :], mlp_banks[2 * c][0:M2, :]).then_inc(s_d, 1)
            steps[0] += NCH
            dve.wait_ge(s_d, steps[0])
            link(V.bn_aggr(aggr[0:M2, 2, :], stats[0:M2, 2, :, :].rearrange("p c s -> p (c s)")))
            norm(M2, slice(2, 3), bnp2[:, :].rearrange("p (c o) -> p c o", o=1), s_v2, s_sq2, s_bn2)
            slope = scal[0:M2, CM2:CM2 + 1]
            for c in range(NCH):
                z, neg = (buf[:, c * CH:(c + 1) * CH] for buf in (z2, z2n))
                dve.wait_ge(s_nz2, c + 1)
                if c % 2 == 0:
                    prelu(z, neg, mlp_banks[2 * c], 2, M2, slope, s_z2)
                else:
                    dve.wait_ge(s_v2n, c // 2 + 1)
                    V.scalar_tensor_tensor(z, neg, slope, z, ALU.mult, ALU.add).then_inc(s_z2, 1)
            dve.wait_ge(s_lg, 1)
            K = TILES * USERS
            V.tensor_tensor(probs[:, :, :], ps_pool[:, 0:2 * K].rearrange("p (k c) -> p k c", c=2),
                            ob_sb[:, :].rearrange("p (o c) -> p o c", o=1).broadcast_to([128, K, 2]),
                            ALU.add).then_inc(s_sh, 1)
            dve.wait_ge(s_sh, 1)
            V.tensor_tensor(lmax[:, 0, :], probs[:, :, 0], probs[:, :, 1], ALU.max).then_inc(s_sh, 1)
            dve.wait_ge(s_sh, 2)
            V.tensor_tensor(probs[:, :, :], probs[:, :, :],
                            lmax[:, 0, :].rearrange("p (k o) -> p k o", o=1).broadcast_to([128, K, 2]),
                            ALU.subtract).then_inc(s_sh, 1)
            dve.wait_ge(s_ex, 1)
            link(V.tensor_tensor(lmax[:, 0, :], probs[:, :, 0], probs[:, :, 1], ALU.add))
            link(V.reciprocal(lmax[:, 1, :], lmax[:, 0, :]))
            V.tensor_tensor(probs[:, :, :], probs[:, :, :],
                            lmax[:, 1, :].rearrange("p (k o) -> p k o", o=1).broadcast_to([128, K, 2]),
                            ALU.mult).then_inc(s_pb, 1)


_INS = ['r_rowData', 'L0_rec_movieFeature', 'L0_rec_emb_movie', 'L0_rec_emb_genre',
        'L0_rec_att_w1', 'L0_rec_att_b1', 'L0_rec_att_a1', 'L0_rec_att_w2', 'L0_rec_att_b2',
        'L0_rec_att_a2', 'L0_rec_att_wo', 'L0_rec_att_bo', 'L0_rec_mlp_w1', 'L0_rec_mlp_b1',
        'L0_rec_bn1_g', 'L0_rec_bn1_b', 'L0_rec_mlp_a1', 'L0_rec_mlp_w2', 'L0_rec_mlp_b2',
        'L0_rec_bn2_g', 'L0_rec_bn2_b', 'L0_rec_mlp_a2', 'L0_rec_out_w', 'L0_rec_out_b']


def kernel(**inputs):
    import numpy as np
    import concourse.bacc as bacc
    from concourse.bass_utils import run_bass_kernel_spmd

    nc = bacc.Bacc("TRN2", target_bir_lowering=False, num_devices=1)
    arrays, args = {}, []
    for name in _INS:
        a = np.ascontiguousarray(inputs[name])
        if a.ndim == 0:
            a = a.reshape(1)
        arrays[f"in_{name}"] = a
        args.append(nc.dram_tensor(f"in_{name}", a.shape, mybir.dt.from_np(a.dtype),
                                   kind="ExternalInput").ap())
    out = nc.dram_tensor("out_0", (inputs['r_rowData'].shape[0], 2), F32, kind="ExternalOutput").ap()
    build(nc, *args, out)
    r = run_bass_kernel_spmd(nc, [arrays], core_ids=[0])
    return r.results[0]["out_0"]
```

```python
from contextlib import ExitStack

import concourse.bass as bass
from concourse import mybir
from concourse.alu_op_type import AluOpType as ALU

ACT = mybir.ActivationFunctionType
F32 = mybir.dt.float32
BF16 = mybir.dt.bfloat16
F16 = mybir.dt.float16
I32 = mybir.dt.int32
U32 = mybir.dt.uint32
AX_X = mybir.AxisListType.X

USERS = 8
HALVES = 2
PARTS = 3
CHUNKS = (4, 4, 3)
GTILES = sum(CHUNKS)
TILE = 128
LAST_TILE = 84
FULL = GTILES - 1
SHORT = TILE * FULL
CAP = SHORT + LAST_TILE
WIDE = TILE * max(CHUNKS)
RUN = 64
PAD = RUN
DEEP = 3
SLOTS_G = 4
RING = SLOTS_G * len(CHUNKS)
BN_EPS = 1e-5
POOL_EPS = 1e-8


class Step:

    def __init__(self, block, slot, first_block, last):
        self.block, self.slot, self.first_block, self.last = block, slot, first_block, last

    def has(self, lag):
        if not isinstance(self.block, int):
            return True
        return 0 <= RING * self.block + self.slot - lag < self.last

    def unit(self, lag):
        return Unit(self.block - (self.slot < lag), (self.slot - lag) % RING, self.first_block)


class Unit:

    def __init__(self, block, slot, first_block):
        self.slot = slot
        self.gslot, self.chunk = divmod(slot, len(CHUNKS))
        self.tiles = CHUNKS[self.chunk]
        self.first_tile = sum(CHUNKS[:self.chunk])
        self.has_last = self.first_tile + self.tiles == GTILES
        self.sizes = [TILE] * (self.tiles - 1) + [LAST_TILE if self.has_last else TILE]
        self.width = sum(self.sizes)
        self.full_tiles = self.tiles - self.has_last
        self.first_pass = isinstance(first_block, int)
        self.group = SLOTS_G * block + self.gslot
        self.turn = block + first_block
        self.n = RING * self.turn + slot
        self.g = SLOTS_G * self.turn + self.gslot

    def after(self, depth):
        return not isinstance(self.n, int) or self.n >= depth

    def group_after(self, depth):
        return not isinstance(self.g, int) or self.g >= depth


def columns(first, n):
    return slice(first, first + n) if isinstance(first, int) else bass.ds(first, n)


def for_length(pe, is_long, u, work):
    if not (u.has_last and u.first_pass):
        work(u.sizes)
        return
    with pe.If(is_long > 0):
        work(u.sizes)
    with pe.Else():
        work(u.sizes[:-1])


def run_pass(eng, step, units, first_block, lag):
    run_steps(eng, step, units, first_block)
    for s in range(lag):
        step(Step(units // RING, s, first_block, units))


def run_steps(eng, step, units, first_block):
    for s in range(RING):
        step(Step(0, s, first_block, units))
    with eng.Fori(1, units // RING) as block:
        for s in range(RING):
            step(Step(block, s, first_block, units))


def build(nc, rows, movie_feature, emb_movie, emb_genre, att_w1, att_b1, att_a1, att_w2, att_b2,
          att_a2, att_wo, att_bo, mlp_w1, mlp_b1, bn1_g, bn1_b, mlp_a1, mlp_w2, mlp_b2, bn2_g,
          bn2_b, mlp_a2, out_w, out_b, out):
    B, NCOL = rows.shape
    T = NCOL - 2
    N_ROWS, FEATS = movie_feature.shape
    GENRES = FEATS - 1
    VOCAB, E = emb_genre.shape
    D = 2 * E
    H1, H2 = att_w2.shape
    M1, M2 = mlp_w2.shape
    TILES = B // (USERS * 128)
    SLOTS = TILES * USERS
    GUSERS = HALVES * SLOTS
    GROUPS = 128 // HALVES
    HALF = 128 // HALVES
    UNITS = GROUPS * len(CHUNKS)
    LAST_ROW = N_ROWS - 1
    PASSES = -(-GUSERS * T // CAP)
    REGION = PAD + (PASSES - 1) * CAP + SHORT + 128
    ONE = H1
    LAYER2 = max(CHUNKS) * H2
    BATCHES = TILES * 2
    HROWS = SLOTS * PARTS
    UROWS = HALF + HROWS
    TP = 125
    TK = N_ROWS // TP
    KB = 5
    PIECE_ENDS = tuple(range(2 * KB, TK + 1, 2 * KB))
    MH = M1 // 2
    NCH = 4
    CH = B // NCH
    TC = D + H1
    assert B % (USERS * 128) == 0 and HROWS <= HALF and N_ROWS == TP * TK and D == 128 and PIECE_ENDS[-1] == TK

    list_dram = nc.dram_tensor("list_dram", [GROUPS * REGION, 1], U32, kind="Internal").ap()
    table_dram = nc.dram_tensor("table_dram", [N_ROWS, D], F32, kind="Internal").ap()
    seg_dram = nc.dram_tensor("seg_dram", [GROUPS, 3, GUSERS], F32, kind="Internal").ap()
    tc_dram = nc.dram_tensor("tc_dram", [GROUPS, HALVES, HROWS, TC], BF16, kind="Internal").ap()
    list_by_group = list_dram.rearrange("(g e) o -> g (e o)", e=REGION)

    with ExitStack() as ctx:
        def sb(name, shape, dt=F32):
            return ctx.enter_context(nc.sbuf_tensor(name, shape, dt))

        def bank(name, shape=(128, 512), dt=F32):
            return ctx.enter_context(nc.psum_tensor(name, list(shape), dt))

        def sem(name):
            return ctx.enter_context(nc.semaphore(name))

        rows_sb = sb("rows_sb", [128, TILES, USERS, NCOL], I32)
        idx_sb = sb("idx_sb", [128, TILES, USERS, NCOL], U32)
        key_sb = sb("key_sb", [128, TILES, USERS, NCOL])
        work = sb("work", [128, TILES, T])
        best = sb("best", [128, TILES, RUN])
        run_idx = sb("run_idx", [128, SLOTS, RUN], U32)
        count = sb("count", [128, SLOTS])
        before = sb("before", [128, SLOTS + 1])
        group_before = sb("group_before", [128, 1])
        seg_sb = sb("seg_sb", [128, 3, SLOTS])
        rep_sb = sb("rep_sb", [128, 2, SLOTS, PARTS])
        seg_rows = sb("seg_rows", [UROWS, 2, GROUPS])
        seg_all = sb("seg_all", [128, GROUPS, 3, GUSERS])
        scatter_to = sb("scatter_to", [128, SLOTS], U32)
        small = sb("small", [128, 4, SLOTS])
        flag_col = sb("flag_col", [128, 1])
        flag_i = sb("flag_i", [1, 1], I32)
        long_col = sb("long_col", [128, 1])
        long_i = sb("long_i", [1, GROUPS], I32)
        last_count = sb("last_count", [1, GROUPS])
        last_i = sb("last_i", [1, GROUPS], I32)
        group_base = sb("group_base", [128, 1], I32)
        plain_start = sb("plain_start", [128, SLOTS], I32)
        ident_wide = sb("ident_wide", [128, HALF + 128])
        ident = ident_wide[:, HALF:HALF + 128]
        ones_col = sb("ones_col", [128, 1])

        feat_sb = sb("feat_sb", [TP, TK, FEATS], I32)
        feat_f = sb("feat_f", [TP, 2, TK, FEATS])
        movie_idx = sb("movie_idx", [TP, TK], U32)
        genre_bf = sb("genre_bf", [TP, GENRES, TK], BF16)
        planes = VOCAB // 2 * GENRES * TK
        genre_area = sb("genre_is", [128, max(planes, 2 * 2 * DEEP * WIDE)], BF16)
        genre_whole = genre_area[:, 0:planes].rearrange("p (v j k) -> p v j k", v=VOCAB // 2, j=GENRES)
        genre_is = genre_whole[0:TP]
        genre_cnt = sb("genre_cnt", [TP, TK, VOCAB])
        genre_cntT = sb("genre_cntT", [KB * VOCAB, 2, TP])
        genre_blocks = sb("genre_blocks", [KB * VOCAB, KB * E])
        genre_len = sb("genre_len", [TP, 2, TK])
        table_whole = sb("table_sb", [128, TK, D])
        table_sb = table_whole[0:TP]

        w1_sb = sb("w1_sb", [D, 3, H1])
        b1_bc = sb("b1_bc", [128, H1])
        w2_sb = sb("w2_sb", [H1 + 1, H2])
        wo_bc = sb("wo_bc", [128, H2])
        scal = sb("scal", [128, 9])
        A1, A2, AM1, AM2, BO, C1, C2, CM1, CM2 = range(9)

        adsT = sb("adsT", [D, SLOTS, 128])

        idx_ring = sb("idx_ring", [128, SLOTS_G, GTILES], U32)
        tc_ring = sb("tc_ring", [UROWS, SLOTS_G, TC], BF16)
        pos_row = sb("pos_row", [UROWS, CAP], F16)
        pos_init = sb("pos_init", [128, GTILES])
        pos_col = sb("pos_col", [128, 2, GTILES])
        reached = sb("reached", [UROWS, 2, 2, WIDE], BF16)
        user_of = sb("user_of", [UROWS, DEEP, WIDE], BF16)
        wts = sb("wts", [128, 2, GTILES, GUSERS], F16)
        wt_tmp = sb("wt_tmp", [128, 3, GTILES, GUSERS], F16)
        extra_all = sb("extra_all", [128, GROUPS, GUSERS], F16)
        two = [whole.bitcast(F32)[:, i * DEEP * WIDE:(i + 1) * DEEP * WIDE]
               .rearrange("p (r e) -> p r e", r=DEEP)
               for whole in (key_sb[:, :, :, :].rearrange("p t u c -> p (t u c)"),
                             genre_area)
               for i in range(2)]
        entT, prodT, neg1, act1 = two[0], two[1], two[2][0:H1], two[3][0:H1 + 1]
        neg2 = sb("neg2", [TILE, DEEP, LAYER2])
        act2 = sb("act2", [TILE, LAYER2])
        scaled2 = sb("scaled2", [TILE, LAYER2])
        att_sum = sb("att_sum", [TILE, max(CHUNKS)])
        att_w = sb("att_w", [TILE, DEEP, max(CHUNKS), GUSERS])
        pooledT = sb("pooledT", [D, SLOTS, HALVES, GROUPS])

        m1_sb = sb("m1_sb", [D, 2, M1])
        m2_sb = sb("m2_sb", [MH, 2, M2])
        bnp1 = sb("bnp1", [MH, 3, 2])
        bnp2 = sb("bnp2", [M2, 3])
        ow_sb = sb("ow_sb", [M2, 2])
        ob_sb = sb("ob_sb", [128, 2])
        stats = sb("stats", [128, 3, NCH, 6])
        aggr = sb("aggr", [128, 3, 2])
        bnv = sb("bnv", [128, 3, 8])
        probs = sb("probs", [128, TILES * USERS, 2])
        lmax = sb("lmax", [128, 2, TILES * USERS])
        arena = table_whole[:, :, :].rearrange("p k d -> p (k d)")
        ring_half = SLOTS_G // 2 * GTILES * D
        sizes = [4 * BATCHES * TC, 4 * 2 * TC, 4 * BATCHES * PARTS * TC // 2, ring_half]
        at = [sum(sizes[:i]) for i in range(5)]
        tc_val = arena[:, at[0]:at[1]].rearrange("p (b u c) -> p b u c", b=BATCHES, u=4)
        tc_res = arena[:, at[1]:at[2]].rearrange("p (b u c) -> p b u c", b=2, u=4)
        entries = [half.rearrange("p (r k d) -> p r k d", r=SLOTS_G // 2, k=GTILES)[:, i]
                   for half in (rows_sb[:, :, :, :].rearrange("p t u c -> p (t u c)")
                                .bitcast(F32)[:, 0:ring_half], arena[:, at[3]:at[4]])
                   for i in range(SLOTS_G // 2)]
        tc_parts = arena[:, at[2]:at[3]].bitcast(BF16).rearrange(
            "p (b u s c) -> p b u s c", b=BATCHES, u=4, s=PARTS)
        z1 = arena[0:MH, 0:2 * B].rearrange("p (h b) -> p h b", h=2)
        z1n = arena[0:MH, 2 * B:4 * B].rearrange("p (h b) -> p h b", h=2)
        z2 = arena[0:M2, 4 * B:5 * B]
        z2n = arena[0:M2, 5 * B:6 * B]

        ps_ent = [bank("ps_ent0"), bank("ps_ent1")]
        ps_tgt = [bank("ps_tgt0"), bank("ps_tgt1")]
        ps_h1 = [bank("ps_h1a"), bank("ps_h1b")]
        ps_h2 = bank("ps_h2")
        ps_pool = bank("ps_pool")

        mlp_banks = ps_ent + ps_tgt + ps_h1 + [ps_h2, ps_pool]

        EMB, SHARE = 0, 1
        cols = (slice(0, D), slice(D, TC))

        s_rows = sem("rows_in")
        s_feat = sem("feat_in")
        s_w = sem("weights_in")
        s_wsc = sem("weights_scaled")
        s_mlpw = sem("mlp_weights_in")
        s_const = sem("constants_made")
        s_ident = sem("identity_zeroed")
        s_d = sem("vector_steps")
        s_idx = sem("row_numbers_made")
        s_seg = sem("segments_made")
        s_movie = sem("movie_numbers_made")
        s_cnt = sem("genre_counts_made")
        s_blocks = sem("genre_blocks_in")
        s_blkz = sem("genre_blocks_zeroed")
        s_listp = sem("plain_lists_out")
        s_segout = sem("segments_out")
        s_segin = sem("segments_in")
        s_flag_ps = sem("flag_summed")
        s_flag = sem("flag_ready")
        s_segT = sem("segments_turned")
        s_segrow = sem("segment_rows_ready")
        s_runs = sem("runs_sorted")
        s_scat = sem("runs_out")
        s_tabrow = [sem(f"table_movies{q}") for q in range(len(PIECE_ENDS))]
        s_cT = sem("counts_turned")
        s_cTc = sem("counts_copied")
        s_gps = sem("genre_products")
        s_gev = sem("genre_halves_written")
        s_table = sem("table_out")
        s_ads = [sem(f"ads_gathered{t}") for t in range(TILES)]
        s_adsps = sem("ads_turned")
        s_adsT = sem("ads_copied")
        s_cps = sem("target_share_products")
        s_tcv = sem("target_shares_ready")
        s_hi, s_rest, s_mid, s_lo = ([sem(f"target_{what}_{of}") for of in ("embedding", "share")]
                                     for what in ("first_part", "rest", "second_part", "last_part"))
        s_tcout = sem("target_parts_out")

        s_ix = [sem(f"group_index{k}") for k in range(SLOTS_G)]
        s_tc = [sem(f"group_target{k}") for k in range(SLOTS_G)]
        s_last = [sem(f"last_tile{k}") for k in range(SLOTS_G)]
        s_long = sem("last_counts_ready")
        s_g = [sem(f"unit_entries{k}") for k in range(RING)]
        s_begun = sem("unit_gathers_begun")
        s_oh_t = sem("reached_made")
        s_pe = sem("stages_begun")
        s_load = sem("group_loads_begun")
        s_sign = sem("reached_begun")
        s_total = sem("totals_made")
        s_before = sem("totals_moved")
        s_oh = sem("user_matrix_made")
        s_wt = sem("weight_steps")
        s_T = sem("entries_turned")
        s_tg = sem("targets_spread")
        s_cp = sem("entries_copied")
        s_pr = sem("products_made")
        s_1 = sem("layer1_summed")
        s_n = sem("layer1_negated")
        s_a1 = sem("layer1_done")
        s_2 = sem("layer2_summed")
        s_n2 = sem("layer2_negated")
        s_a2 = sem("layer2_done")
        s_m2w = sem("layer2_scaled")
        s_at = sem("attention_summed")
        s_aw = sem("attention_weighted")
        s_pl = sem("pool_summed")
        s_pa = sem("pool_added")
        s_pos = sem("positions_moved")
        s_main_dve = sem("vector_main_done")

        s_m1 = sem("mlp1_summed")
        s_p1 = sem("mlp1_shifted")
        s_v1 = sem("norm1_variance")
        s_sq1 = sem("norm1_root")
        s_bn1 = sem("norm1_ready")
        s_n1 = sem("mlp1_negated")
        s_z1 = sem("mlp1_done")
        s_m2 = sem("mlp2_summed")
        s_p2 = sem("mlp2_shifted")
        s_v2 = sem("norm2_variance")
        s_sq2 = sem("norm2_root")
        s_bn2 = sem("norm2_ready")
        s_nz2 = sem("mlp2_negated")
        s_z2 = sem("mlp2_done")
        s_lg = sem("logits_summed")
        s_sh = sem("logits_shifted")
        s_ex = sem("exponentials")
        s_pb = sem("probabilities")
        s_out = sem("output_out")

        N_CONST = 9
        N_W = 10
        block = ctx.enter_context(nc.Block())

        @block.sync
        def _(sp):
            rows_v = rows.rearrange("(t p u) c -> t p (u c)", t=TILES, u=USERS)
            sp.dma_start(feat_sb[:, :, :].rearrange("p k c -> p (k c)"),
                         movie_feature.rearrange("(p k) c -> p (k c)", p=TP)).then_inc(s_feat, 16)
            for t in range(TILES):
                sp.dma_start(rows_sb[:, t, :, :].rearrange("p u c -> p (u c)"),
                             rows_v[t]).then_inc(s_rows, 16)
            sp.wait_ge(s_blkz, 1)
            for i in range(KB):
                sp.dma_start(genre_blocks[i * VOCAB:(i + 1) * VOCAB, i * E:(i + 1) * E],
                             emb_genre).then_inc(s_blocks, 16)

            sp.wait_ge(s_idx, TILES)
            for t in range(TILES):
                for h in range(HALVES):
                    at = PAD + (h * SLOTS + t * USERS) * T
                    sp.dma_start(list_by_group[:, at:at + USERS * T].rearrange("g (u e) -> g u e", u=USERS),
                                 idx_sb[h * HALF:(h + 1) * HALF, t, :, 1:1 + T]).then_inc(s_listp, 16)
            filled = PAD + GUSERS * T
            sp.dma_start(list_by_group[:, filled:REGION],
                         idx_sb[0:GROUPS, 0, :, :].rearrange("p u c -> p (u c)")[:, 0:REGION - filled]
                         ).then_inc(s_listp, 16)

            sp.wait_ge(s_seg, 1)
            for h in range(HALVES):
                sp.dma_start(seg_dram[:, :, h * SLOTS:(h + 1) * SLOTS],
                             seg_sb[h * HALF:(h + 1) * HALF, :, :]).then_inc(s_segout, 16)
            sp.wait_ge(s_segout, 16 * HALVES)
            sp.dma_start(seg_all[:, :, :, :].rearrange("p g s u -> p (g s u)"),
                         seg_dram.rearrange("(o g) s u -> o (g s u)", o=1)
                         .broadcast_to([128, GROUPS * 3 * GUSERS])).then_inc(s_segin, 16)

            table_v = table_dram.rearrange("(p k) d -> p (k d)", p=TP)
            for q, end in enumerate(PIECE_ENDS):
                first = PIECE_ENDS[q - 1] if q else 0
                sp.wait_ge(s_tabrow[q], 16 * (end - first))
                sp.wait_ge(s_gev, end // KB)
                sp.dma_start(table_v[:, first * D:end * D],
                             table_sb[:, first:end, :].rearrange("p k d -> p (k d)")
                             ).then_inc(s_table, 16)

            def load_index(u, chunk):
                group = list_by_group[columns(u.group, 1), :]
                sp.dma_start(idx_ring[:, u.gslot, 0:FULL],
                             group[:, columns(chunk * CAP + PAD, 128 * FULL)]
                             .rearrange("g (p k) -> (g p) k", p=128)).then_inc(s_ix[u.gslot], 16)
                sp.dma_start(idx_ring[:, u.gslot, FULL:GTILES],
                             group[:, columns(chunk * CAP + (PAD + SHORT), 128)]
                             .rearrange("g (p k) -> (g p) k", p=128)).then_inc(s_ix[u.gslot], 16)

            def load_targets(u):
                for h in range(HALVES):
                    sp.dma_start(tc_ring[h * HALF:h * HALF + HROWS, u.gslot, :],
                                 tc_dram[columns(u.group, 1), h].rearrange("g r c -> (g r) c")
                                 ).then_inc(s_tc[u.gslot], 16)

            first_units = [Unit(0, k * len(CHUNKS), 0) for k in range(SLOTS_G)]
            sp.wait_ge(s_scat, 16 * SLOTS)
            for u in first_units:
                load_index(u, 0)

            for kind in (EMB, SHARE):
                sp.wait_ge(s_lo[kind], BATCHES)
            for u in first_units:
                for h in range(HALVES):
                    p = h * HALF + u.group
                    sp.dma_start(tc_ring[h * HALF:h * HALF + HROWS, u.gslot, :],
                                 tc_parts[p:p + 1].rearrange("p b u s c -> p (b u s) c")
                                 ).then_inc(s_tc[u.gslot], 16)
            for h in range(HALVES):
                sp.dma_start(tc_dram[:, h].rearrange("g r c -> g (r c)"),
                             tc_parts[h * HALF:(h + 1) * HALF].rearrange("p b u s c -> p (b u s c)")
                             ).then_inc(s_tcout, 16)
            sp.wait_ge(s_tcout, 16 * HALVES)
            sp.wait_ge(s_flag, 1)
            general = sp.value_load(flag_i[0:1, 0:1], min_val=0, max_val=128)

            def step_sp(s, chunk):
                u = s.unit(0)
                if s.has(0) and u.chunk == 0 and u.after(RING):
                    sp.wait_ge(s_1, u.n - RING + len(CHUNKS))
                    sp.sem_inc(s_load, 1)
                    load_index(u, chunk)
                    load_targets(u)

            run_pass(sp, lambda s: step_sp(s, 0), UNITS, 0, 0)
            with sp.If(general > 0):
                with sp.Fori(1, PASSES) as p:
                    run_pass(sp, lambda s: step_sp(s, p), UNITS, p * (UNITS // RING), 0)
            with sp.Else():
                sp.nop()

            sp.wait_ge(s_pb, 1)
            sp.dma_start(out.rearrange("(t p u) c -> p t (u c)", t=TILES, u=USERS),
                         probs[:, :, :].rearrange("p (t u) c -> p t (u c)", t=TILES)
                         ).then_inc(s_out, 16)
            sp.wait_ge(s_out, 16)

        @block.gpsimd
        def _(pool):
            pool.memset(genre_blocks[:, :], 0.0).then_inc(s_blkz, 1)
            pool.memset(ident_wide[:, :], 0.0).then_inc(s_ident, 1)
            pool.wait_ge(s_ident, 1)
            pool.affine_select(out=ident_wide[:, :], in_=ident_wide[:, :], compare_op=ALU.not_equal,
                               fill=1.0, base=HALF, pattern=[[-1, HALF + 128]],
                               channel_multiplier=1).then_inc(s_const, 1)
            pool.memset(ones_col[:, :], 1.0).then_inc(s_const, 1)
            pool.memset(pooledT[:, :, :, :], 0.0).then_inc(s_const, 1)
            pool.iota(group_base[:, :], pattern=[[0, 1]], channel_multiplier=REGION).then_inc(s_const, 1)
            pool.iota(plain_start[:, :], pattern=[[T, SLOTS]], channel_multiplier=0).then_inc(s_const, 1)
            for pos, tiles, patterns, first in (
                    (pos_init[:, 0:FULL], FULL, [[1, FULL]], 0),
                    (pos_init[:, FULL:GTILES], 1, [[0, 1]], SHORT),
                    (pos_row[:, 0:SHORT], 0, [[1, FULL], [FULL, TILE]], 0),
                    (pos_row[:, SHORT:CAP], 0, [[1, LAST_TILE]], SHORT)):
                pool.iota(pos, pattern=patterns, base=first, channel_multiplier=tiles,
                          allow_small_or_imprecise_dtypes=True).then_inc(s_const, 1)

            def gather_movies(k):
                pool.indirect_dma_start(
                    out=table_sb[:, k, 0:E], out_offset=None, in_=emb_movie,
                    in_offset=bass.IndirectOffsetOnAxis(ap=movie_idx[:, k:k + 1], axis=0),
                ).then_inc(s_tabrow[sum(k >= end for end in PIECE_ENDS)], 16)

            def scatter_run(j):
                pool.wait_ge(s_runs, 2 * (j + 1))
                if j:
                    pool.wait_ge(s_scat, 16 * j)
                pool.indirect_dma_start(
                    out=list_dram,
                    out_offset=bass.IndirectOffsetOnAxis(ap=scatter_to[:, j:j + 1], axis=0),
                    in_=run_idx[:, j, :], in_offset=None).then_inc(s_scat, 16)

            def gather_target(t, u):
                pool.indirect_dma_start(
                    out=tc_val[:, 2 * t + u // 4, u % 4, 0:D], out_offset=None, in_=table_dram,
                    in_offset=bass.IndirectOffsetOnAxis(ap=idx_sb[:, t, u, NCOL - 1:NCOL], axis=0),
                ).then_inc(s_ads[t], 16)

            between = [3, 4] * 6 + [3, 5] * 2
            assert len(between) == TILES * USERS
            movies_between = sum(between[:12])
            assert sum(between[12:]) == TILES * USERS
            early = TK - movies_between
            pool.wait_ge(s_movie, 1)
            for k in range(early):
                gather_movies(k)
            pool.wait_ge(s_flag, 1)
            general = pool.value_load(flag_i[0:1, 0:1], min_val=0, max_val=128)
            pool.wait_ge(s_listp, 16 * (HALVES * TILES + 1))
            with pool.If(general > 0):
                for k in range(early, TK):
                    gather_movies(k)
                pool.wait_ge(s_table, 16 * len(PIECE_ENDS))
                for i in range(TILES * USERS):
                    gather_target(*divmod(i, USERS))
                pool.sem_inc(s_scat, 16 * SLOTS)
            with pool.Else():
                k = early
                target = 0
                for i in range(TILES * USERS):
                    scatter_run(i)
                    if i == 12:
                        pool.wait_ge(s_table, 16 * len(PIECE_ENDS))
                    for _ in range(between[i]):
                        if i < 12:
                            gather_movies(k)
                            k += 1
                        else:
                            gather_target(*divmod(target, USERS))
                            target += 1

            def step_pool(s):
                if s.has(0):
                    u = s.unit(0)
                    if u.chunk == 0:
                        pool.wait_ge(s_ix[u.gslot], 32 * (u.turn + 1))
                    if u.after(RING):
                        pool.wait_ge(s_pl, u.n - RING + 1)
                    pool.sem_inc(s_begun, 1)

                    def gather(k, landed):
                        pool.indirect_dma_start(
                            out=entries[u.gslot][:, k, :], out_offset=None, in_=table_dram,
                            in_offset=bass.IndirectOffsetOnAxis(ap=idx_ring[:, u.gslot, k:k + 1], axis=0),
                        ).then_inc(landed, 16)

                    for k in range(u.first_tile, u.first_tile + u.full_tiles):
                        gather(k, s_g[u.slot])

                    if u.has_last and u.first_pass:
                        is_long = pool.value_load(long_i[0:1, columns(u.group, 1)], min_val=0, max_val=1)
                        with pool.If(is_long > 0):
                            gather(FULL, s_last[u.gslot])
                        with pool.Else():
                            pool.nop()
                    elif u.has_last:
                        gather(FULL, s_last[u.gslot])

            pool.wait_ge(s_segrow, 1)
            run_pass(pool, step_pool, UNITS, 0, 0)
            with pool.If(general > 0):
                with pool.Fori(1, PASSES) as p:
                    run_pass(pool, step_pool, UNITS, p * (UNITS // RING), 0)
            with pool.Else():
                pool.nop()

            pool.wait_ge(s_bn1, 1)
            for i in range(2 * NCH):
                c, h = divmod(i, 2)
                pool.wait_ge(s_n1, i + 1)
                pool.tensor_scalar(z1[:, h, c * CH:(c + 1) * CH], z1n[:, h, c * CH:(c + 1) * CH],
                                   scal[0:MH, CM1:CM1 + 1], bnv[0:MH, h, 5:6],
                                   ALU.mult, ALU.add).then_inc(s_p1, 1)
            pool.wait_ge(s_bn2, 1)
            for c in range(NCH):
                pool.wait_ge(s_nz2, c + 1)
                pool.tensor_scalar(z2[:, c * CH:(c + 1) * CH], z2n[:, c * CH:(c + 1) * CH],
                                   scal[0:M2, CM2:CM2 + 1], bnv[0:M2, 2, 5:6],
                                   ALU.mult, ALU.add).then_inc(s_p2, 1)

        @block.scalar
        def _(act):
            def load(dst, src, s):
                act.dma_start(dst, src).then_inc(s, 16)

            def col(v):
                return v.rearrange("(p o) -> p o", o=1)

            load(w1_sb[:, :, :], att_w1.rearrange("(s p) h -> p s h", p=D), s_w)
            load(b1_bc[:, :], att_b1.rearrange("(o h) -> o h", o=1).broadcast_to([128, H1]), s_w)
            for c, v in ((A1, att_a1), (A2, att_a2), (AM1, mlp_a1), (AM2, mlp_a2), (BO, att_bo)):
                load(scal[:, c:c + 1], v.rearrange("(o h) -> o h", o=1).broadcast_to([128, 1]), s_w)
            load(w2_sb[0:H1, :], att_w2, s_w)
            load(w2_sb[ONE:ONE + 1, :], att_b2.rearrange("(o h) -> o h", o=1), s_w)
            load(wo_bc[:, :], att_wo.rearrange("h o -> o h").broadcast_to([128, H2]), s_w)

            for i in range(TK // KB):
                act.wait_ge(s_cT, i + 1)
                if i >= 2:
                    act.wait_ge(s_gps, i - 1)
                act.activation(genre_cntT[:, i % 2, :], ps_ent[i % 2][0:KB * VOCAB, 0:TP],
                               ACT.Copy).then_inc(s_cTc, 1)

            for h in range(2):
                load(m1_sb[:, h, :], mlp_w1[h * D:(h + 1) * D, :], s_mlpw)
                load(m2_sb[:, h, :], mlp_w2[h * MH:(h + 1) * MH, :], s_mlpw)
                for c, v in enumerate((mlp_b1, bn1_g, bn1_b)):
                    load(bnp1[:, c, h:h + 1], col(v[h * MH:(h + 1) * MH]), s_mlpw)
            for c, v in enumerate((mlp_b2, bn2_g, bn2_b)):
                load(bnp2[:, c:c + 1], col(v), s_mlpw)
            load(ow_sb[:, :], out_w, s_mlpw)
            load(ob_sb[:, :], out_b.rearrange("(o h) -> o h", o=1).broadcast_to([128, 2]), s_mlpw)

            def first_part(b, kind):
                act.activation(tc_parts[:, b, :, 0, cols[kind]], tc_val[:, b, :, cols[kind]],
                               ACT.Copy, scale=0.5).then_inc(s_hi[kind], 1)

            def second_part(b, kind):
                act.wait_ge(s_rest[kind], b + 1)
                act.activation(tc_parts[:, b, :, 1, cols[kind]], tc_res[:, b % 2, :, cols[kind]],
                               ACT.Copy).then_inc(s_mid[kind], 1)

            for t in range(TILES):
                pair = (2 * t, 2 * t + 1)
                act.wait_ge(s_ads[t], 16 * USERS)
                for b in pair:
                    first_part(b, EMB)
                    act.wait_ge(s_adsps, b + 1)
                    act.activation(adsT[:, 4 * b:4 * b + 4, :],
                                   ps_ent[b % 2][:, :].rearrange("p (u g) -> p u g", u=4),
                                   ACT.Copy).then_inc(s_adsT, 1)
                for b in pair:
                    second_part(b, EMB)
                for b in pair:
                    act.wait_ge(s_tcv, b + 1)
                    first_part(b, SHARE)
                for b in pair:
                    second_part(b, SHARE)

            act.wait_ge(s_flag, 1)
            general = act.value_load(flag_i[0:1, 0:1], min_val=0, max_val=128)

            def step_act(s):
                if s.has(2):
                    u = s.unit(2)
                    act.wait_ge(s_T, u.n + 1)
                    if u.after(DEEP):
                        act.wait_ge(s_1, u.n - DEEP + 1)
                    act.activation(entT[:, u.slot % DEEP, 0:u.width], ps_ent[u.slot % 2][:, 0:u.width],
                                   ACT.Copy).then_inc(s_cp, 1)
                if s.has(0):
                    u = s.unit(0)
                    if u.after(2):
                        act.wait_ge(s_oh, u.n - 1)
                    act.sem_inc(s_sign, 1)
                    at = u.first_tile * TILE
                    for w in range(2):
                        act.activation(reached[:, u.slot % 2, w, 0:u.width], pos_row[:, at:at + u.width],
                                       ACT.Sign, bias=seg_rows[:, w, columns(u.group, 1)]
                                       ).then_inc(s_oh_t, 1)
                if s.has(3):
                    u = s.unit(3)
                    act.wait_ge(s_1, u.n + 1)
                    if u.after(DEEP):
                        act.wait_ge(s_a1, u.n - DEEP + 1)
                    act.activation(neg1[:, u.slot % DEEP, 0:u.width],
                                   ps_h1[u.slot % 2][0:H1, 0:u.width],
                                   ACT.Relu, scale=-1.0).then_inc(s_n, 1)
                if s.has(4):
                    u = s.unit(4)
                    act.wait_ge(s_2, u.n + 1)
                    if u.after(DEEP):
                        act.wait_ge(s_a2, u.n - DEEP + 1)
                    act.activation(neg2[:, u.slot % DEEP, 0:u.tiles * H2],
                                   ps_h2[0:TILE, 0:u.tiles * H2], ACT.Relu,
                                   scale=-1.0).then_inc(s_n2, 1)

            act.wait_ge(s_segrow, 1)
            run_pass(act, step_act, UNITS, 0, 4)
            with act.If(general > 0):
                with act.Fori(1, PASSES) as p:
                    act.wait_ge(s_pos, 2 * p)
                    run_pass(act, step_act, UNITS, p * (UNITS // RING), 4)
            with act.Else():
                act.nop()

            act.wait_ge(s_v1, 1)
            act.activation(bnv[0:MH, 0:2, 1], bnv[0:MH, 0:2, 0], ACT.Sqrt).then_inc(s_sq1, 1)
            act.wait_ge(s_bn1, 1)
            for i in range(2 * NCH):
                c, h = divmod(i, 2)
                act.activation(z1n[:, h, c * CH:(c + 1) * CH], mlp_banks[i][0:MH, :],
                               ACT.Relu, bias=bnv[0:MH, h, 7:8], scale=bnv[0:MH, h, 6:7]
                               ).then_inc(s_n1, 1)
            act.wait_ge(s_v2, 1)
            act.activation(bnv[0:M2, 2:3, 1], bnv[0:M2, 2:3, 0], ACT.Sqrt).then_inc(s_sq2, 1)
            act.wait_ge(s_bn2, 1)
            for c in range(NCH):
                act.activation(z2n[:, c * CH:(c + 1) * CH], mlp_banks[2 * c][0:M2, :],
                               ACT.Relu, bias=bnv[0:M2, 2, 7:8], scale=bnv[0:M2, 2, 6:7]
                               ).then_inc(s_nz2, 1)
            act.wait_ge(s_sh, 3)
            act.activation(probs[:, :, :], probs[:, :, :], ACT.Exp).then_inc(s_ex, 1)

        @block.tensor
        def _(pe):
            pe.wait_ge(s_const, N_CONST)

            pe.wait_ge(s_total, 1)
            nc.tensor.matmul(ps_pool[:, 1:2], ident_wide[:, 0:128], before[:, SLOTS:SLOTS + 1],
                             start=True, stop=True).then_inc(s_before, 1)
            pe.wait_ge(s_flag_ps, 1)
            nc.tensor.matmul(ps_pool[0:1, 0:1], flag_col[:, :], ones_col[:, :],
                             start=True, stop=True).then_inc(s_segT, 1)
            pe.wait_ge(s_seg, 1)
            for w in range(2):
                nc.tensor.transpose(ps_tgt[0][0:HROWS, w * 128:(w + 1) * 128],
                                    rep_sb[:, w, :, :].rearrange("p u s -> p (u s)"), ident)
            nc.tensor.matmul(ps_tgt[0][0:1, 256:384], long_col[:, :], ident,
                             start=True, stop=True).then_inc(s_segT, 1)

            pe.wait_ge(s_cnt, 1)
            pe.wait_ge(s_blocks, 16 * KB)

            def turn_counts(i):
                if i >= 2:
                    pe.wait_ge(s_cTc, i - 1)
                nc.tensor.transpose(ps_ent[i % 2][0:KB * VOCAB, 0:TP],
                                    genre_cnt[:, i * KB:(i + 1) * KB, :].rearrange("p k v -> p (k v)"),
                                    ident[0:TP, 0:TP]).then_inc(s_cT, 1)

            turn_counts(0)
            for i in range(TK // KB):
                if i + 1 < TK // KB:
                    turn_counts(i + 1)
                pe.wait_ge(s_cTc, i + 1)
                if i >= 2:
                    pe.wait_ge(s_gev, i - 1)
                nc.tensor.matmul(ps_h1[i % 2][0:TP, 0:KB * E], genre_cntT[:, i % 2, :],
                                 genre_blocks[:, :], start=True, stop=True).then_inc(s_gps, 1)

            pe.wait_ge(s_w, 16 * N_W)
            pe.wait_ge(s_gev, TK // KB)
            for t in range(TILES):
                pe.wait_ge(s_ads[t], 16 * USERS)
                if t:
                    pe.wait_ge(s_adsT, 2 * t)
                for b in (2 * t, 2 * t + 1):
                    for i in range(4):
                        mm = nc.tensor.transpose(ps_ent[b % 2][:, i * 128:(i + 1) * 128],
                                                 tc_val[:, b, i, 0:D], ident)
                    mm.then_inc(s_adsps, 1)
                for b in (2 * t, 2 * t + 1):
                    pe.wait_ge(s_adsT, b + 1)
                    if t:
                        pe.wait_ge(s_tcv, b - 1)
                    for i in range(4):
                        dst = ps_h1[b % 2][:, i * H1:(i + 1) * H1]
                        mm = nc.tensor.matmul(dst, adsT[:, 4 * b + i, :],
                                              w1_sb[:, 1, :], start=True, stop=True)
                    mm.then_inc(s_cps, 1)

            pe.wait_ge(s_tcv, BATCHES)
            pe.wait_ge(s_segrow, 1)
            pe.wait_ge(s_flag, 1)
            general = pe.value_load(flag_i[0:1, 0:1], min_val=0, max_val=128)

            def length(u):
                if u.has_last and u.first_pass:
                    return pe.value_load(long_i[0:1, columns(u.group, 1)], min_val=0, max_val=1)

            def step_pe(s):
                if s.has(0):
                    u = s.unit(0)
                    q, d = u.slot % 2, u.slot % DEEP
                    pe.wait_ge(s_g[u.slot], 16 * u.full_tiles * (u.turn + 1))
                    if u.has_last and u.first_pass:
                        pe.wait_ge(s_last[u.gslot],
                                   pe.value_load(last_i[0:1, columns(u.group, 1)],
                                                 min_val=16, max_val=16 * (GROUPS // SLOTS_G)))
                    elif u.has_last:
                        pe.wait_ge(s_last[u.gslot], 16 * (u.turn + 1))
                    if u.after(2):
                        pe.wait_ge(s_cp, u.n - 1)
                    pe.sem_inc(s_pe, 1)

                    def turn(sizes):
                        for k, size in enumerate(sizes):
                            mm = nc.tensor.transpose(ps_ent[q][:, k * TILE:k * TILE + size],
                                                     entries[u.gslot][0:size, u.first_tile + k, :],
                                                     ident[0:size, 0:size])
                        mm.then_inc(s_T, 1)
                        pe.wait_ge(s_tc[u.gslot], 16 * HALVES * (u.turn + 1))
                        pe.wait_ge(s_oh, u.n + 1)
                        if u.after(2):
                            pe.wait_ge(s_pr, u.n - 1)
                        nc.tensor.matmul(ps_tgt[q][:, 0:sum(sizes)], tc_ring[:, u.gslot, 0:D],
                                         user_of[:, d, 0:sum(sizes)],
                                         start=True, stop=True).then_inc(s_tg, 1)

                    for_length(pe, length(u), u, turn)
                if s.has(1):
                    v = s.unit(1)
                    vq, vd = v.slot % 2, v.slot % DEEP
                    pe.wait_ge(s_cp, v.n + 1)
                    if v.after(2):
                        pe.wait_ge(s_a1, v.n - 1)
                    if v.has_last:
                        pe.sem_inc(s_pe, 1)

                    def layer1(sizes):
                        n = sum(sizes)
                        dst = ps_h1[vq][0:H1, 0:n]
                        nc.tensor.matmul(dst, w1_sb[:, 0, :], entT[:, vd, 0:n], start=True, stop=False)
                        nc.tensor.matmul(dst, tc_ring[:, v.gslot, D:TC], user_of[:, vd, 0:n],
                                         start=False, stop=False)
                        pe.wait_ge(s_pr, v.n + 1)
                        nc.tensor.matmul(dst, w1_sb[:, 2, :], prodT[:, vd, 0:n],
                                         start=False, stop=True).then_inc(s_1, 1)

                    for_length(pe, length(v), v, layer1)
                if s.has(2):
                    w = s.unit(2)
                    wd = w.slot % DEEP
                    pe.wait_ge(s_a1, w.n + 1)
                    if w.after(1):
                        pe.wait_ge(s_a2, w.n)
                    if w.has_last:
                        pe.sem_inc(s_pe, 1)

                    def layer2(sizes):
                        for k, size in enumerate(sizes):
                            mm = nc.tensor.matmul(ps_h2[0:size, k * H2:(k + 1) * H2],
                                                  act1[:, wd, k * TILE:k * TILE + size], w2_sb[:, :],
                                                  start=True, stop=True)
                        mm.then_inc(s_2, 1)

                    for_length(pe, length(w), w, layer2)
                if s.has(4):
                    x = s.unit(4)
                    xd = x.slot % DEEP
                    pe.wait_ge(s_aw, x.n + 1)
                    if x.chunk == 0 and x.group_after(1):
                        pe.wait_ge(s_pa, x.g)
                    if x.has_last:
                        pe.sem_inc(s_pe, 1)

                    def pool_entries(sizes):
                        for k, size in enumerate(sizes):
                            mm = nc.tensor.matmul(ps_pool[:, 0:GUSERS],
                                                  entries[x.gslot][0:size, x.first_tile + k, :],
                                                  att_w[0:size, xd, k, :], start=(x.first_tile + k == 0),
                                                  stop=(x.has_last and k == len(sizes) - 1))
                        mm.then_inc(s_pl, 1)

                    for_length(pe, length(x), x, pool_entries)

            pooled_v = pooledT[:, :, :, :].rearrange("p u h g -> p (u h g)")
            ads_v = adsT[:, :, :].rearrange("p u g -> p (u g)")

            def mlp1(i, part):
                c, h = divmod(i, 2)
                data = (pooled_v, ads_v)[part][:, c * CH:(c + 1) * CH]
                return nc.tensor.matmul(mlp_banks[i][0:MH, :], m1_sb[:, part, h * MH:(h + 1) * MH],
                                        data, start=(part == 1), stop=(part == 0))

            last_steps = 4
            pe.wait_ge(s_long, 1)
            run_steps(pe, step_pe, UNITS, 0)
            pe.wait_ge(s_mlpw, 16 * 15)
            with pe.If(general > 0):
                for k in range(last_steps):
                    step_pe(Step(UNITS // RING, k, 0, UNITS))
                with pe.Fori(1, PASSES) as p:
                    run_pass(pe, step_pe, UNITS, p * (UNITS // RING), last_steps)
                pe.wait_ge(s_cp, UNITS * PASSES)
                pe.wait_ge(s_pr, UNITS * PASSES)
                for i in range(4):
                    mlp1(i, 1)
            with pe.Else():
                step_pe(Step(UNITS // RING, 0, 0, UNITS))
                pe.wait_ge(s_cp, UNITS)
                for i in range(2):
                    mlp1(i, 1)
                step_pe(Step(UNITS // RING, 1, 0, UNITS))
                pe.wait_ge(s_pr, UNITS)
                for i in range(2, 4):
                    mlp1(i, 1)
                step_pe(Step(UNITS // RING, 2, 0, UNITS))
                step_pe(Step(UNITS // RING, 3, 0, UNITS))

            pe.wait_ge(s_main_dve, 1)
            for i in range(2 * NCH):
                if i >= 4:
                    mlp1(i, 1)
                mlp1(i, 0).then_inc(s_m1, 1)
            for c in range(NCH):
                pe.wait_ge(s_z1, 2 * (c + 1))
                for h in range(2):
                    mm = nc.tensor.matmul(mlp_banks[2 * c][0:M2, :], m2_sb[:, h, :],
                                          z1[:, h, c * CH:(c + 1) * CH], start=(h == 0), stop=(h == 1))
                mm.then_inc(s_m2, 1)
            for c in range(NCH):
                pe.wait_ge(s_z2, c + 1)
                for j in range(4 * c, 4 * c + 4):
                    at = 2 * j
                    mm = nc.tensor.matmul(ps_pool[:, at:at + 2], z2[:, j * 128:(j + 1) * 128],
                                          ow_sb[:, :], start=True, stop=True)
            mm.then_inc(s_lg, 1)

        @block.vector
        def _(dve):
            V = nc.vector
            steps = [0]

            def link(ins):
                steps[0] += 1
                ins.then_inc(s_d, 1)
                dve.wait_ge(s_d, steps[0])

            def row_numbers(dst, raw, tmp, n):
                link(V.tensor_scalar(tmp, raw, 0.0, float(n), ALU.is_lt, ALU.mult))
                link(V.tensor_tensor(tmp, tmp, raw, ALU.add))
                link(V.tensor_scalar(dst, tmp, 0.0, float(n - 1), ALU.max, ALU.min))

            dve.wait_ge(s_feat, 16)
            movies = feat_sb[:, :, 0]
            row_numbers(movie_idx[:, :], movies, feat_f[:, 0, :, 0], N_ROWS)
            dve.sem_inc(s_movie, 1)

            dve.wait_ge(s_rows, 16 * TILES)
            flat = "p u c -> p (u c)"
            for t in range(TILES):
                key = key_sb[:, t].rearrange(flat)
                row_numbers(idx_sb[:, t].rearrange(flat), rows_sb[:, t].rearrange(flat), key, N_ROWS)
                dve.sem_inc(s_idx, 1)
                link(V.tensor_scalar(key, idx_sb[:, t].rearrange(flat), -1.0, float(LAST_ROW),
                                     ALU.mult, ALU.add))
                ones = rows_sb[:, t].rearrange(flat).bitcast(F32)
                link(V.tensor_scalar(ones, key, 1.0, None, ALU.min))
                link(V.tensor_reduce(count[:, t * USERS:(t + 1) * USERS],
                                     rows_sb[:, t, :, 1:1 + T].bitcast(F32), AX_X, ALU.add))

            link(V.memset(before[:, 0:1], 0.0))
            length = small[:, 0, :]
            link(V.tensor_scalar(length, count[:, :], 1.0, None, ALU.add))
            for j in range(SLOTS):
                link(V.tensor_tensor(before[:, j + 1:j + 2], before[:, j:j + 1], length[:, j:j + 1],
                                     ALU.add))
            dve.sem_inc(s_total, 1)
            starts, ends, extra = (seg_sb[:, i, :] for i in range(3))
            one, two_ = slice(0, HALF), slice(HALF, 128)
            total = before[one, SLOTS:SLOTS + 1]
            link(V.tensor_scalar(starts[one], before[one, 1:SLOTS + 1], -1.0, total, ALU.mult, ALU.add))
            link(V.tensor_scalar(ends[one], before[one, 0:SLOTS], -1.0, total, ALU.mult, ALU.add))
            link(V.tensor_scalar(extra, count[:, :], -1.0, float(T - 1), ALU.mult, ALU.add))
            dve.wait_ge(s_before, 1)
            link(V.tensor_copy(group_before[:, :], ps_pool[:, 1:2]))
            other = group_before[two_, :]
            link(V.tensor_scalar(starts[two_], before[two_, 0:SLOTS], other, None, ALU.add))
            link(V.tensor_scalar(ends[two_], before[two_, 1:SLOTS + 1], other, None, ALU.add))
            over = small[:, 1, :]
            link(V.tensor_scalar(over, ends, float(CAP), None, ALU.is_gt))
            link(V.tensor_scalar(small[:, 2, :], length, float(RUN), None, ALU.is_gt))
            link(V.tensor_tensor(over, over, small[:, 2, :], ALU.max))
            link(V.tensor_reduce(flag_col[:, :], over, AX_X, ALU.max))
            dve.sem_inc(s_flag_ps, 1)
            dve.wait_ge(s_const, N_CONST)
            link(V.tensor_scalar(small[one, 3, :], ends[one], float(PAD - RUN), None, ALU.add))
            link(V.tensor_scalar(small[two_, 3, :], starts[two_], float(PAD - GROUPS * REGION), None,
                                 ALU.add))
            link(V.tensor_tensor(scatter_to[:, :], small[:, 3, :],
                                 group_base[:, :].broadcast_to([128, SLOTS]), ALU.add))
            dve.wait_ge(s_segT, 1)
            link(V.tensor_copy(flag_i[:, :], ps_pool[0:1, 0:1]))
            dve.sem_inc(s_flag, 1)
            general = dve.value_load(flag_i[0:1, 0:1], min_val=0, max_val=128)
            base = steps[0]
            with dve.If(general > 0):
                V.tensor_copy(starts[one], plain_start[one, :]).then_inc(s_d, 1)
                V.tensor_scalar(starts[two_], plain_start[two_, :], float(SLOTS * T), None,
                                ALU.add).then_inc(s_d, 1)
                V.memset(extra, 0.0).then_inc(s_d, 1)
                dve.wait_ge(s_d, base + 3)
                V.tensor_scalar(ends, starts, float(T), None, ALU.add).then_inc(s_d, 1)
            with dve.Else():
                dve.sem_inc(s_d, 4)
            steps[0] = base + 4
            dve.wait_ge(s_d, steps[0])
            link(V.tensor_scalar(long_col[:, :], ends[:, SLOTS - 1:SLOTS], float(SHORT), None, ALU.is_gt))
            for w in range(2):
                link(V.tensor_copy(rep_sb[:, w, :, :],
                                   seg_sb[:, w, :].rearrange("p (u o) -> p u o", o=1)
                                   .broadcast_to([128, SLOTS, PARTS])))
            dve.sem_inc(s_seg, 1)

            row_numbers(genre_bf[:, :, :].rearrange("p j k -> p k j"), feat_sb[:, :, 1:FEATS],
                        feat_f[:, 0, :, 1:FEATS], VOCAB)
            for half in range(2):
                for v in range(VOCAB // 2):
                    ins = V.tensor_scalar(genre_is[:, v, :, :], genre_bf[:, :, :],
                                          float(half * VOCAB // 2 + v), None, ALU.is_equal)
                    ins.then_inc(s_d, 1)
                steps[0] += VOCAB // 2
                dve.wait_ge(s_d, steps[0])
                for j in range(1, GENRES - 1):
                    link(V.tensor_tensor(genre_is[:, :, 0, :], genre_is[:, :, 0, :],
                                         genre_is[:, :, j, :], ALU.add))
                link(V.tensor_tensor(
                    genre_cnt[:, :, half * (VOCAB // 2):(half + 1) * (VOCAB // 2)]
                    .rearrange("p k v -> p v k"),
                    genre_is[:, :, 0, :], genre_is[:, :, GENRES - 1, :], ALU.add))
            dve.sem_inc(s_cnt, 1)
            link(V.memset(act1[64:ONE + 1, :, :], 1.0))
            link(V.tensor_scalar(feat_f[:, 1, :, 1:FEATS], feat_sb[:, :, 1:FEATS], 0.0, None, ALU.is_gt))
            link(V.tensor_reduce(genre_len[:, 0, :], feat_f[:, 1, :, 1:FEATS], AX_X, ALU.add))
            link(V.tensor_scalar(genre_len[:, 0, :], genre_len[:, 0, :], POOL_EPS, None, ALU.add))
            link(V.reciprocal(genre_len[:, 1, :], genre_len[:, 0, :]))
            dve.wait_ge(s_segT, 2)
            between_rows = slice(HALF // 2, HALF)
            link(V.memset(seg_rows[between_rows, :, :], 0.0))
            link(V.memset(tc_ring[between_rows, :, :], 0.0))
            turned = ps_tgt[0][0:HROWS, 0:2 * 128].rearrange("p (w h g) -> p w h g", w=2, h=HALVES)
            link(V.tensor_copy(long_i[:, :], ps_tgt[0][0:1, 256 + HALF:384]))
            for h in range(HALVES):
                link(V.tensor_scalar(seg_rows[h * HALF:h * HALF + HROWS, :, :], turned[:, :, h, :],
                                     -1.0, 0.5, ALU.mult, ALU.add))
            link(V.memset(long_i[:, 0:SLOTS_G], 1))
            dve.sem_inc(s_segrow, 1)
            link(V.tensor_scalar(last_count[:, 0:SLOTS_G], long_i[:, 0:SLOTS_G], 16.0, None, ALU.mult))
            for g in range(SLOTS_G, GROUPS, SLOTS_G):
                link(V.scalar_tensor_tensor(last_count[:, g:g + SLOTS_G], long_i[:, g:g + SLOTS_G], 16.0,
                                            last_count[:, g - SLOTS_G:g], ALU.mult, ALU.add))
            link(V.tensor_copy(last_i[:, :], last_count[:, :]))
            dve.sem_inc(s_long, 1)

            dve.wait_ge(s_w, 16 * N_W)
            V.tensor_scalar(scal[:, C1:CM2 + 1], scal[:, A1:AM2 + 1], -1.0, 1.0,
                            ALU.mult, ALU.add).then_inc(s_wsc, 1)
            dve.wait_ge(s_wsc, 1)

            def write_genres(i):
                dve.wait_ge(s_gps, i + 1)
                V.tensor_tensor(table_sb[:, i * KB:(i + 1) * KB, E:D],
                                ps_h1[i % 2][0:TP, 0:KB * E].rearrange("p (k e) -> p k e", k=KB),
                                genre_len[:, 1, i * KB:(i + 1) * KB].rearrange("p (k o) -> p k o", o=1)
                                .broadcast_to([TP, KB, E]), ALU.mult).then_inc(s_gev, 1)

            blocks_left = iter(range(TK // KB))
            for pair in range(SLOTS // 2):
                t, first = divmod(2 * pair, USERS)
                for r in range(RUN // 8):
                    for i in range(2):
                        src = work[:, i, :] if r else key_sb[:, t, first + i, 1:1 + T]
                        if r:
                            dve.wait_ge(s_d, steps[0] - 1)
                        V.max(best[:, i, 8 * r:8 * r + 8], src).then_inc(s_d, 1)
                        steps[0] += 1
                    if r < RUN // 8 - 1:
                        for i in range(2):
                            src = work[:, i, :] if r else key_sb[:, t, first + i, 1:1 + T]
                            dve.wait_ge(s_d, steps[0] - 1)
                            V.match_replace(work[:, i, :], best[:, i, 8 * r:8 * r + 8], src,
                                            -1.0).then_inc(s_d, 1)
                            steps[0] += 1
                    for i in blocks_left:
                        write_genres(i)
                        break
                dve.wait_ge(s_d, steps[0])
                for i in range(2):
                    V.tensor_scalar(run_idx[one, 2 * pair + i, :], best[one, i, ::-1], -1.0,
                                    float(LAST_ROW), ALU.mult, ALU.add).then_inc(s_runs, 1)
                    V.tensor_scalar(run_idx[two_, 2 * pair + i, :], best[two_, i, :], -1.0,
                                    float(LAST_ROW), ALU.mult, ALU.add).then_inc(s_runs, 1)
                dve.wait_ge(s_runs, 4 * (pair + 1))

            dve.wait_ge(s_segin, 16)
            link(V.tensor_copy(extra_all[:, :, :], seg_all[:, :, 2, :]))
            link(V.tensor_copy(pos_col[:, 0, :], pos_init[:, :]))
            link(V.tensor_scalar(pos_col[:, 1, :], pos_col[:, 0, :], 1.0, None, ALU.add))

            def rest(b, kind):
                dve.wait_ge(s_hi[kind], b + 1)
                if b >= 2:
                    dve.wait_ge(s_lo[kind], b - 1)
                V.scalar_tensor_tensor(tc_res[:, b % 2, :, cols[kind]], tc_val[:, b, :, cols[kind]], 0.5,
                                       tc_parts[:, b, :, 0, cols[kind]],
                                       ALU.mult, ALU.subtract).then_inc(s_rest[kind], 1)

            def last_part(b, kind):
                dve.wait_ge(s_rest[kind], b + 1)
                dve.wait_ge(s_mid[kind], b + 1)
                V.tensor_tensor(tc_parts[:, b, :, 2, cols[kind]], tc_res[:, b % 2, :, cols[kind]],
                                tc_parts[:, b, :, 1, cols[kind]], ALU.subtract).then_inc(s_lo[kind], 1)

            def share(b):
                dve.wait_ge(s_cps, b + 1)
                V.tensor_tensor(tc_val[:, b, :, D:TC], ps_h1[b % 2][:, 0:4 * H1]
                                .rearrange("p (u h) -> p u h", u=4),
                                b1_bc[:, :].rearrange("p (o h) -> p o h", o=1)
                                .broadcast_to([128, 4, H1]), ALU.add).then_inc(s_tcv, 1)
                dve.wait_ge(s_tcv, b + 1)

            for t in range(TILES):
                b, c = 2 * t, 2 * t + 1
                rest(b, EMB)
                rest(c, EMB)
                last_part(b, EMB)
                share(b)
                last_part(c, EMB)
                share(c)
                rest(b, SHARE)
                rest(c, SHARE)
                last_part(b, SHARE)
                last_part(c, SHARE)

            WT_STEPS = 7

            def entry_weights(u, part):
                done = WT_STEPS * u.g
                shape = [128, GTILES, GUSERS]
                start, end = (seg_all[:, columns(u.group, 1), i, :].broadcast_to(shape)
                              for i in range(2))
                pos, next_pos = (pos_col[:, i, :].rearrange("p (k b) -> p k b", b=1)
                                 .broadcast_to(shape) for i in range(2))
                tmp, out_half = wt_tmp, wts[:, u.gslot % 2]
                more = extra_all[:, columns(u.group, 1), :].broadcast_to(shape)

                def op(out, in0, in1, alu):
                    V.tensor_tensor(out, in0, in1, alu).then_inc(s_wt, 1)

                if part == (0, 0):
                    if u.group_after(1):
                        dve.wait_ge(s_wt, done)
                    op(tmp[:, 0], pos, start, ALU.is_ge)
                elif part == (0, 1):
                    op(tmp[:, 1], pos, end, ALU.is_ge)
                elif part == (1, 0):
                    op(tmp[:, 2, :, 0:SLOTS], pos[:, :, 0:SLOTS], start[:, :, 0:SLOTS], ALU.is_equal)
                elif part == (1, 1):
                    op(tmp[:, 2, :, SLOTS:], next_pos[:, :, SLOTS:], end[:, :, SLOTS:], ALU.is_equal)
                elif part == (1, 2):
                    dve.wait_ge(s_wt, done + 2)
                    op(tmp[:, 0], tmp[:, 0], tmp[:, 1], ALU.subtract)
                elif part == (2, 0):
                    dve.wait_ge(s_wt, done + 5)
                    op(tmp[:, 2], tmp[:, 2], more, ALU.mult)
                elif part == (2, 1):
                    dve.wait_ge(s_wt, done + 6)
                    if u.group_after(2):
                        dve.wait_ge(s_aw, u.n - len(CHUNKS))
                    op(out_half, tmp[:, 0], tmp[:, 2], ALU.add)

            def step_dve(s):
                att, ahead = s.has(4), s.has(0)
                if att:
                    u = s.unit(4)
                    d, n2 = u.slot % DEEP, u.tiles * H2
                    by_tile = "p (k h) -> p k h"
                    dve.wait_ge(s_n2, u.n + 1)
                    if u.after(1):
                        dve.wait_ge(s_aw, u.n)
                    V.scalar_tensor_tensor(act2[:, 0:n2], neg2[:, d, 0:n2], scal[0:TILE, C2:C2 + 1],
                                           ps_h2[0:TILE, 0:n2], ALU.mult, ALU.add).then_inc(s_a2, 1)
                if ahead:
                    v = s.unit(0)
                    e = v.slot % 2
                    dve.wait_ge(s_oh_t, 2 * v.n + 2)
                    if v.after(DEEP):
                        dve.wait_ge(s_1, v.n - DEEP + 1)
                    V.tensor_tensor(user_of[:, v.slot % DEEP, 0:v.width], reached[:, e, 0, 0:v.width],
                                    reached[:, e, 1, 0:v.width], ALU.subtract).then_inc(s_oh, 1)
                if att:
                    dve.wait_ge(s_a2, u.n + 1)
                    V.tensor_tensor(scaled2[:, 0:n2].rearrange(by_tile, h=H2),
                                    act2[:, 0:n2].rearrange(by_tile, h=H2),
                                    wo_bc[0:TILE, :].rearrange("p (o h) -> p o h", o=1)
                                    .broadcast_to([TILE, u.tiles, H2]), ALU.mult).then_inc(s_m2w, 1)
                if s.has(6) and s.unit(6).chunk == len(CHUNKS) - 1:
                    w = s.unit(6)
                    dve.wait_ge(s_pl, w.n + 1)
                    dst = (pooledT[:, :, :, columns(w.group, 1)]
                           .rearrange("p j h g -> p h (j g)"))
                    V.tensor_tensor(dst, dst, ps_pool[:, 0:GUSERS].rearrange("p (h j) -> p h j", h=HALVES),
                                    ALU.add).then_inc(s_pa, 1)
                if ahead:
                    first = Step(s.block, v.slot - v.chunk, s.first_block, s.last).unit(0)
                    entry_weights(first, (v.chunk, 0))
                if att:
                    dve.wait_ge(s_m2w, u.n + 1)
                    V.tensor_reduce(att_sum[:, 0:u.tiles], scaled2[:, 0:n2].rearrange(by_tile, h=H2),
                                    AX_X, ALU.add).then_inc(s_at, 1)
                if ahead:
                    entry_weights(first, (v.chunk, 1))
                if att:
                    dve.wait_ge(s_at, u.n + 1)
                    dve.wait_ge(s_wt, WT_STEPS * (u.g + 1))
                    if u.after(DEEP):
                        dve.wait_ge(s_pl, u.n - DEEP + 1)
                    V.scalar_tensor_tensor(
                        att_w[:, d, 0:u.tiles], att_sum[:, 0:u.tiles].rearrange("p (k o) -> p k o", o=1)
                        .broadcast_to([TILE, u.tiles, GUSERS]), scal[0:TILE, BO:BO + 1],
                        wts[0:TILE, u.gslot % 2, u.first_tile:u.first_tile + u.tiles],
                        ALU.add, ALU.mult).then_inc(s_aw, 1)
                if ahead:
                    entry_weights(first, (v.chunk, 2))
                if s.has(1):
                    u = s.unit(1)
                    dve.wait_ge(s_cp, u.n + 1)
                    dve.wait_ge(s_tg, u.n + 1)
                    if u.after(DEEP):
                        dve.wait_ge(s_1, u.n - DEEP + 1)
                    V.tensor_tensor(prodT[:, u.slot % DEEP, 0:u.width], entT[:, u.slot % DEEP, 0:u.width],
                                    ps_tgt[u.slot % 2][:, 0:u.width], ALU.mult).then_inc(s_pr, 1)
                if s.has(2):
                    u = s.unit(2)
                    d = u.slot % DEEP
                    dve.wait_ge(s_n, u.n + 1)
                    if u.after(DEEP):
                        dve.wait_ge(s_2, u.n - DEEP + 1)
                    V.scalar_tensor_tensor(act1[0:H1, d, 0:u.width], neg1[:, d, 0:u.width],
                                           scal[0:H1, C1:C1 + 1], ps_h1[u.slot % 2][0:H1, 0:u.width],
                                           ALU.mult, ALU.add).then_inc(s_a1, 1)

            run_pass(dve, step_dve, UNITS, 0, 6)
            with dve.If(general > 0):
                with dve.Fori(1, PASSES) as p:
                    dve.wait_ge(s_pa, GROUPS * p)
                    V.tensor_scalar(pos_col[:, :, :], pos_col[:, :, :], float(CAP), None,
                                    ALU.add).then_inc(s_pos, 1)
                    V.tensor_scalar(seg_rows[:, :, :], seg_rows[:, :, :], float(CAP), None,
                                    ALU.add).then_inc(s_pos, 1)
                    dve.wait_ge(s_pos, 2 * p)
                    run_pass(dve, step_dve, UNITS, p * (UNITS // RING), 6)
                dve.wait_ge(s_pa, GROUPS * PASSES)
            with dve.Else():
                dve.wait_ge(s_pa, GROUPS)
            dve.sem_inc(s_main_dve, 1)

            def norm(P, cols, bnp, var_ready, root_ready, bn_ready):
                v = bnv[0:P, cols, :]
                link(V.tensor_scalar(v[:, :, 0], aggr[0:P, cols, 1], BN_EPS, None, ALU.add))
                dve.sem_inc(var_ready, 1)
                link(V.tensor_tensor(v[:, :, 5], aggr[0:P, cols, 0], bnp[:, 0], ALU.add))
                link(V.tensor_tensor(v[:, :, 5], v[:, :, 5], bnp[:, 0], ALU.subtract))
                dve.wait_ge(root_ready, 1)
                link(V.reciprocal(v[:, :, 2], v[:, :, 1]))
                V.tensor_tensor(v[:, :, 3], v[:, :, 2], v[:, :, 2], ALU.mult).then_inc(s_d, 1)
                V.tensor_tensor(v[:, :, 1], v[:, :, 2], bnp[:, 1], ALU.mult).then_inc(s_d, 1)
                steps[0] += 2
                dve.wait_ge(s_d, steps[0])
                link(V.scalar_tensor_tensor(v[:, :, 3], v[:, :, 3], -0.5, v[:, :, 0], ALU.mult, ALU.mult))
                link(V.scalar_tensor_tensor(v[:, :, 4], v[:, :, 3], 1.5, v[:, :, 1], ALU.add, ALU.mult))
                link(V.tensor_tensor(v[:, :, 3], v[:, :, 4], v[:, :, 5], ALU.mult))
                V.tensor_tensor(v[:, :, 5], bnp[:, 2], v[:, :, 3], ALU.subtract).then_inc(s_d, 1)
                V.tensor_tensor(v[:, :, 7], v[:, :, 3], bnp[:, 2], ALU.subtract).then_inc(s_d, 1)
                V.tensor_scalar(v[:, :, 6], v[:, :, 4], -1.0, None, ALU.mult).then_inc(s_d, 1)
                steps[0] += 3
                dve.wait_ge(s_d, steps[0])
                dve.sem_inc(bn_ready, 1)

            def prelu(z, bank, col, P, done):
                V.scalar_tensor_tensor(z, bank[0:P, :], bnv[0:P, col, 4:5], z,
                                       ALU.mult, ALU.add).then_inc(done, 1)

            dve.wait_ge(s_mlpw, 16 * 15)
            for i in range(2 * NCH):
                c, h = divmod(i, 2)
                dve.wait_ge(s_m1, i + 1)
                V.bn_stats(stats[0:MH, h, c, :], mlp_banks[i][0:MH, :]).then_inc(s_d, 1)
            steps[0] += 2 * NCH
            dve.wait_ge(s_d, steps[0])
            for h in range(2):
                V.bn_aggr(aggr[0:MH, h, :], stats[0:MH, h, :, :].rearrange("p c s -> p (c s)")
                          ).then_inc(s_d, 1)
            steps[0] += 2
            dve.wait_ge(s_d, steps[0])
            norm(MH, slice(0, 2), bnp1[:, :, :], s_v1, s_sq1, s_bn1)
            for i in range(2 * NCH):
                c, h = divmod(i, 2)
                dve.wait_ge(s_p1, i + 1)
                prelu(z1[:, h, c * CH:(c + 1) * CH], mlp_banks[i], h, MH, s_z1)
            for c in range(NCH):
                dve.wait_ge(s_m2, c + 1)
                V.bn_stats(stats[0:M2, 2, c, :], mlp_banks[2 * c][0:M2, :]).then_inc(s_d, 1)
            steps[0] += NCH
            dve.wait_ge(s_d, steps[0])
            link(V.bn_aggr(aggr[0:M2, 2, :], stats[0:M2, 2, :, :].rearrange("p c s -> p (c s)")))
            norm(M2, slice(2, 3), bnp2[:, :].rearrange("p (c o) -> p c o", o=1), s_v2, s_sq2, s_bn2)
            for c in range(NCH):
                dve.wait_ge(s_p2, c + 1)
                prelu(z2[:, c * CH:(c + 1) * CH], mlp_banks[2 * c], 2, M2, s_z2)
            dve.wait_ge(s_lg, 1)
            K = TILES * USERS
            V.tensor_tensor(probs[:, :, :], ps_pool[:, 0:2 * K].rearrange("p (k c) -> p k c", c=2),
                            ob_sb[:, :].rearrange("p (o c) -> p o c", o=1).broadcast_to([128, K, 2]),
                            ALU.add).then_inc(s_sh, 1)
            dve.wait_ge(s_sh, 1)
            V.tensor_tensor(lmax[:, 0, :], probs[:, :, 0], probs[:, :, 1], ALU.max).then_inc(s_sh, 1)
            dve.wait_ge(s_sh, 2)
            V.tensor_tensor(probs[:, :, :], probs[:, :, :],
                            lmax[:, 0, :].rearrange("p (k o) -> p k o", o=1).broadcast_to([128, K, 2]),
                            ALU.subtract).then_inc(s_sh, 1)
            dve.wait_ge(s_ex, 1)
            link(V.tensor_tensor(lmax[:, 0, :], probs[:, :, 0], probs[:, :, 1], ALU.add))
            link(V.reciprocal(lmax[:, 1, :], lmax[:, 0, :]))
            V.tensor_tensor(probs[:, :, :], probs[:, :, :],
                            lmax[:, 1, :].rearrange("p (k o) -> p k o", o=1).broadcast_to([128, K, 2]),
                            ALU.mult).then_inc(s_pb, 1)


_INS = ['r_rowData', 'L0_rec_movieFeature', 'L0_rec_emb_movie', 'L0_rec_emb_genre',
        'L0_rec_att_w1', 'L0_rec_att_b1', 'L0_rec_att_a1', 'L0_rec_att_w2', 'L0_rec_att_b2',
        'L0_rec_att_a2', 'L0_rec_att_wo', 'L0_rec_att_bo', 'L0_rec_mlp_w1', 'L0_rec_mlp_b1',
        'L0_rec_bn1_g', 'L0_rec_bn1_b', 'L0_rec_mlp_a1', 'L0_rec_mlp_w2', 'L0_rec_mlp_b2',
        'L0_rec_bn2_g', 'L0_rec_bn2_b', 'L0_rec_mlp_a2', 'L0_rec_out_w', 'L0_rec_out_b']


def kernel(**inputs):
    import numpy as np
    import concourse.bacc as bacc
    from concourse.bass_utils import run_bass_kernel_spmd

    nc = bacc.Bacc("TRN2", target_bir_lowering=False, num_devices=1)
    arrays, args = {}, []
    for name in _INS:
        a = np.ascontiguousarray(inputs[name])
        if a.ndim == 0:
            a = a.reshape(1)
        arrays[f"in_{name}"] = a
        args.append(nc.dram_tensor(f"in_{name}", a.shape, mybir.dt.from_np(a.dtype),
                                   kind="ExternalInput").ap())
    out = nc.dram_tensor("out_0", (inputs['r_rowData'].shape[0], 2), F32, kind="ExternalOutput").ap()
    build(nc, *args, out)
    r = run_bass_kernel_spmd(nc, [arrays], core_ids=[0])
    return r.results[0]["out_0"]
```
